# Optimizing a Trainium2 kernel written in Bass

```python
import numpy as np
import jax
import jax.numpy as jnp

def _softmax(x, axis=-1):
    return jax.nn.softmax(x, axis=axis)

def _gelu(x):
    return jax.nn.gelu(x, approximate=True)

def _silu(x):
    return jax.nn.silu(x)

def _sigmoid(x):
    return jax.nn.sigmoid(x)

def _layernorm(x, axis=-1, eps=1e-05):
    m = jnp.mean(x, axis=axis, keepdims=True)
    v = jnp.var(x, axis=axis, keepdims=True)
    return (x - m) / jnp.sqrt(v + eps)

def _scatter_add(tgt, idx, src, axis=0):
    return tgt.at[idx].add(src)

def _segment_sum(src, seg, n):
    return jax.ops.segment_sum(src, seg, n)
kernel_name = 'mk_perceiver_d1_seqx_r2_9a9650'

def setup_inputs(seed: int=0):
    np.random.seed(seed)
    _w = jnp.asarray

    def _rec_inputs():
        import jax
        import jax.numpy as jnp
        _rk = jax.random.key(seed)
        x = -0.0003929 + 0.9999 * jax.random.normal(jax.random.fold_in(_rk, 1), (16, 64, 512), jnp.float32)
        _lenS = 64 - jax.random.randint(jax.random.fold_in(_rk, 7), (16,), 0, max(1, 64 // 4) + 1, jnp.int32)
        _lenS2 = 1601 - jax.random.randint(jax.random.fold_in(_rk, 8), (16,), 0, max(1, 1601 // 4) + 1, jnp.int32)
        _ctx_768P = jax.random.normal(jax.random.fold_in(_rk, 11), (16, 16, 384), jnp.float32)
        _ctx_768c = jax.random.dirichlet(jax.random.fold_in(_rk, 511), 0.3 * jnp.ones((16,), jnp.float32), (16, 1601))
        _ctx_768t = jnp.einsum('bsk,bkd->bsd', _ctx_768c, _ctx_768P)
        _ctx_768t = _ctx_768t * jax.lax.rsqrt(jnp.mean(jnp.square(_ctx_768t)) + 1e-12) * 0.953939
        ctx_768 = -7.36909e-05 + 0.999899 * (_ctx_768t + 0.3 * jax.random.normal(jax.random.fold_in(_rk, 611), (16, 1601, 384), jnp.float32))
        return (x, ctx_768)
    x, ctx_768 = _rec_inputs()

    def _L0_xattn_setup():
        import jax, jax.numpy as jnp
        import numpy as np
        EPS = 1e-05

        def layernorm(x, g, b):
            mu = jnp.mean(x, axis=-1, keepdims=True)
            var = jnp.mean(jnp.square(x - mu), axis=-1, keepdims=True)
            return (x - mu) * jax.lax.rsqrt(var + EPS) * g + b
        key = jax.random.key(seed)
        ks = jax.random.split(key, 12)
        B, L1, L2 = (8, 1024, 1024)
        D1, D2, E = (512, 384, 512)
        s1, s2, se = (D1 ** (-0.5), D2 ** (-0.5), E ** (-0.5))
        return {'modality1': jax.random.normal(ks[0], (B, L1, D1), jnp.float32), 'modality2': jax.random.normal(ks[1], (B, L2, D2), jnp.float32), 'ln1_g': jnp.ones((D1,), jnp.float32), 'ln1_b': jnp.zeros((D1,), jnp.float32), 'ln2_g': jnp.ones((D2,), jnp.float32), 'ln2_b': jnp.zeros((D2,), jnp.float32), 'Wq': jax.random.normal(ks[2], (D1, E), jnp.float32) * s1, 'bq': jax.random.normal(ks[3], (E,), jnp.float32) * 0.01, 'Wk': jax.random.normal(ks[4], (D2, E), jnp.float32) * s2, 'bk': jax.random.normal(ks[5], (E,), jnp.float32) * 0.01, 'Wv': jax.random.normal(ks[6], (D2, E), jnp.float32) * s2, 'bv': jax.random.normal(ks[7], (E,), jnp.float32) * 0.01, 'Wo': jax.random.normal(ks[8], (E, D1), jnp.float32) * se, 'bo': jax.random.normal(ks[9], (D1,), jnp.float32) * 0.01}
    _L0_xattn_all = _L0_xattn_setup()
    _L0_xattn_in = {k: v for k, v in _L0_xattn_all.items() if k in ('ln1_g', 'ln1_b', 'ln2_g', 'ln2_b', 'Wq', 'bq', 'Wk', 'bk', 'Wv', 'bv', 'Wo', 'bo')}
    del _L0_xattn_all

    def _L0_attn_setup():
        import jax, jax.numpy as jnp
        import numpy as np
        import math
        B, L, HID, H = (4, 512, 512, 16)
        DH = HID // H
        MAX_SEQ = 512
        key = jax.random.key(seed)
        ks = jax.random.split(key, 6)
        s = 0.02
        return {'x': jax.random.normal(ks[0], (B, L, HID), jnp.float32), 'Wq': jax.random.normal(ks[1], (HID, HID), jnp.float32) * s, 'bq': jnp.zeros((HID,), jnp.float32), 'Wk': jax.random.normal(ks[2], (HID, HID), jnp.float32) * s, 'bk': jnp.zeros((HID,), jnp.float32), 'Wv': jax.random.normal(ks[3], (HID, HID), jnp.float32) * s, 'bv': jnp.zeros((HID,), jnp.float32), 'Wo': jax.random.normal(ks[4], (HID, HID), jnp.float32) * s, 'bo': jnp.zeros((HID,), jnp.float32), 'rel_emb': jax.random.normal(ks[5], (2 * MAX_SEQ - 1, DH), jnp.float32) * s}
    _L0_attn_all = _L0_attn_setup()
    _L0_attn_in = {k: v for k, v in _L0_attn_all.items() if k in ('Wq', 'bq', 'Wk', 'bk', 'Wv', 'bv', 'Wo', 'bo', 'rel_emb')}
    del _L0_attn_all

    def _L0_ffn_setup():
        import jax, jax.numpy as jnp
        import numpy as np
        EMB = 512
        FF = 4 * EMB

        def _ternary(w):
            scale = jnp.maximum(jnp.mean(jnp.abs(w)), 1e-08)
            w_t = jnp.clip(jnp.round(w / scale), -1.0, 1.0)
            return w + jax.lax.stop_gradient(w_t - w)
        key = jax.random.key(seed)
        kx, k1, k2, kb1, kb2 = jax.random.split(key, 5)
        x = jax.random.normal(kx, (4, 1024, EMB), dtype=jnp.float32)
        lim1 = 1.0 / np.sqrt(EMB)
        lim2 = 1.0 / np.sqrt(FF)
        W1 = jax.random.uniform(k1, (FF, EMB), jnp.float32, -lim1, lim1)
        b1 = jax.random.uniform(kb1, (FF,), jnp.float32, -lim1, lim1)
        W2 = jax.random.uniform(k2, (EMB, FF), jnp.float32, -lim2, lim2)
        b2 = jax.random.uniform(kb2, (EMB,), jnp.float32, -lim2, lim2)
        return {'x': x, 'W1': W1, 'b1': b1, 'W2': W2, 'b2': b2}
    _L0_ffn_all = _L0_ffn_setup()
    _L0_ffn_in = {k: v for k, v in _L0_ffn_all.items() if k in ('W1', 'b1', 'W2', 'b2')}
    del _L0_ffn_all
    return {'x': x, 'ctx_768': ctx_768, 'L0_xattn_ln1_g': _L0_xattn_in['ln1_g'], 'L0_xattn_ln1_b': _L0_xattn_in['ln1_b'], 'L0_xattn_ln2_g': _L0_xattn_in['ln2_g'], 'L0_xattn_ln2_b': _L0_xattn_in['ln2_b'], 'L0_xattn_Wq': _L0_xattn_in['Wq'], 'L0_xattn_bq': _L0_xattn_in['bq'], 'L0_xattn_Wk': _L0_xattn_in['Wk'], 'L0_xattn_bk': _L0_xattn_in['bk'], 'L0_xattn_Wv': _L0_xattn_in['Wv'], 'L0_xattn_bv': _L0_xattn_in['bv'], 'L0_xattn_Wo': _L0_xattn_in['Wo'], 'L0_xattn_bo': _L0_xattn_in['bo'], 'L0_attn_Wq': _L0_attn_in['Wq'], 'L0_attn_bq': _L0_attn_in['bq'], 'L0_attn_Wk': _L0_attn_in['Wk'], 'L0_attn_bk': _L0_attn_in['bk'], 'L0_attn_Wv': _L0_attn_in['Wv'], 'L0_attn_bv': _L0_attn_in['bv'], 'L0_attn_Wo': _L0_attn_in['Wo'], 'L0_attn_bo': _L0_attn_in['bo'], 'L0_attn_rel_emb': _L0_attn_in['rel_emb'], 'L0_ffn_W1': _L0_ffn_in['W1'], 'L0_ffn_b1': _L0_ffn_in['b1'], 'L0_ffn_W2': _L0_ffn_in['W2'], 'L0_ffn_b2': _L0_ffn_in['b2']}

def reference(x, ctx_768, L0_xattn_ln1_g, L0_xattn_ln1_b, L0_xattn_ln2_g, L0_xattn_ln2_b, L0_xattn_Wq, L0_xattn_bq, L0_xattn_Wk, L0_xattn_bk, L0_xattn_Wv, L0_xattn_bv, L0_xattn_Wo, L0_xattn_bo, L0_attn_Wq, L0_attn_bq, L0_attn_Wk, L0_attn_bk, L0_attn_Wv, L0_attn_bv, L0_attn_Wo, L0_attn_bo, L0_attn_rel_emb, L0_ffn_W1, L0_ffn_b1, L0_ffn_W2, L0_ffn_b2):
    import jax
    import jax.numpy as jnp

    def _L0_xattn_ref(modality1, modality2, ln1_g, ln1_b, ln2_g, ln2_b, Wq, bq, Wk, bk, Wv, bv, Wo, bo):
        import jax, jax.numpy as jnp
        import numpy as np
        EPS = 1e-05

        def layernorm(x, g, b):
            mu = jnp.mean(x, axis=-1, keepdims=True)
            var = jnp.mean(jnp.square(x - mu), axis=-1, keepdims=True)
            return (x - mu) * jax.lax.rsqrt(var + EPS) * g + b
        E = Wq.shape[1]
        scaling = E ** (-0.5)
        x1 = layernorm(modality1, ln1_g, ln1_b)
        x2 = layernorm(modality2, ln2_g, ln2_b)
        q = x1 @ Wq + bq
        k = x2 @ Wk + bk
        v = x2 @ Wv + bv
        scores = jnp.einsum('bqe,bke->bqk', q, k) * scaling
        attn = jax.nn.softmax(scores, axis=-1)
        ctx = jnp.einsum('bqk,bke->bqe', attn, v)
        return ctx @ Wo + bo

    def _L0_attn_ref(x, Wq, bq, Wk, bk, Wv, bv, Wo, bo, rel_emb):
        import jax, jax.numpy as jnp
        import numpy as np
        import math
        B, L, HID, H = (4, 512, 512, 16)
        DH = HID // H
        MAX_SEQ = 512
        b, l, hid = x.shape
        dh = rel_emb.shape[1]
        h = hid // dh
        max_seq = (rel_emb.shape[0] + 1) // 2

        def heads(y):
            return y.reshape(b, l, h, dh).transpose(0, 2, 1, 3)
        q = heads(x @ Wq + bq)
        k = heads(x @ Wk + bk)
        v = heads(x @ Wv + bv)
        scores = jnp.einsum('bhid,bhjd->bhij', q, k) / math.sqrt(dh)
        scores = jnp.clip(scores, -100000.0, 100000.0)
        pos_idx = jnp.arange(l)[:, None] - jnp.arange(l)[None, :] + max_seq - 1
        rel_pos = rel_emb[pos_idx]
        scores = scores + jnp.einsum('bhid,ijd->bhij', q, rel_pos)
        attn = jax.nn.softmax(scores, axis=-1)
        attn = attn / (attn.sum(axis=-1, keepdims=True) + 1e-08)
        ctx = jnp.einsum('bhij,bhjd->bhid', attn, v)
        ctx = ctx.transpose(0, 2, 1, 3).reshape(b, l, hid)
        return ctx @ Wo + bo

    def _L0_ffn_ref(x, W1, b1, W2, b2):
        import jax, jax.numpy as jnp
        import numpy as np
        EMB = 512
        FF = 4 * EMB

        def _ternary(w):
            scale = jnp.maximum(jnp.mean(jnp.abs(w)), 1e-08)
            w_t = jnp.clip(jnp.round(w / scale), -1.0, 1.0)
            return w + jax.lax.stop_gradient(w_t - w)
        h = jnp.einsum('bsd,fd->bsf', x, _ternary(W1)) + b1
        h = jax.nn.gelu(h, approximate=False)
        out = jnp.einsum('bsf,df->bsd', h, _ternary(W2)) + b2
        return out
    x = x + _L0_xattn_ref(_layernorm(x, axis=-1), ctx_768, L0_xattn_ln1_g, L0_xattn_ln1_b, L0_xattn_ln2_g, L0_xattn_ln2_b, L0_xattn_Wq, L0_xattn_bq, L0_xattn_Wk, L0_xattn_bk, L0_xattn_Wv, L0_xattn_bv, L0_xattn_Wo, L0_xattn_bo)
    x = x + _L0_attn_ref(_layernorm(x, axis=-1), L0_attn_Wq, L0_attn_bq, L0_attn_Wk, L0_attn_bk, L0_attn_Wv, L0_attn_bv, L0_attn_Wo, L0_attn_bo, L0_attn_rel_emb)
    x = x + _L0_ffn_ref(_layernorm(x, axis=-1), L0_ffn_W1, L0_ffn_b1, L0_ffn_W2, L0_ffn_b2)
    return x

_drawn_inputs = setup_inputs


def setup_inputs(seed=0):
    import zlib

    import numpy as np

    out = dict(_drawn_inputs(seed))
    spreads = {'L0_xattn_ln1_g': (1.0, 0.2),
     'L0_xattn_ln1_b': (0.0, 0.621),
     'L0_xattn_ln2_g': (1.0, 0.2),
     'L0_xattn_ln2_b': (0.0, 0.1),
     'L0_attn_bq': (0.0, 0.8),
     'L0_attn_bk': (0.0, 2.0),
     'L0_attn_bv': (0.0, 0.1),
     'L0_attn_bo': (0.0, 0.1)}
    factors = {'L0_xattn_bq': 37.261,
     'L0_xattn_bk': 64.0,
     'L0_xattn_bv': 7.594,
     'L0_xattn_bo': 7.241,
     'L0_attn_Wq': 8.0,
     'L0_attn_Wk': 8.0,
     'L0_attn_rel_emb': 8.0,
     'L0_ffn_b1': 50.597,
     'L0_ffn_b2': 64.0}
    for name, (base, spread) in spreads.items():
        noise = np.random.default_rng([zlib.crc32(name.encode()), seed]).standard_normal(out[name].shape)
        drawn = base * np.exp(spread * noise) if base else spread * noise
        out[name] = jnp.asarray(drawn.astype(out[name].dtype))
    for name, factor in factors.items():
        out[name] = (out[name] * factor).astype(out[name].dtype)
    return out
```

```python
from contextlib import ExitStack

import concourse.bass as bass
from concourse import mybir

F32 = mybir.dt.float32
F16 = mybir.dt.float16
BF16 = mybir.dt.bfloat16
ALU = mybir.AluOpType
ACT = mybir.ActivationFunctionType
AX = mybir.AxisListType

P = 128


def build_program(nc, A, out, dump=None):
    B, L, D = A["x"].shape
    _, S, DC = A["ctx_768"].shape
    E = A["L0_xattn_Wq"].shape[1]
    ROWS = B * L
    NT = ROWS // P
    KD, KC, KE = D // P, DC // P, E // P
    FT = S // P
    TAIL = S - FT * P
    NJ = FT + 1
    GROUPS = [range(0, 4), range(4, 9), range(9, NJ)]
    NG = len(GROUPS)
    GROUP_OF = {j: g for g, js in enumerate(GROUPS) for j in js}
    BANKT = 512 // L
    SCALE = float(E) ** -0.5
    EPS = 1e-5
    SHIFT = 9.0

    ctx = ExitStack()
    with ctx:
        def sb(name, shape, dt=F32, stack=ctx):
            return stack.enter_context(nc.sbuf_tensor(name, shape, dt))

        def sem(name):
            return ctx.enter_context(nc.semaphore(name))

        bank = [ctx.enter_context(nc.psum_tensor(f"bank{i}", [P, 512], F32)) for i in range(2)]
        scores_ps = [ctx.enter_context(nc.psum_tensor(f"scores_ps{i}", [P, 1024], F32)) for i in range(2)]
        u_ps = ctx.enter_context(nc.psum_tensor("u_ps", [P, 512], F32))
        max_ps = ctx.enter_context(nc.psum_tensor("max_ps", [P, 512], F32))

        ones_f = sb("ones_f", [P, P])
        ident_f = sb("ident_f", [P, P])
        ident_h = sb("ident_h", [P, P], F16)
        ones_h = sb("ones_h", [P, P], F16)
        ones_b = sb("ones_b", [P, P], BF16)
        minus_half = sb("minus_half", [P, 16])
        x_sb = sb("x_sb", [P, NT, D])
        VEC = {}
        rows = 0
        for key, n in (("xattn_ln1_g", KD), ("xattn_ln1_b", KD), ("xattn_bq", KE), ("xattn_bk", KE),
                       ("xattn_ln2_g", KC), ("xattn_ln2_b", KC), ("xattn_bv", KE), ("attn_bq", KD),
                       ("attn_bk", KD), ("ffn_b1", A["L0_ffn_b1"].shape[0] // P)):
            VEC[key] = (rows, n)
            rows += n
        NVEC = rows
        vec_rows = sb("vec_rows", [NVEC, P])
        vec = sb("vec", [P, NVEC])
        vec_s = sb("vec_s", [P, NVEC])

        def cols(key, c):
            return vec_s[:, VEC[key][0] + c:VEC[key][0] + c + 1]

        def col(key, c):
            return vec[:, VEC[key][0] + c:VEC[key][0] + c + 1]

        x1T = sb("x1T", [P, KD, ROWS])
        cT = x1T[:, 0:KC, :]
        AREA = 172 * 1024
        area = sb("area", [P, AREA // 4])

        def carve(at, shape, dt=F32):
            size = 1
            for n in shape[1:]:
                size *= n
            size *= mybir.dt.size(dt)
            assert at % 4 == 0 and at + size <= AREA, (at, size)
            v = area[0:shape[0], at // 4:(at + size + 3) // 4]
            v = v if dt == F32 else v.bitcast(dt)
            if len(shape) > 2:
                letters = "abcde"[:len(shape) - 1]
                v = v.rearrange(f"p ({' '.join(letters)}) -> p {' '.join(letters)}", **{l: n for l, n in zip(letters[1:], shape[2:])})
            return v, at + (size + 3) // 4 * 4

        at = 0
        wq, at = carve(at, [P, KD, E])
        wk, at = carve(at, [P, KC, E])
        wkT, at = carve(at, [P, KE, DC])
        y, at = carve(at, [P, NT, D])
        qT, _ = carve(at - NT * D * 4, [P, KE, ROWS])
        a_f, at = carve(at, [P, KC + 1, 512])
        END_A = at
        ln_st = sb("ln_st", [P, NT, 6])
        ln_mv = sb("ln_mv", [P, NT, 2])
        ln_ve = sb("ln_ve", [P, NT])
        ln_r = sb("ln_r", [P, NT])

        def pair(shape, dt=F32):
            nonlocal at
            v0, at = carve(at, shape, dt)
            v1, at = carve(at, shape, dt)
            return [v0, v1]

        a_all, at = carve(at, [P, B, 12, L], BF16)
        raw = pair([P, NJ, DC])
        xh = pair([P, NJ, DC], F16)
        xl = pair([P, NJ, DC], F16)
        xT = pair([P, 2, KC, P], F16)
        st = pair([P, NJ, 6])
        mv = pair([P, NJ, 2])
        ve = pair([P, NJ])
        rs = pair([P, NJ])
        nb = pair([P, NJ])
        acur = pair([P, 12, L], BF16)
        pf = pair([P, NJ, L])
        ph = pair([P, NJ, L], F16)
        pl = pair([P, NJ, L], F16)
        mxa, at = carve(at, [P, L])
        mxb, at = carve(at, [P, L])
        mx, at = carve(at, [P, P])
        mq, at = carve(at, [L, 1])
        mbc, at = carve(at, [P, L])
        rz, at = carve(at, [P, L])


        F = A["L0_ffn_b1"].shape[0]
        KF = F // P
        H = D // A["L0_attn_rel_emb"].shape[1]
        DH = D // H
        HC = P // DH
        HP = H // 2
        REL = 2 * L
        MAXP = (A["L0_attn_rel_emb"].shape[0] + 1) // 2
        at = 0
        xwv, at = carve(at, [P, KC, E])
        xwo, at = carve(at, [P, KE, D])
        awq, at = carve(at, [P, KD, D])
        awk, at = carve(at, [P, KD, D])
        awv, at = carve(at, [P, KD, D])
        awo, at = carve(at, [P, KD, D])
        w1T, at = carve(at, [P, KD, F], F16)
        w2T, at = carve(at, [P, KF, D], F16)
        rel_rows, at = carve(at, [REL, HC, DH])
        relbd, at = carve(at, [P, HC, REL])
        xbo, at = carve(at, [P, D])
        abo, at = carve(at, [P, D])
        fb2, at = carve(at, [P, D])
        abv, at = carve(at, [P, HP * DH])
        small, at = carve(at, [P, 64])
        BUF = at
        wraw, at = carve(at, [P, 4 * F])
        wneg, at = carve(at, [P, 4 * F], F16)
        wter, at = carve(at, [P, 4 * F], F16)
        at = BUF
        c2T, at = carve(at, [P, KC, P])
        vT, at = carve(at, [P, KE, P])
        yn, at = carve(at, [P, D])
        yT, at = carve(at, [P, KD, P])
        q2T, at = carve(at, [P, KD, P])
        kbd, at = carve(at, [P, KD, 2, HC, L])
        vbd, at = carve(at, [P, HP, 2, 2, DH])
        gs, at = carve(at, [P, H, REL])
        rsk, at = carve(at, [P, H, L])
        ssb, at = carve(at, [P, H, L])
        psb, at = carve(at, [P, H, L])
        ptT, at = carve(at, [P, HP, P])
        ctxT, at = carve(at, [P, KD, P])
        zn, at = carve(at, [P, D])
        zh, at = carve(at, [P, KD, P], F16)
        zl, at = carve(at, [P, KD, P], F16)
        gf, at = carve(at, [P, KF, P])
        gh, at = carve(at, [P, KF, P], F16)
        gl, at = carve(at, [P, KF, P], F16)
        xb2, at = carve(at, [P, D])
        ot, at = carve(at, [P, D])
        xc, at = carve(at, [P, D])
        zc, at = carve(at, [P, D])
        def sm(a, n=1):
            return small[:, a:a + n]
        STAT1, MV1, VE1, RS1, STAT2, MV2, VE2, RS2 = 0, 6, 8, 9, 10, 16, 18, 19
        WSUM, WSCALE, WTHR, WNTHR, BMAX, FS, FINV, BEXP = 20, 36, 37, 38, 39, 40, 41, 42
        ksc = sb("ksc", [P, KD])
        rows16, _ = carve(at, [P, 6, H]); at = _
        skew = nc.dram_tensor("skew", (P, H * REL), F32, kind="Internal").ap()
        anti_f = sb("anti_f", [P, P])
        ws, wr, ww = bank[0], bank[1], max_ps
        gbank = [scores_ps[1][:, 0:512], scores_ps[1][:, 512:1024]]

        names = """consts_ready ident_ready vec_loaded vec_T vec_ready x_loaded wq_loaded wk_loaded
            ln_stat ln_aggr ln_var ln_rstd ln_done xT_ready x1T_ready wkT_ps wkT_ready q_ready qT_ready ua_ready a_step
            a_ready raw_tail_zero bn_done aggr_done var_ready negmu_ready rstd_ready nb_ready xn_done hi_ready lo_ready
            tp_ready evac_done score_done max_a max_b max_tail max_all maxT_ready maxq_ready maxbc_ready maxbc_copied
            sub_done exp_done ph_ready pl_ready pv_done rz_ready c_ready out_stored
            dense_loaded rows_loaded w_loaded zeros_done rel_ps rel_step ab_step sum_ps ternary_step turned_w_ps turned_w
            c2_ready v_ps v_taken o_ps o_taken yT_ps yT_taken q2_ps q2_taken k2_ps k2_taken v2_ps v2_taken
            g_ps g_taken g_stored r_loaded s_ps s_step clip_done radd_done rowmax_done rowsub_done rowexp_done rowsum_done
            inv_step pn_done pt_ps pt_taken ctx_ps ctx_taken ao_ps ao_taken zT_ps zh_taken zT_taken f_ps gelu_done
            gh_ready gl_ready0 gl_ready1 out_ps out_ready x1_step st1 ag1 va1 rs1 y_ready st2 ag2 va2 rs2 z_ready xb_ready
            xb2_ready stored ab2_step""".split()
        s = {n: sem(n) for n in names}
        raw_loaded = [[sem(f"raw_loaded{u}{g}") for g in range(NG)] for u in range(2)]
        acur_loaded = [sem(f"acur_loaded{u}") for u in range(2)]

        ctx_in = A["ctx_768"]

        FBANK = [wr, ww, wr, ww]
        GW = 2 * KD

        def before(k, u):
            return (k, 0) if u == 1 else (k - 1, 1)

        def after(k, u):
            return (k, 1) if u == 0 else (k + 1, 0)

        def turned(u, j):
            return bank[(u + j) % 2][:, 0:KC * P].bitcast(F16).rearrange("p (h c k) -> p h c k", h=2, c=KC)

        PV_AT = {j: (2, [j + 5]) for j in range(8)}
        PV_AT |= {9: (1, [0, 1]), 10: (1, [2]), 11: (1, [3]), 12: (1, [4])}

        def back(k, u, d):
            return (k, u) if d == 0 else back(*before(k, u), d - 1)

        def at_least(eng, semaphore, value):
            if not (isinstance(value, int) and value <= 0):
                eng.wait_ge(semaphore, value)

        def wait_alone(eng, semaphore, value):
            eng.wait_ge(s["ident_ready"], 1)
            eng.wait_ge(semaphore, value)

        out_rows = out.rearrange("b l d -> (b l) d")

        def rows(t):
            return slice(t * P, (t + 1) * P) if isinstance(t, int) else bass.ds(t * P, P)

        def tile(t):
            return x_sb[:, t, :] if isinstance(t, int) else x_sb[:, bass.ds(t, 1), :].squeeze(1)

        def run_dense(eng, step):
            step(0, True, False, False)
            step(1, True, True, False)
            step(2, True, True, True)
            with eng.Fori(3, NT) as t:
                step(t, True, True, True)
            step(NT, False, True, True)
            step(NT + 1, False, False, True)

        block = ctx.enter_context(nc.Block())

        @block.sync
        def _(sp):
            for t in range(NT):
                sp.dma_start(x_sb[:, t, :], A["x"].rearrange("b l d -> (b l) d")[t * P:(t + 1) * P, :]).then_inc(s["x_loaded"], 16)
            for key, (r, n) in VEC.items():
                sp.dma_start(vec_rows[r:r + n, :], A["L0_" + key].rearrange("(c p) -> c p", p=P)).then_inc(s["vec_loaded"], 16)
            sp.dma_start(wk[:, :, :], A["L0_xattn_Wk"].rearrange("(c p) e -> p c e", p=P)).then_inc(s["wk_loaded"], 16)
            sp.dma_start(wq[:, :, :], A["L0_xattn_Wq"].rearrange("(c p) e -> p c e", p=P)).then_inc(s["wq_loaded"], 16)

            def load_group(n, u, g):
                full = ctx_in[n, 0:FT * P, :] if isinstance(n, int) else ctx_in[bass.ds(n, 1), 0:FT * P, :].squeeze(0)
                full = full.rearrange("(p j) d -> p j d", j=FT)
                js = [j for j in GROUPS[g] if j < FT]
                sp.dma_start(raw[u][:, js[0]:js[-1] + 1, :], full[:, js[0]:js[-1] + 1, :]).then_inc(raw_loaded[u][g], 16)
                if g == NG - 1:
                    tail = ctx_in[n, FT * P:S, :] if isinstance(n, int) else ctx_in[bass.ds(n, 1), FT * P:S, :].squeeze(0)
                    sp.dma_start(raw[u][0:TAIL, FT, :], tail).then_inc(raw_loaded[u][g], 16)

            for n in range(2):
                for g in range(NG):
                    load_group(n, n, g)

            def load_a(n, u):
                sp.dma_start(acur[u][:, :, :], a_all[:, n, :, :] if isinstance(n, int) else
                             a_all[:, bass.ds(n, 1), :, :].squeeze(1)).then_inc(acur_loaded[u], 16)

            sp.wait_ge(s["a_ready"], 2)
            load_a(0, 0)
            load_a(1, 1)
            with sp.Fori(0, B // 2 - 1) as k:
                for u in range(2):
                    for g in range(NG):
                        wait_alone(sp, s["lo_ready"], NJ * 2 * k + NJ * u + GROUPS[g][-1] + 1)
                        load_group(2 * k + 2 + u, u, g)
                    wait_alone(sp, s["score_done"], NJ * 2 * k + NJ * (u + 1))
                    load_a(2 * k + 2 + u, u)

            sp.wait_ge(s["c_ready"], B)
            for dst, key in ((xwv, "xattn_Wv"), (xwo, "xattn_Wo"), (awq, "attn_Wq"), (awk, "attn_Wk"), (awv, "attn_Wv"), (awo, "attn_Wo")):
                sp.dma_start(dst, A["L0_" + key].rearrange("(c p) e -> p c e", p=P)).then_inc(s["dense_loaded"], 16)
            first_rel = MAXP - 1 - L
            for h in range(HC):
                sp.dma_start(rel_rows[:, h, :], A["L0_attn_rel_emb"][first_rel:first_rel + REL, :]).then_inc(s["rows_loaded"], 16)
            for dst, key in ((xbo, "xattn_bo"), (abo, "attn_bo"), (fb2, "ffn_b2")):
                sp.dma_start(dst, A["L0_" + key].partition_broadcast(P)).then_inc(s["rows_loaded"], 16)
            bv = A["L0_attn_bv"].rearrange("(hp two d) -> two hp d", two=2, d=DH)
            for v in range(2):
                sp.dma_start(abv[v * L:(v + 1) * L, :].rearrange("p (hp d) -> p hp d", d=DH), bv[v].partition_broadcast(L)).then_inc(s["rows_loaded"], 16)
            sp.dma_start(wraw[:, :].rearrange("p (c e) -> p c e", c=KF), A["L0_ffn_W1"].rearrange("(c p) e -> p c e", p=P)).then_inc(s["w_loaded"], 16)
            sp.wait_ge(s["ternary_step"], 5)
            sp.dma_start(wraw[:, :].rearrange("p (c e) -> p c e", c=KD), A["L0_ffn_W2"].rearrange("(c p) e -> p c e", p=P)).then_inc(s["w_loaded"], 16)

            def skew_store(t):
                at_least(sp, s["radd_done"], t)
                sp.wait_ge(s["g_taken"], KD * (t + 1))
                sp.dma_start(skew, gs.rearrange("p h r -> p (h r)")).then_inc(s["g_stored"], 16)

            def skew_load(t):
                sp.wait_ge(s["g_stored"], 16 * (t + 1))
                for v in range(2):
                    src = bass.AP(tensor=skew.tensor, offset=v * L * H * REL + L - 1, ap=[[H * REL - 1, L], [REL, H], [1, L]])
                    sp.dma_start(rsk[v * L:(v + 1) * L, :, :], src).then_inc(s["r_loaded"], 16)

            def store(t):
                wait_alone(sp, s["out_ready"], t + 1)
                sp.dma_start(out_rows[rows(t), :], ot).then_inc(s["stored"], 16)

            def dense(t, c1, c2, c3):
                if c1:
                    skew_store(t)
                    skew_load(t)
                if c3:
                    store(t - 2)
            run_dense(sp, dense)
            sp.wait_ge(s["stored"], 16 * NT)

        @block.gpsimd
        def _(pool):
            pool.memset(ones_f[:, :], 1.0).then_inc(s["consts_ready"], 1)
            pool.memset(minus_half[:, :], -0.5).then_inc(s["consts_ready"], 1)
            pool.wait_ge(s["consts_ready"], 2)
            pool.affine_select(out=ident_f[:, :], in_=ones_f[:, :], compare_op=ALU.is_equal, fill=0.0, base=0,
                               pattern=[[-1, P]], channel_multiplier=1).then_inc(s["ident_ready"], 1)
            for i in range(2):
                pool.wait_ge(s["ln_var"], i + 1)
                pool.tensor_tensor(ln_r[:, :], ln_ve[:, :], minus_half[:, 0:NT], ALU.pow).then_inc(s["ln_rstd"], 1)

            def rstd(k, u, g):
                n = 2 * k + u
                js = GROUPS[g]
                sl = slice(js[0], js[-1] + 1)
                pool.wait_ge(s["var_ready"], NG * n + g + 1)
                pool.tensor_tensor(rs[u][:, sl], ve[u][:, sl], minus_half[:, 0:len(js)], ALU.pow).then_inc(s["rstd_ready"], 1)
                pool.wait_ge(s["rstd_ready"], NG * n + g + 1)
                pool.tensor_tensor(nb[u][:, sl], nb[u][:, sl], rs[u][:, sl], ALU.mult).then_inc(s["nb_ready"], 1)

            def low_part(k, u, j):
                n = 2 * k + u
                m = P if j < FT else TAIL
                pool.wait_ge(s["hi_ready"], NJ * n + j + 1)
                pool.tensor_tensor(xl[u][0:m, j, :], raw[u][0:m, j, :], xh[u][0:m, j, :], ALU.subtract).then_inc(s["lo_ready"], 1)

            def p_low(k, u):
                n = 2 * k + u
                pool.wait_ge(s["ph_ready"], n + 1)
                pool.tensor_tensor(pl[u][:, :, :], pf[u][:, :, :], ph[u][:, :, :], ALU.subtract).then_inc(s["pl_ready"], 1)

            def step(k, u, first=False, last=False):
                for j in range(NJ):
                    low_part(k, u, j)
                    if j == 1:
                        rstd(k, u, 1)
                    if j == 5:
                        rstd(k, u, 2)
                    if j == 9 and not last:
                        rstd(*after(k, u), 0)
                    if j == 10 and not first:
                        p_low(*before(k, u))

            rstd(0, 0, 0)
            step(0, 0, first=True)
            step(0, 1)
            with pool.Fori(1, B // 2 - 1) as k:
                step(k, 0)
                step(k, 1)
            step(B // 2 - 1, 0)
            step(B // 2 - 1, 1, last=True)
            p_low(B // 2 - 1, 1)

            def pw(a, b, t, var, done):
                pool.wait_ge(s[var], t + 1)
                pool.tensor_tensor(sm(b), sm(a), minus_half[:, 0:1], ALU.pow).then_inc(s[done], 1)

            pool.affine_select(out=anti_f[:, :], in_=ones_f[:, :], compare_op=ALU.is_equal, fill=0.0, base=-(P - 1),
                               pattern=[[1, P]], channel_multiplier=1).then_inc(s["rel_step"], 1)

            pool.wait_ge(s["c_ready"], B)
            pool.wait_ge(s["rows_loaded"], 16 * (HC + 5))
            for t in range(NT):
                pool.tensor_tensor(x_sb[:, t, :], x_sb[:, t, :], xbo, ALU.add).then_inc(s["xb_ready"], 1)

            def dense(t, c1, c2, c3):
                if c1:
                    pw(VE1, RS1, t, "va1", "rs1")
                if c2:
                    pw(VE2, RS2, t - 1, "va2", "rs2")
                    pool.wait_ge(s["ao_taken"], t)
                    at_least(pool, s["out_ready"], t - 1)
                    pool.tensor_tensor(xb2, zc, fb2, ALU.add).then_inc(s["xb2_ready"], 1)
            run_dense(pool, dense)

        @block.scalar
        def _(act):
            act.wait_ge(s["ident_ready"], 1)
            act.copy(ident_h[:, :], ident_f[:, :]).then_inc(s["ident_ready"], 1)
            act.copy(ones_h[:, :], ones_f[:, :]).then_inc(s["ident_ready"], 1)
            act.copy(ones_b[:, :], ones_f[:, :]).then_inc(s["ident_ready"], 1)
            for e in range(KE):
                act.wait_ge(s["wkT_ps"], e + 1)
                act.copy(wkT[:, e, :], bank[e % 2][:, 0:DC]).then_inc(s["wkT_ready"], 1)
            for h in range(2):
                for m in range(KE):
                    i = KE * h + m
                    act.wait_ge(s["q_ready"], i + 1)
                    act.activation(qT[:, m, h * 512:(h + 1) * 512], bank[i % 2][:, :], ACT.Identity, bias=col("xattn_bq", m),
                                   scale=1.0).then_inc(s["qT_ready"], 1)

            def norm(k, u, j):
                n = 2 * k + u
                m = P if j < FT else TAIL
                act.wait_ge(s["nb_ready"], NG * n + GROUP_OF[j] + 1)
                act.activation(raw[u][0:m, j, :], raw[u][0:m, j, :], ACT.Identity, bias=nb[u][0:m, j:j + 1],
                               scale=rs[u][0:m, j:j + 1]).then_inc(s["xn_done"], 1)

            def high_part(k, u, j):
                n = 2 * k + u
                m = P if j < FT else TAIL
                act.wait_ge(s["xn_done"], NJ * n + j + 1)
                at_least(act, s["pv_done"], NJ * (n - 2) + j + 1 if not isinstance(n, int) or n >= 2 else 0)
                act.copy(xh[u][0:m, j, :], raw[u][0:m, j, :]).then_inc(s["hi_ready"], 1)

            def exps(k, u):
                n = 2 * k + u
                act.wait_ge(s["sub_done"], n + 1)
                act.activation(pf[u][:, :, :], pf[u][:, :, :], ACT.Exp, bias=0.0, scale=1.0).then_inc(s["exp_done"], 1)

            def p_high(k, u):
                n = 2 * k + u
                act.wait_ge(s["exp_done"], n + 1)
                act.copy(ph[u][:, :, :], pf[u][:, :, :]).then_inc(s["ph_ready"], 1)

            def step(k, u, first=False):
                for j in range(NJ):
                    norm(k, u, j)
                    if j >= 1:
                        high_part(k, u, j - 1)
                    if j == 8 and not first:
                        exps(*before(k, u))
                    if j == 9 and not first:
                        p_high(*before(k, u))
                high_part(k, u, NJ - 1)

            step(0, 0, first=True)
            step(0, 1)
            with act.Fori(1, B // 2 - 1) as k:
                step(k, 0)
                step(k, 1)
            step(B // 2 - 1, 0)
            step(B // 2 - 1, 1)
            exps(B // 2 - 1, 1)
            p_high(B // 2 - 1, 1)

            def v_out(t):
                act.wait_ge(s["v_ps"], t + 1)
                for m in range(KE):
                    act.activation(vT[:, m, :], ws[:, m * P:(m + 1) * P], ACT.Identity, bias=col("xattn_bv", m), scale=1.0).then_inc(s["v_taken"], 1)

            def gelus(t, half):
                for f4 in range(2 * half, 2 * half + 2):
                    act.wait_ge(s["f_ps"], 4 * t + f4 + 1)
                    if f4 % 2 == 0:
                        at_least(act, s["gl_ready%d" % half], t)
                    for f in range(4):
                        act.activation(gf[:, 4 * f4 + f, :], FBANK[f4][:, f * P:(f + 1) * P], ACT.Gelu, bias=col("ffn_b1", 4 * f4 + f),
                                       scale=1.0).then_inc(s["gelu_done"], 1)

            def row_exp(t):
                act.wait_ge(s["rowsub_done"], t + 1)
                act.activation(psb, ssb, ACT.Exp, bias=0.0, scale=1.0).then_inc(s["rowexp_done"], 1)

            def pt_out(t):
                for i in range(2):
                    act.wait_ge(s["pt_ps"], 2 * t + i + 1)
                    at_least(act, s["ctx_ps"], 2 * t)
                    act.copy(ptT[:, 4 * i:4 * i + 4, :].rearrange("p a b -> p (a b)"), gbank[i]).then_inc(s["pt_taken"], 1)

            def yT_out(t):
                act.wait_ge(s["yT_ps"], t + 1)
                at_least(act, s["v2_ps"], t)
                act.copy(yT.rearrange("p a b -> p (a b)"), ws[:, :]).then_inc(s["yT_taken"], 1)

            def qk_out(t):
                act.wait_ge(s["q2_ps"], t + 1)
                for m in range(KD):
                    act.activation(q2T[:, m, :], wr[:, m * P:(m + 1) * P], ACT.Identity, bias=col("attn_bq", m), scale=1.0).then_inc(s["q2_taken"], 1)
                act.wait_ge(s["k2_ps"], t + 1)
                for m in range(KD):
                    for h in range(HC):
                        act.activation(kbd[h * DH:(h + 1) * DH, m, :, h, :],
                                       ww[h * DH:(h + 1) * DH, m * P:(m + 1) * P].rearrange("p (b j) -> p b j", b=2), ACT.Identity,
                                       bias=ksc[h * DH:(h + 1) * DH, m:m + 1], scale=DH ** -0.5).then_inc(s["k2_taken"], 1)

            def g_out(t, cs):
                for c in cs:
                    act.wait_ge(s["g_ps"], KD * t + c + 1)
                    if c == cs[0]:
                        at_least(act, s["g_stored"], 16 * t)
                    act.copy(gs[:, HC * c:HC * (c + 1), :].rearrange("p a b -> p (a b)"), gbank[c % 2]).then_inc(s["g_taken"], 1)

            def z_out(t):
                act.wait_ge(s["zT_ps"], t + 1)
                at_least(act, s["f_ps"], 4 * t)
                act.copy(zh.rearrange("p a b -> p (a b)"), ww[:, :]).then_inc(s["zh_taken"], 1)

            def dense(t, c1, c2, c3):
                if c1:
                    v_out(t)
                if c3:
                    gelus(t - 2, 0)
                if c2:
                    row_exp(t - 1)
                if c3:
                    gelus(t - 2, 1)
                if c2:
                    pt_out(t - 1)
                if c1:
                    yT_out(t)
                    qk_out(t)
                    g_out(t, range(KD))
                if c2:
                    z_out(t - 1)
            act.wait_ge(s["ab_step"], 2)
            run_dense(act, dense)

        @block.tensor
        def _(pe):
            pe.wait_ge(s["ident_ready"], 4)
            pe.wait_ge(s["vec_loaded"], 16 * len(VEC))
            pe.transpose(max_ps[:, 0:NVEC], vec_rows[:, :], ident_f[0:NVEC, 0:NVEC]).then_inc(s["vec_T"], 1)
            pe.wait_ge(s["wk_loaded"], 16)
            for e in range(KE):
                if e >= 2:
                    pe.wait_ge(s["wkT_ready"], e - 1)
                for c in range(KC):
                    ins = pe.transpose(bank[e % 2][:, c * P:(c + 1) * P], wk[:, c, e * P:(e + 1) * P], ident_f[:, :])
                ins.then_inc(s["wkT_ps"], 1)
            tb = [scores_ps[0][:, 0:512], scores_ps[0][:, 512:1024], scores_ps[1][:, 0:512], scores_ps[1][:, 512:1024]]
            for t in range(NT):
                pe.wait_ge(s["ln_done"], 9 + t)
                if t >= 4:
                    pe.wait_ge(s["x1T_ready"], KD * (t - 3))
                for c in range(KD):
                    ins = pe.transpose(tb[t % 4][:, c * P:(c + 1) * P], y[:, t, c * P:(c + 1) * P], ident_f[:, :])
                ins.then_inc(s["xT_ready"], 1)
            pe.wait_ge(s["wq_loaded"], 16)
            pe.wait_ge(s["x1T_ready"], KD * NT)
            pe.wait_ge(s["wkT_ready"], KE)
            for h in range(2):
                for m in range(KE):
                    i = KE * h + m
                    if i >= 2:
                        pe.wait_ge(s["qT_ready"], i - 1)
                    for c in range(KD):
                        ins = pe.matmul(bank[i % 2][:, :], wq[:, c, m * P:(m + 1) * P], x1T[:, c, h * 512:(h + 1) * 512],
                                        start=(c == 0), stop=(c == KD - 1))
                    ins.then_inc(s["q_ready"], 1)
            for h in range(2):
                pe.wait_ge(s["qT_ready"], KE * (h + 1))
                at_least(pe, s["a_step"], h * (KE + 2 * KC))
                for m in range(KC):
                    for e in range(KE):
                        ins = pe.matmul(tb[m][:, :], wkT[:, e, m * P:(m + 1) * P], qT[:, e, h * 512:(h + 1) * 512],
                                        start=(e == 0), stop=(e == KE - 1))
                ins.then_inc(s["ua_ready"], 1)
        
            def turn(k, u, j):
                n, m = 2 * k + u, P if j < FT else TAIL
                pe.wait_ge(s["lo_ready"], NJ * n + j + 1)
                at_least(pe, s["evac_done"], NJ * n + j - 1)
                tp = turned(u, j)
                for h, src in enumerate((xh, xl)):
                    for c in range(KC):
                        ins = pe.transpose(tp[:, h, c, 0:m], src[u][0:m, j, c * P:(c + 1) * P], ident_h[0:m, 0:m])
                ins.then_inc(s["tp_ready"], 1)

            def scores(k, u, j):
                n, m = 2 * k + u, P if j < FT else TAIL
                if j == 0:
                    at_least(pe, s["sub_done"], n - 1)
                    pe.wait_ge(acur_loaded[u], 16 * (k + 1))
                if j % BANKT == 0:
                    w = min(BANKT, NJ - j)
                    o = scores_ps[u][:, j * L:(j + w) * L].rearrange("p (t q) -> p t q", t=w)
                    for part in range(3):
                        pe.matmul(o, ones_b[:, :], acur[u][:, 4 * part + 3, :].unsqueeze(1).to_broadcast([P, w, L]),
                                  start=(part == 0), stop=False, skip_group_check=True)
                pe.wait_ge(s["evac_done"], NJ * n + j + 1)
                for c in range(KC):
                    for h, parts in ((0, range(3)), (1, range(2))):
                        for part in parts:
                            ins = pe.matmul(scores_ps[u][0:m, j * L:(j + 1) * L], xT[(u + j) % 2][:, h, c, 0:m],
                                            acur[u][:, 4 * part + c, :], start=False, stop=(c == KC - 1 and h == 1 and part == 1),
                                            skip_group_check=True)
                ins.then_inc(s["score_done"], 1)

            def turn_max(k, u):
                pe.wait_ge(s["max_all"], 2 * k + u + 1)
                pe.transpose(max_ps[:, 0:P], mx[:, :], ident_f[:, :]).then_inc(s["maxT_ready"], 1)

            def spread_max(k, u):
                pe.wait_ge(s["maxq_ready"], 2 * k + u + 1)
                pe.matmul(max_ps[:, P:P + L], mq[:, 0:1].to_broadcast([L, P]), ident_f[0:L, 0:L], start=True,
                          stop=True).then_inc(s["maxbc_ready"], 1)

            def products(k, u, js):
                n = 2 * k + u
                if js[0] == 0:
                    pe.wait_ge(s["pl_ready"], n + 1)
                    at_least(pe, s["c_ready"], n)
                for j in js:
                    m = P if j < FT else TAIL
                    for c in range(KC):
                        for a, b in ((xh, ph), (xh, pl), (xl, ph)):
                            pe.matmul(u_ps[:, c * L:(c + 1) * L], a[u][0:m, j, c * P:(c + 1) * P], b[u][0:m, j, :],
                                      start=(j == 0 and c == 0 and a is xh and b is ph), stop=(j == NJ - 1 and a is xl),
                                      skip_group_check=True)
                    for b in (ph, pl):
                        ins = pe.matmul(u_ps[:, KC * L:(KC + 1) * L], ones_h[0:m, :], b[u][0:m, j, :], start=False,
                                        stop=(j == NJ - 1 and b is pl), skip_group_check=True)
                    ins.then_inc(s["pv_done"], 1)

            def step(k, u, done=2):
                for j in range(NJ):
                    turn(k, u, j)
                    if j >= 1:
                        scores(k, u, j - 1)
                    elif done:
                        scores(*before(k, u), NJ - 1)
                    if done:
                        if j == 1:
                            turn_max(*before(k, u))
                        if j == 2:
                            spread_max(*before(k, u))
                    if j in PV_AT and PV_AT[j][0] <= done:
                        products(*back(k, u, PV_AT[j][0]), PV_AT[j][1])

            step(0, 0, done=0)
            step(0, 1, done=1)
            with pe.Fori(1, B // 2 - 1) as k:
                step(k, 0)
                step(k, 1)
            step(B // 2 - 1, 0)
            step(B // 2 - 1, 1)
            scores(B // 2 - 1, 1, NJ - 1)
            products(B // 2 - 1, 0, range(5, NJ))
            turn_max(B // 2 - 1, 1)
            spread_max(B // 2 - 1, 1)
            products(B // 2 - 1, 1, range(NJ))

            pe.wait_ge(s["c_ready"], B)
            pe.wait_ge(s["rel_step"], 1)
            pe.wait_ge(s["rows_loaded"], 16 * (HC + 5))
            pe.matmul(ws[:, 0:REL], rel_rows.rearrange("r h d -> r (h d)"), anti_f[:, :], start=True, stop=True).then_inc(s["rel_ps"], 1)
            pe.wait_ge(s["ab_step"], 1)
            pe.transpose(ws[0:1, 256:384], sm(BMAX), ident_f[:, :]).then_inc(s["rel_ps"], 1)
            pe.wait_ge(s["ab_step"], 2)
            pe.matmul(ws[:, 384:386], ones_f[0:1, :], small[0:1, 44:46], start=True, stop=True).then_inc(s["rel_ps"], 1)
            for w in range(2):
                pe.wait_ge(s["ternary_step"], 5 * w + 1)
                pe.matmul(wr[:, 0:16], ones_f[:, :], sm(WSUM, 16), start=True, stop=True).then_inc(s["sum_ps"], 1)
                pe.wait_ge(s["ternary_step"], 5 * w + 5)
                tb = [ws, ww]
                wv = wter[:, :].rearrange("p (c e) -> p c e", c=KF if w == 0 else KD)
                nin, nout = (KF, KD) if w == 0 else (KD, KF)
                i = 0
                for o in range(nout):
                    for c8 in range(0, nin, 8 if nin > 4 else 4):
                        n8 = min(8, nin)
                        at_least(pe, s["turned_w"], GW * w + i - 1)
                        for c in range(c8, c8 + n8):
                            ins = pe.transpose(tb[i % 2][:, (c - c8) * P // 2:(c - c8 + 1) * P // 2].bitcast(F16), wv[:, c, o * P:(o + 1) * P], ident_h[:, :])
                        ins.then_inc(s["turned_w_ps"], 1)
                        i += 1
            pe.wait_ge(s["dense_loaded"], 16 * 6)
            pe.wait_ge(s["turned_w"], GW + KF)
            pe.wait_ge(s["zeros_done"], 2)

            def xattn_v(t):
                pe.wait_ge(s["c2_ready"], KC * (t + 1))
                at_least(pe, s["ao_taken"], t - 1)
                for m in range(KE):
                    for c in range(KC):
                        ins = pe.matmul(ws[:, m * P:(m + 1) * P], xwv[:, c, m * P:(m + 1) * P], c2T[:, c, :], start=(c == 0), stop=(c == KC - 1))
                ins.then_inc(s["v_ps"], 1)

            def xattn_o(t):
                pe.wait_ge(s["v_taken"], KE * (t + 1))
                for c in range(KE):
                    ins = pe.matmul(ws[:, :], vT[:, c, :], xwo[:, c, :], start=(c == 0), stop=(c == KE - 1))
                ins.then_inc(s["o_ps"], 1)

            def att_scores(t):
                pe.wait_ge(s["k2_taken"], KD * HC * (t + 1))
                pe.wait_ge(s["q2_taken"], KD * (t + 1))
                at_least(pe, s["ctx_taken"], 4 * t)
                for c in range(KD):
                    for v in range(2):
                        ins = pe.matmul(scores_ps[0][v * L:(v + 1) * L, c * HC * L:(c + 1) * HC * L], q2T[:, c, v * L:(v + 1) * L],
                                        kbd[:, c, v, :, :].rearrange("p h j -> p (h j)"), start=True, stop=True)
                ins.then_inc(s["s_ps"], 1)

            def ffn_in(t, half):
                for f4 in range(2 * half, 2 * half + 2):
                    if f4 == 0:
                        pe.wait_ge(s["zT_taken"], t + 1)
                    if f4 >= 2:
                        pe.wait_ge(s["gelu_done"], KF * t + 4 * (f4 - 1))
                    for f in range(4):
                        for c in range(KD):
                            for z in (zh, zl):
                                ins = pe.matmul(FBANK[f4][:, f * P:(f + 1) * P], w1T[:, c, (4 * f4 + f) * P:(4 * f4 + f + 1) * P], z[:, c, :],
                                                start=(c == 0 and z is zh), stop=(c == KD - 1 and z is zl))
                    ins.then_inc(s["f_ps"], 1)

            def att_turn(t):
                pe.wait_ge(s["pn_done"], t + 1)
                for i in range(2):
                    for q in range(4):
                        hp = 4 * i + q
                        ins = pe.transpose(gbank[i][:, q * P:(q + 1) * P], psb[:, 2 * hp:2 * hp + 2, :].rearrange("p a b -> p (a b)"), ident_f[:, :])
                    ins.then_inc(s["pt_ps"], 1)

            def y_turn(t):
                pe.wait_ge(s["y_ready"], t + 1)
                for c in range(KD):
                    ins = pe.transpose(ws[:, c * P:(c + 1) * P], yn[:, c * P:(c + 1) * P], ident_f[:, :])
                ins.then_inc(s["yT_ps"], 1)

            def ffn_out(t, half):
                pe.wait_ge(s["gl_ready%d" % half], t + 1)
                if half == 0:
                    at_least(pe, s["out_ready"], t)
                for f in range(KF // 2 * half, KF // 2 * (half + 1)):
                    for g in (gh, gl):
                        ins = pe.matmul(u_ps[:, :], g[:, f, :], w2T[:, f, :], start=(f == 0 and g is gh), stop=(f == KF - 1 and g is gl))
                if half == 1:
                    ins.then_inc(s["out_ps"], 1)

            def att_values(t):
                pe.wait_ge(s["pt_taken"], 2 * (t + 1))
                pe.wait_ge(s["v2_taken"], 2 * (t + 1))
                for i in range(2):
                    for q in range(4):
                        hp = 4 * i + q
                        ins = pe.matmul(scores_ps[0][:, hp * P:(hp + 1) * P], vbd[:, hp, :, :, :].rearrange("p a b c -> p (a b c)"), ptT[:, hp, :],
                                        start=True, stop=True)
                    ins.then_inc(s["ctx_ps"], 1)

            def qk(t):
                pe.wait_ge(s["yT_taken"], t + 1)
                for dst, w, done in ((wr, awq, "q2_ps"), (ww, awk, "k2_ps")):
                    for m in range(KD):
                        for c in range(KD):
                            ins = pe.matmul(dst[:, m * P:(m + 1) * P], w[:, c, m * P:(m + 1) * P], yT[:, c, :], start=(c == 0), stop=(c == KD - 1))
                    ins.then_inc(s[done], 1)

            def att_o(t):
                pe.wait_ge(s["ctx_taken"], 4 * (t + 1))
                for c in range(KD):
                    ins = pe.matmul(ws[:, :], ctxT[:, c, :], awo[:, c, :], start=(c == 0), stop=(c == KD - 1))
                ins.then_inc(s["ao_ps"], 1)

            def vg(t):
                pe.wait_ge(s["q2_taken"], KD * (t + 1))
                wv = awv.rearrange("p c (hp two d) -> p c two hp d", two=2, d=DH)
                for b2 in range(2):
                    for v in range(2):
                        for c in range(KD):
                            ins = pe.matmul(wr[v * L:(v + 1) * L, b2 * HP * DH:(b2 + 1) * HP * DH], yT[:, c, b2 * L:(b2 + 1) * L], wv[:, c, v, :, :],
                                            start=(c == 0), stop=(c == KD - 1))
                ins.then_inc(s["v2_ps"], 1)
                for c in range(KD):
                    if c >= 2:
                        pe.wait_ge(s["g_taken"], KD * t + c - 1)
                    pe.matmul(gbank[c % 2], q2T[:, c, :], relbd.rearrange("p h r -> p (h r)"), start=True, stop=True).then_inc(s["g_ps"], 1)

            def z_turn(t):
                pe.wait_ge(s["z_ready"], t + 1)
                for c in range(KD):
                    ins = pe.transpose(ww[:, c * P:(c + 1) * P], zn[:, c * P:(c + 1) * P], ident_f[:, :])
                ins.then_inc(s["zT_ps"], 1)

            def dense(t, c1, c2, c3):
                if c2:
                    att_scores(t - 1)
                if c1:
                    xattn_v(t)
                if c3:
                    ffn_in(t - 2, 0)
                if c1:
                    xattn_o(t)
                if c3:
                    ffn_in(t - 2, 1)
                if c2:
                    pe.wait_ge(s["g_taken"], KD * t)
                    att_turn(t - 1)
                if c1:
                    pe.wait_ge(s["o_taken"], t + 1)
                    y_turn(t)
                if c3:
                    ffn_out(t - 2, 0)
                if c2:
                    att_values(t - 1)
                if c1:
                    if c3:
                        pe.wait_ge(s["gelu_done"], KF * (t - 1))
                    at_least(pe, s["v2_taken"], 2 * t)
                    qk(t)
                if c2:
                    att_o(t - 1)
                if c1:
                    if c2:
                        pe.wait_ge(s["pt_taken"], 2 * t)
                    vg(t)
                if c3:
                    ffn_out(t - 2, 1)
                if c2:
                    if c1:
                        pe.wait_ge(s["k2_taken"], KD * HC * (t + 1))
                    elif c3:
                        pe.wait_ge(s["gelu_done"], KF * (t - 1))
                    z_turn(t - 1)
            run_dense(pe, dense)

        @block.vector
        def _(dve):
            def stats(k, u, j):
                m, g = P if j < FT else TAIL, GROUP_OF[j]
                if j == GROUPS[g][0]:
                    dve.wait_ge(raw_loaded[u][g], (32 if g == NG - 1 else 16) * (k + 1))
                dve.bn_stats(st[u][0:m, j, :], raw[u][0:m, j, :]).then_inc(s["bn_done"], 1)

            def gather(k, u, j):
                n, m = 2 * k + u, P if j < FT else TAIL
                if isinstance(n, int):
                    dve.wait_ge(s["bn_done"], NJ * n + j + 1)
                dve.bn_aggr(mv[u][0:m, j, :], st[u][0:m, j, :]).then_inc(s["aggr_done"], 1)
                if j == GROUPS[GROUP_OF[j]][-1]:
                    variances(k, u, GROUP_OF[j])

            def variances(k, u, g):
                n, js = 2 * k + u, GROUPS[g]
                sl = slice(js[0], js[-1] + 1)
                dve.wait_ge(s["aggr_done"], NJ * n + js[-1] + 1)
                dve.tensor_scalar(nb[u][:, sl], mv[u][:, sl, 0], -1.0, None, ALU.mult).then_inc(s["negmu_ready"], 1)
                dve.tensor_scalar(ve[u][:, sl], mv[u][:, sl, 1], EPS, None, ALU.add).then_inc(s["var_ready"], 1)

            def early_stats():
                dve.wait_ge(s["raw_tail_zero"], 3)
                for j in range(NJ - 1):
                    stats(0, 0, j)
                for j in range(NJ - 1):
                    gather(0, 0, j)

            dve.wait_ge(s["vec_T"], 1)
            dve.tensor_copy(vec[:, :], max_ps[:, 0:NVEC]).then_inc(s["vec_ready"], 1)
            dve.tensor_scalar(vec_s[:, :], max_ps[:, 0:NVEC], SCALE, None, ALU.mult).then_inc(s["vec_ready"], 1)
            dve.memset(mx[:, L:P], 0.0).then_inc(s["raw_tail_zero"], 1)
            for u in range(2):
                dve.memset(mv[u][:, :, :], 1.0).then_inc(s["raw_tail_zero"], 1)
            dve.wait_ge(s["x_loaded"], 16 * NT)
            for i, src in enumerate((x_sb, y)):
                at_least(dve, s["ln_done"], NT * i)
                for t in range(NT):
                    dve.bn_stats(ln_st[:, t, :], src[:, t, :]).then_inc(s["ln_stat"], 1)
                for t in range(NT):
                    dve.wait_ge(s["ln_stat"], NT * i + t + 1)
                    dve.bn_aggr(ln_mv[:, t, :], ln_st[:, t, :]).then_inc(s["ln_aggr"], 1)
                dve.wait_ge(s["ln_aggr"], NT * (i + 1))
                dve.tensor_scalar(ln_ve[:, :], ln_mv[:, :, 1], EPS, None, ALU.add).then_inc(s["ln_var"], 1)
                dve.wait_ge(s["ln_rstd"], i + 1)
                for t in range(NT):
                    dve.tensor_scalar(y[:, t, :], src[:, t, :], ln_mv[:, t, 0:1], ln_r[:, t:t + 1], ALU.subtract,
                                      ALU.mult).then_inc(s["ln_done"], 1)
            dve.wait_ge(s["vec_ready"], 2)
            tb = [scores_ps[0][:, 0:512], scores_ps[0][:, 512:1024], scores_ps[1][:, 0:512], scores_ps[1][:, 512:1024]]
            for t in range(NT):
                dve.wait_ge(s["xT_ready"], t + 1)
                for c in range(KD):
                    ins = dve.tensor_scalar(x1T[:, c, t * P:(t + 1) * P], tb[t % 4][:, c * P:(c + 1) * P], col("xattn_ln1_g", c),
                                            col("xattn_ln1_b", c), ALU.mult, ALU.add)
                    ins.then_inc(s["x1T_ready"], 1)
            early_stats()
            HB = 512 // L
            done = 0
            def link(ins):
                nonlocal done
                ins.then_inc(s["a_step"], 1)
                done += 1
                dve.wait_ge(s["a_step"], done)
            for h in range(2):
                dve.wait_ge(s["qT_ready"], KE * (h + 1))
                at_least(dve, s["a_ready"], h)
                link(dve.tensor_scalar(a_f[:, KC, :], qT[:, 0, h * 512:(h + 1) * 512], cols("xattn_bk", 0), None, ALU.mult))
                for e in range(1, KE):
                    link(dve.scalar_tensor_tensor(out=a_f[:, KC, :], in0=qT[:, e, h * 512:(h + 1) * 512], scalar=cols("xattn_bk", e),
                                                  in1=a_f[:, KC, :], op0=ALU.mult, op1=ALU.add))
                dve.wait_ge(s["ua_ready"], h + 1)
                for c in range(KC):
                    link(dve.scalar_tensor_tensor(out=a_f[:, KC, :], in0=tb[c][:, :], scalar=cols("xattn_ln2_b", c),
                                                  in1=a_f[:, KC, :], op0=ALU.mult, op1=ALU.add))
                for c in range(KC):
                    ins = dve.tensor_scalar(a_f[:, c, :], tb[c][:, :], cols("xattn_ln2_g", c), None, ALU.mult)
                    link(ins)
                src = a_f[:, :, :].rearrange("p c (b l) -> p c b l", l=L)
                for part in range(3):
                    for c in range(KC + 1):
                        dst = a_all[:, h * HB:(h + 1) * HB, 4 * part + c, :]
                        ins = dve.tensor_copy(dst, src[:, c, :, :])
                        if part == 2 and c == KC:
                            ins.then_inc(s["a_ready"], 1)
                        else:
                            link(ins)
                        if part < 2:
                            link(dve.tensor_tensor(src[:, c, :, :], src[:, c, :, :], dst, ALU.subtract))

            def evacuate(k, u, j, ahead):
                n, m = 2 * k + u, P if j < FT else TAIL + 1
                if ahead:
                    dve.wait_ge(s["bn_done"], NJ * (2 * ahead[0] + ahead[1]) + ahead[2] + 1)
                dve.wait_ge(s["tp_ready"], NJ * n + j + 1)
                at_least(dve, s["score_done"], NJ * n + j - 1)
                dve.tensor_copy(xT[(u + j) % 2][:, :, :, 0:m], turned(u, j)[:, :, :, 0:m]).then_inc(s["evac_done"], 1)

            def tiles_of(u, lo, hi):
                return scores_ps[u][:, lo * L:hi * L].rearrange("p (t q) -> p q t", q=L)

            def max_first(k, u):
                n = 2 * k + u
                dve.wait_ge(s["score_done"], NJ * n + BANKT)
                dve.tensor_reduce(mxa[:, :], tiles_of(u, 0, BANKT), AX.X, ALU.max).then_inc(s["max_a"], 1)

            def max_rest(k, u):
                n = 2 * k + u
                dve.wait_ge(s["score_done"], NJ * (n + 1))
                dve.tensor_reduce(mxb[:, :], tiles_of(u, BANKT, FT), AX.X, ALU.max).then_inc(s["max_b"], 1)
                dve.wait_ge(s["max_b"], n + 1)
                dve.tensor_tensor(mxb[0:TAIL, :], mxb[0:TAIL, :], scores_ps[u][0:TAIL, FT * L:NJ * L], ALU.max).then_inc(s["max_tail"], 1)
                dve.wait_ge(s["max_tail"], n + 1)
                dve.wait_ge(s["max_a"], n + 1)
                dve.tensor_tensor(mx[:, 0:L], mxa[:, :], mxb[:, :], ALU.max).then_inc(s["max_all"], 1)

            def max_of_query(k, u):
                n = 2 * k + u
                dve.wait_ge(s["maxT_ready"], n + 1)
                dve.tensor_reduce(mq[:, :], max_ps[0:L, 0:P], AX.X, ALU.max).then_inc(s["maxq_ready"], 1)

            def copy_max(k, u):
                n = 2 * k + u
                dve.wait_ge(s["maxbc_ready"], n + 1)
                dve.tensor_copy(mbc[:, :], max_ps[:, P:P + L]).then_inc(s["maxbc_copied"], 1)

            def subtract_max(k, u):
                n = 2 * k + u
                dve.wait_ge(s["maxbc_copied"], n + 1)
                at_least(dve, s["pl_ready"], n - 1)
                dve.tensor_tensor(pf[u][:, :, :], scores_ps[u][:, 0:NJ * L].rearrange("p (t q) -> p t q", q=L),
                                  mbc[:, :].unsqueeze(1).to_broadcast([P, NJ, L]), ALU.subtract).then_inc(s["sub_done"], 1)

            def context(k, u):
                n = 2 * k + u
                dve.wait_ge(s["pv_done"], NJ * (n + 1))
                dve.reciprocal(rz[:, :], u_ps[:, KC * L:(KC + 1) * L]).then_inc(s["rz_ready"], 1)
                dve.wait_ge(s["rz_ready"], n + 1)
                dve.tensor_tensor(cT[:, :, bass.ds(n * L, L)], u_ps[:, 0:KC * L].rearrange("p (c q) -> p c q", q=L),
                                  rz[:, :].unsqueeze(1).to_broadcast([P, KC, L]), ALU.mult).then_inc(s["c_ready"], 1)

            def step(k, u, done=2, last=False):
                for j in range(NJ):
                    ahead = (k, u, NJ - 1) if j == 0 else None if last else (*after(k, u), j - 1)
                    if ahead:
                        stats(*ahead)
                    if done and j == 1:
                        max_rest(*before(k, u))
                    evacuate(k, u, j, ahead)
                    if ahead:
                        gather(*ahead)
                    if done:
                        if j == 1:
                            max_of_query(*before(k, u))
                        if j == 3:
                            copy_max(*before(k, u))
                            subtract_max(*before(k, u))
                    if j == 8 and done == 2:
                        context(*back(k, u, 2))
                    if j == 9:
                        max_first(k, u)

            step(0, 0, done=0)
            step(0, 1, done=1)
            with dve.Fori(1, B // 2 - 1) as k:
                step(k, 0)
                step(k, 1)
            step(B // 2 - 1, 0)
            step(B // 2 - 1, 1, last=True)
            K = B // 2 - 1
            max_rest(K, 1)
            max_of_query(K, 1)
            copy_max(K, 1)
            subtract_max(K, 1)
            context(K, 0)
            context(K, 1)

            chain = [0]

            def link2(ins):
                chain[0] += 1
                ins.then_inc(s["ab2_step"], 1)
                dve.wait_ge(s["ab2_step"], chain[0])

            dve.wait_ge(s["c_ready"], B)
            dve.wait_ge(s["pl_ready"], B)
            dve.tensor_reduce(sm(BMAX), vec[:, VEC["ffn_b1"][0]:VEC["ffn_b1"][0] + KF], AX.X, ALU.max, apply_absolute_value=True).then_inc(s["ab_step"], 1)
            dve.wait_ge(s["rel_ps"], 2)
            dve.tensor_reduce(small[0:1, 44:45], ws[0:1, 256:384], AX.X, ALU.max).then_inc(s["inv_step"], 1)
            dve.tensor_reduce(small[0:1, 45:46], ws[0:1, 256:384], AX.X, ALU.max).then_inc(s["inv_step"], 1)
            dve.wait_ge(s["inv_step"], 2)
            dve.tensor_scalar(ksc[:, :], vec[:, VEC["attn_bk"][0]:VEC["attn_bk"][0] + KD], DH ** -0.5, None, ALU.mult).then_inc(s["ab_step"], 1)
            dve.wait_ge(s["rel_ps"], 3)
            INT = mybir.dt.int32
            link2(dve.tensor_scalar(sm(BEXP), ws[:, 384:385], float(D), None, ALU.add))
            link2(dve.tensor_scalar(sm(BEXP).bitcast(INT), sm(BEXP).bitcast(INT), 0x7F800000, None, ALU.bitwise_and))
            link2(dve.tensor_scalar(sm(FS).bitcast(INT), sm(BEXP).bitcast(INT), -1.0, float((127 + 14 + 127) << 23), ALU.mult, ALU.add))
            link2(dve.tensor_scalar(sm(FINV).bitcast(INT), sm(BEXP).bitcast(INT), 1.0, float(-(14 << 23)), ALU.mult, ALU.add))
            link2(dve.memset(relbd, 0.0))
            for h in range(HC):
                link2(dve.tensor_copy(relbd[h * DH:(h + 1) * DH, h, :], ws[h * DH:(h + 1) * DH, 0:REL]))
            for w in range(2):
                nin = KF if w == 0 else KD
                dve.wait_ge(s["w_loaded"], 16 * (w + 1))
                dve.tensor_reduce(sm(WSUM, 16), wraw.rearrange("p (a b) -> p a b", a=16), AX.X, ALU.add, apply_absolute_value=True).then_inc(s["ternary_step"], 1)
                dve.wait_ge(s["sum_ps"], w + 1)
                dve.tensor_reduce(sm(WSCALE), wr[:, 0:16], AX.X, ALU.add).then_inc(s["ternary_step"], 1)
                dve.wait_ge(s["ternary_step"], 5 * w + 2)
                link2(dve.tensor_scalar(sm(WTHR), sm(WSCALE), 1.0 / (F * D), 1e-8, ALU.mult, ALU.max))
                link2(dve.tensor_scalar(sm(WNTHR), sm(WTHR), -0.5, None, ALU.mult))
                dve.tensor_scalar(sm(WTHR), sm(WTHR), 0.5, None, ALU.mult).then_inc(s["ternary_step"], 1)
                dve.wait_ge(s["ternary_step"], 5 * w + 3)
                if w == 1:
                    dve.wait_ge(s["turned_w_ps"], GW)
                dve.tensor_scalar(wneg, wraw, sm(WNTHR), None, ALU.is_lt).then_inc(s["ternary_step"], 1)
                dve.wait_ge(s["ternary_step"], 5 * w + 4)
                dve.scalar_tensor_tensor(out=wter, in0=wraw, scalar=sm(WTHR), in1=wneg, op0=ALU.is_gt, op1=ALU.subtract).then_inc(s["ternary_step"], 1)
                tb = [ws, ww]
                nin, nout = (KF, KD) if w == 0 else (KD, KF)
                i = 0
                for o in range(nout):
                    for c8 in range(0, nin, 8 if nin > 4 else 4):
                        n8 = min(8, nin)
                        dve.wait_ge(s["turned_w_ps"], GW * w + i + 1)
                        dst = w1T[:, o, c8 * P:(c8 + n8) * P] if w == 0 else w2T[:, o, :]
                        dve.tensor_copy(dst, tb[i % 2][:, 0:n8 * P // 2].bitcast(F16)).then_inc(s["turned_w"], 1)
                        i += 1
            dve.wait_ge(s["turned_w"], GW + KF)
            dve.memset(kbd, 0.0).then_inc(s["zeros_done"], 1)
            dve.memset(vbd, 0.0).then_inc(s["zeros_done"], 1)

            def c2(t):
                at_least(dve, s["v_ps"], t)
                for c in range(KC):
                    src = cT[:, c, t * P:(t + 1) * P] if isinstance(t, int) else cT[:, c, bass.ds(t * P, P)]
                    dve.tensor_scalar(c2T[:, c, :], src, col("xattn_ln2_g", c), col("xattn_ln2_b", c), ALU.mult, ALU.add).then_inc(s["c2_ready"], 1)

            def layer_norm(t, src, dst, stat, mvc, vec_, rsc, names):
                a, b, c_, d_, e_ = names
                dve.bn_stats(sm(stat, 6), src).then_inc(s[a], 1)
                wait_alone(dve, s[a], t + 1)
                dve.bn_aggr(sm(mvc, 2), sm(stat, 6)).then_inc(s[b], 1)
                dve.wait_ge(s[b], t + 1)
                dve.tensor_scalar(sm(vec_), sm(mvc + 1), EPS, None, ALU.add).then_inc(s[c_], 1)
                dve.wait_ge(s[d_], t + 1)
                dve.tensor_scalar(dst, src, sm(mvc), sm(rsc), ALU.subtract, ALU.mult).then_inc(s[e_], 1)

            def softmax_a(t):
                dve.wait_ge(s["s_ps"], t + 1)
                at_least(dve, s["rowexp_done"], t)
                dve.tensor_scalar(ssb.rearrange("p a b -> p (a b)"), scores_ps[0][:, :], 1e5, -1e5, ALU.min, ALU.max).then_inc(s["clip_done"], 1)
                dve.wait_ge(s["clip_done"], t + 1)
                dve.wait_ge(s["r_loaded"], 32 * (t + 1))
                dve.tensor_tensor(ssb, ssb, rsk, ALU.add).then_inc(s["radd_done"], 1)
                dve.wait_ge(s["radd_done"], t + 1)
                dve.tensor_reduce(rows16[:, 0, :], ssb, AX.X, ALU.max).then_inc(s["rowmax_done"], 1)
                dve.wait_ge(s["rowmax_done"], t + 1)
                dve.tensor_tensor(ssb, ssb, rows16[:, 0, :].unsqueeze(2).to_broadcast([P, H, L]), ALU.subtract).then_inc(s["rowsub_done"], 1)

            def softmax_b(t):
                dve.wait_ge(s["rowexp_done"], t + 1)
                dve.tensor_reduce(rows16[:, 1, :], psb, AX.X, ALU.add).then_inc(s["rowsum_done"], 1)
                dve.wait_ge(s["rowsum_done"], t + 1)
                def lk(ins, i):
                    ins.then_inc(s["s_step"], 1)
                    dve.wait_ge(s["s_step"], 5 * t + i)
                lk(dve.reciprocal(rows16[:, 2, :], rows16[:, 1, :]), 1)
                lk(dve.tensor_tensor(rows16[:, 3, :], rows16[:, 1, :], rows16[:, 2, :], ALU.mult), 2)
                lk(dve.tensor_scalar(rows16[:, 3, :], rows16[:, 3, :], 1e-8, None, ALU.add), 3)
                lk(dve.reciprocal(rows16[:, 4, :], rows16[:, 3, :]), 4)
                lk(dve.tensor_tensor(rows16[:, 4, :], rows16[:, 4, :], rows16[:, 2, :], ALU.mult), 5)
                dve.tensor_tensor(psb, psb, rows16[:, 4, :].unsqueeze(2).to_broadcast([P, H, L]), ALU.mult).then_inc(s["pn_done"], 1)

            def x1(t):
                dve.wait_ge(s["o_ps"], t + 1)
                dve.tensor_tensor(xc, tile(t), ws[:, :], ALU.add).then_inc(s["o_taken"], 1)
                dve.wait_ge(s["o_taken"], t + 1)
                dve.tensor_tensor(tile(t), xc, abo, ALU.add).then_inc(s["x1_step"], 1)
                layer_norm(t, xc, yn, STAT1, MV1, VE1, RS1, ("st1", "ag1", "va1", "rs1", "y_ready"))

            def x2(t):
                dve.wait_ge(s["x1_step"], t + 1)
                dve.wait_ge(s["ao_ps"], t + 1)
                at_least(dve, s["xb2_ready"], t)
                dve.tensor_tensor(zc, tile(t), ws[:, :], ALU.add).then_inc(s["ao_taken"], 1)
                dve.wait_ge(s["ao_taken"], t + 1)
                layer_norm(t, zc, zn, STAT2, MV2, VE2, RS2, ("st2", "ag2", "va2", "rs2", "z_ready"))

            def gelu_parts(t, half):
                sl = slice(KF // 2 * half, KF // 2 * (half + 1))
                dve.wait_ge(s["gelu_done"], KF * t + KF // 2 * (half + 1))
                if half == 0:
                    at_least(dve, s["out_ps"], t)
                dve.tensor_scalar(gh[:, sl, :], gf[:, sl, :], sm(FS), None, ALU.mult).then_inc(s["gh_ready"], 1)
                dve.wait_ge(s["gh_ready"], 2 * t + half + 1)
                dve.scalar_tensor_tensor(out=gl[:, sl, :], in0=gf[:, sl, :], scalar=sm(FS), in1=gh[:, sl, :], op0=ALU.mult,
                                         op1=ALU.subtract).then_inc(s["gl_ready%d" % half], 1)

            def ctx_out(t):
                dve.wait_ge(s["ctx_ps"], 2 * (t + 1))
                pv = scores_ps[0][:, :].rearrange("p (hc two r) -> p two hc r", two=2, r=P)
                for v in range(2):
                    for b2 in range(2):
                        dve.tensor_copy(ctxT[v * L:(v + 1) * L, :, b2 * L:(b2 + 1) * L],
                                        pv[b2 * L:(b2 + 1) * L, v, :, b2 * L:(b2 + 1) * L]).then_inc(s["ctx_taken"], 1)

            def v_out(t):
                dve.wait_ge(s["v2_ps"], t + 1)
                for v in range(2):
                    dve.tensor_tensor(vbd[v * L:(v + 1) * L, :, :, v, :], wr[v * L:(v + 1) * L, :].rearrange("p (b hp d) -> p hp b d", b=2, d=DH),
                                      abv[v * L:(v + 1) * L, :].rearrange("p (hp d) -> p hp d", d=DH).unsqueeze(2).to_broadcast([L, HP, 2, DH]),
                                      ALU.add).then_inc(s["v2_taken"], 1)

            def z_low(t):
                dve.wait_ge(s["zh_taken"], t + 1)
                dve.tensor_tensor(zl.rearrange("p a b -> p (a b)"), ww[:, :], zh.rearrange("p a b -> p (a b)"), ALU.subtract).then_inc(s["zT_taken"], 1)

            def result(t):
                dve.wait_ge(s["out_ps"], t + 1)
                dve.wait_ge(s["xb2_ready"], t + 1)
                at_least(dve, s["stored"], 16 * t)
                dve.scalar_tensor_tensor(out=ot, in0=u_ps[:, :], scalar=sm(FINV), in1=xb2, op0=ALU.mult, op1=ALU.add).then_inc(s["out_ready"], 1)

            def dense(t, c1, c2_, c3):
                if c1:
                    c2(t)
                if c2_:
                    softmax_a(t - 1)
                if c3:
                    gelu_parts(t - 2, 0)
                if c1:
                    x1(t)
                if c2_:
                    softmax_b(t - 1)
                if c3:
                    gelu_parts(t - 2, 1)
                if c2_:
                    ctx_out(t - 1)
                    x2(t - 1)
                if c1:
                    v_out(t)
                if c3:
                    result(t - 2)
                if c2_:
                    z_low(t - 1)
            dve.wait_ge(s["xb_ready"], NT)
            run_dense(dve, dense)


def kernel(**inputs):
    import numpy as _np
    import concourse.bacc as _bacc
    from concourse import mybir as _mybir
    from concourse.bass_utils import run_bass_kernel_spmd as _run

    nc = _bacc.Bacc("TRN2", target_bir_lowering=False, num_devices=1)
    arrays, args = {}, {}
    for name, a in inputs.items():
        a = _np.ascontiguousarray(a)
        arrays[f"in_{name}_dram"] = a
        args[name] = nc.dram_tensor(f"in_{name}_dram", a.shape, _mybir.dt.from_np(a.dtype), kind="ExternalInput").ap()
    out = nc.dram_tensor("out_dram", inputs["x"].shape, _mybir.dt.float32, kind="ExternalOutput").ap()
    build_program(nc, args, out)
    return _run(nc, [arrays], core_ids=[0]).results[0]["out_dram"]
```

```python
from contextlib import ExitStack

import concourse.bass as bass
from concourse import mybir

F32 = mybir.dt.float32
F16 = mybir.dt.float16
BF16 = mybir.dt.bfloat16
ALU = mybir.AluOpType
ACT = mybir.ActivationFunctionType
AX = mybir.AxisListType

P = 128


def build_program(nc, A, out, dump=None):
    B, L, D = A["x"].shape
    _, S, DC = A["ctx_768"].shape
    E = A["L0_xattn_Wq"].shape[1]
    ROWS = B * L
    NT = ROWS // P
    KD, KC, KE = D // P, DC // P, E // P
    FT = S // P
    TAIL = S - FT * P
    NJ = FT + 1
    GROUPS = [range(0, 4), range(4, 9), range(9, NJ)]
    NG = len(GROUPS)
    GROUP_OF = {j: g for g, js in enumerate(GROUPS) for j in js}
    BANKT = 512 // L
    SCALE = float(E) ** -0.5
    EPS = 1e-5

    ctx = ExitStack()
    with ctx:
        def sb(name, shape, dt=F32, stack=ctx):
            return stack.enter_context(nc.sbuf_tensor(name, shape, dt))

        def sem(name):
            return ctx.enter_context(nc.semaphore(name))

        bank = [ctx.enter_context(nc.psum_tensor(f"bank{i}", [P, 512], F32)) for i in range(2)]
        scores_ps = [ctx.enter_context(nc.psum_tensor(f"scores_ps{i}", [P, 1024], F32)) for i in range(2)]
        u_ps = ctx.enter_context(nc.psum_tensor("u_ps", [P, 512], F32))
        max_ps = ctx.enter_context(nc.psum_tensor("max_ps", [P, 512], F32))

        ones_f = sb("ones_f", [P, P])
        ident_f = sb("ident_f", [P, P])
        ident_h = sb("ident_h", [P, P], F16)
        ones_h = sb("ones_h", [P, P], F16)
        
        minus_half = sb("minus_half", [P, 16])
        x_sb = sb("x_sb", [P, NT, D])
        VEC = {}
        rows = 0
        for key, n in (("xattn_ln1_g", KD), ("xattn_ln1_b", KD), ("xattn_bq", KE), ("xattn_bk", KE),
                       ("xattn_ln2_g", KC), ("xattn_ln2_b", KC), ("xattn_bv", KE), ("attn_bq", KD),
                       ("attn_bk", KD), ("ffn_b1", A["L0_ffn_b1"].shape[0] // P)):
            VEC[key] = (rows, n)
            rows += n
        NVEC = rows
        vec = sb("vec", [P, NVEC])
        vec_s = sb("vec_s", [P, NVEC])

        def cols(key, c):
            return vec_s[:, VEC[key][0] + c:VEC[key][0] + c + 1]

        def col(key, c):
            return vec[:, VEC[key][0] + c:VEC[key][0] + c + 1]

        yT_all = sb("yT_all", [P, KD, ROWS])
        cT = yT_all[:, 0:KC, :]
        sel_b = sb("sel_b", [P, P], BF16)
        t_vec = sb("t_vec", [P, KE])
        u_const = sb("u_const", [P, KC])
        c_const = sb("c_const", [P, 1])
        sv_vec = sb("sv_vec", [P, KE])
        AREA = 173 * 1024 + 288
        area = sb("area", [P, AREA // 4])

        def carve(at, shape, dt=F32):
            size = 1
            for n in shape[1:]:
                size *= n
            size *= mybir.dt.size(dt)
            assert at % 4 == 0 and at + size <= AREA, (at, size)
            v = area[0:shape[0], at // 4:(at + size + 3) // 4]
            v = v if dt == F32 else v.bitcast(dt)
            if len(shape) > 2:
                letters = "abcde"[:len(shape) - 1]
                v = v.rearrange(f"p ({' '.join(letters)}) -> p {' '.join(letters)}", **{l: n for l, n in zip(letters[1:], shape[2:])})
            return v, at + (size + 3) // 4 * 4

        at = 0
        wq, at = carve(at, [P, KD, E])
        wk, at = carve(at, [P, KC, E])
        wqT, at = carve(at, [P, KE, D])
        wkT, at = carve(at, [P, KE, DC + 1])
        wqk, at = carve(at, [P, KD, DC + 1])
        xwo, _ = carve(0, [P, KE, D])
        xwv, _ = carve(KD * E * 4, [P, KC, E])
        wvT, _ = carve((KD + KC) * E * 4, [P, KE, DC])
        DENSE_KEPT = at
        vec_rows, _ = carve(at, [NVEC, P])
        xwvo, at = carve(at, [P, KC, D])
        ln_st, ln_at = carve(at, [P, NT, 6])
        ln_mv, ln_at = carve(ln_at, [P, NT, 2])
        ln_ve, ln_at = carve(ln_at, [P, NT])
        ln_r, ln_at = carve(ln_at, [P, NT])
        abv, _ = carve(at, [P, D])
        xvo_bias, at = carve(at, [P, D])
        a_f, _ = carve(at, [P, KC + 1, 512])
        F = A["L0_ffn_b1"].shape[0]
        KF = F // P
        H = D // A["L0_attn_rel_emb"].shape[1]
        DH = D // H
        HC = P // DH
        HP = H // 2
        REL = 2 * L
        MAXP = (A["L0_attn_rel_emb"].shape[0] + 1) // 2
        rows16, _ = carve(at, [P, 5, H])
        rel_rows, at = carve(at, [REL, HC, DH])
        relbd, at = carve(at, [P, HC, REL])
        xbo, at = carve(at, [P, D])
        abo, at = carve(at, [P, D])
        fb2, at = carve(at, [P, D])
        small, at = carve(at, [P, 64])
        DENSE_BIG = at
        WPIECE = 4 * F // 4
        wsum_raw, _ = carve(0, [P, 4, WPIECE])

        def pair(shape, dt=F32):
            nonlocal at
            v0, at = carve(at, shape, dt)
            v1, at = carve(at, shape, dt)
            return [v0, v1]

        NPART = 3
        a_all, at = carve(at, [P, B, NPART * KC + 1, L], BF16)
        raw = pair([P, NJ, DC])
        y, _ = carve(at - NJ * DC * 4, [P, NT, D])
        xh, xl = [None, None], [None, None]
        for i in range(2):
            xh[i], at = carve(at, [P, NJ, DC], F16)
            xl[i], at = carve(at, [P, NJ, DC], F16)
        xT = pair([P, 2, KC, P], F16)
        st = pair([P, NJ, 6])
        mv = pair([P, NJ, 2])
        ve = pair([P, NJ])
        rs = pair([P, NJ])
        nb = pair([P, NJ])
        acur = pair([P, NPART * KC + 1, L], BF16)
        pf = pair([P, NJ, L])
        ph = pair([P, NJ, L], F16)
        pl = pair([P, NJ, L], F16)
        mxa, at = carve(at, [P, L])
        mxb, at = carve(at, [P, L])
        mx, at = carve(at, [P, P])
        mq, at = carve(at, [L, 1])
        mbc, at = carve(at, [P, L])
        rz, at = carve(at, [P, L])


        at = 0
        awq, at = carve(at, [P, KD, D])
        awk, at = carve(at, [P, KD, D])
        awv, at = carve(at, [P, KD, D])
        awo, at = carve(at, [P, KD, D])
        assert at <= DENSE_KEPT
        at = DENSE_BIG
        w1T, at = carve(at, [P, KD, F], F16)
        w2T, at = carve(at, [P, KF, D], F16)
        c2T, at = carve(at, [P, KC, P])
        yn, at = carve(at, [P, D])
        yT, at = carve(at, [P, KD, P])
        q2T, at = carve(at, [P, KD, P])
        kbd, at = carve(at, [P, KD, 2, HC, L])
        vbd, at = carve(at, [P, HP, 2, 2, DH])
        anti_f, _ = carve(at, [P, P])
        gs, at = carve(at, [P, H, REL])
        rsk, at = carve(at, [P, H, L])
        early_wraw = [carve(at + i * WPIECE * 4, [P, WPIECE])[0] for i in range(2)]
        ssb, at = carve(at, [P, H, L])
        psb, at = carve(at, [P, H, L])
        ptT, at = carve(at, [P, HP, P])
        ctxT, at = carve(at, [P, KD, P])
        zn, at = carve(at, [P, D])
        zh, at = carve(at, [P, KD, P], F16)
        zl, at = carve(at, [P, KD, P], F16)
        wneg, _ = carve(at, [P, WPIECE], F16)
        wter = [carve(at + (i + 1) * WPIECE * 2, [P, WPIECE], F16)[0] for i in range(3)]
        gf, at = carve(at, [P, KF, P])
        gh, at = carve(at, [P, KF, P], F16)
        gl, at = carve(at, [P, KF, P], F16)
        xb2, at = carve(at, [P, D])
        ot, at = carve(at, [P, D])
        xc, at = carve(at, [P, D])
        zc, at = carve(at, [P, D])
        wraw = [None, None]
        for i in range(2):
            wraw[i], at = carve(at, [P, WPIECE])
        wraw += early_wraw
        def sm(a, n=1):
            return small[:, a:a + n]
        STAT1, MV1, VE1, RS1, STAT2, MV2, VE2, RS2 = 0, 6, 8, 9, 10, 16, 18, 19
        WSUM, WSCALE, WTHR, WNTHR, BMAX, FS, FINV, BEXP = 20, 28, 30, 32, 39, 40, 41, 42
        ksc = sm(48, KD)
        skew = nc.dram_tensor("skew", (P, H * REL), F32, kind="Internal").ap()
        ws, wr, ww = bank[0], bank[1], max_ps
        gbank = [scores_ps[1][:, 0:512], scores_ps[1][:, 512:1024]]

        names = """consts_ready ident_ready vec_loaded vec_T vec_ready wq_loaded wk_loaded
            ln_stat ln_aggr ln_var ln_rstd ln_done xT_ready yT_out prep_ps prep_out uc_ready a_fp32 a_part
            xvo_loaded wo_ps wo_out sel_ready raw_tail_zero bn_done aggr_done var_ready negmu_ready rstd_ready nb_ready xn_done hi_ready lo_ready
            tp_ready evac_done score_done max_a max_b max_tail max_all maxT_ready maxq_ready maxbc_ready maxbc_copied
            sub_done exp_done ph_ready pl_ready pv_done rz_ready c_ready out_stored
            dense_loaded rows_loaded abv_loaded zeros_done rel_ps rel_step ab_step wsum_done wthr_ready neg_done ter_done turned_w_ps turned_w
            small_done
            c2_ready o_ps o_taken yT_ps yT_taken q2_ps q2_taken k2_ps k2_taken v2_ps v2_taken
            g_ps g_taken g_stored r_loaded s_ps s_step clip_done radd_done rowmax_done rowsub_done rowexp_done rowsum_done
            inv_step pn_done pt_ps pt_taken ctx_ps ctx_taken ao_ps ao_taken zT_ps zh_taken zT_taken f_ps gelu_done
            gh_ready gl_ready0 gl_ready1 out_ps out_ready x1_step st1 ag1 va1 rs1 y_ready st2 ag2 va2 rs2 z_ready xb_ready
            xb2_ready stored ab2_step""".split()
        s = {n: sem(n) for n in names}
        raw_loaded = [[sem(f"raw_loaded{u}{g}") for g in range(NG)] for u in range(2)]
        x_loaded = [sem(f"x_loaded{h}") for h in range(2)]
        wsum_loaded = [sem(f"wsum_loaded{i}") for i in range(4)]
        wraw_loaded = [sem(f"wraw_loaded{i}") for i in range(4)]
        acur_loaded = [sem(f"acur_loaded{u}") for u in range(2)]

        ctx_in = A["ctx_768"]
        NAF = NPART * (KC + 1)
        tb = [scores_ps[0][:, 0:512], scores_ps[0][:, 512:1024], scores_ps[1][:, 0:512], scores_ps[1][:, 512:1024]]
        xb3 = [bank[0], bank[1], max_ps]
        OUT_WKT = KE
        OUT_WQT = OUT_WKT + KE
        OUT_S = OUT_WQT + KE
        OUT_T = OUT_S + KE
        OUT_QK = OUT_T + KD
        OUT_UC = OUT_QK + 1
        OUT_C = OUT_UC + 1
        XVO_TURNED, XVO_ROW = KE, KE + KC + 1
        WO_OUT = KE
        XVO_EARLY = KE + 2
        EXTRA = {0: ("fold", 0, tb[2], ("a_fp32", KC + 1)),
                 2: ("fold", 1, tb[3], ("a_fp32", KC + 1)),
                 4: ("xvo", XVO_EARLY, u_ps, ("wo_out", WO_OUT + XVO_EARLY - 2)),
                 6: ("fold", 2, tb[2], ("a_fp32", NAF + 1)),
                 8: ("xvo", XVO_EARLY + 1, tb[3], ("a_fp32", NAF + 2)),
                 10: ("fold", 3, u_ps, ("wo_out", WO_OUT + XVO_EARLY)),
                 12: ("xvo", XVO_EARLY + 2, tb[2], ("a_fp32", NAF + 3))}
        FBANK = [wr, ww, wr, ww]
        TURN_AT = [{"k": [0], "relative": [1, 2], "values": [3]},
                   {"scores": [4], "xattn_o": [5], "y_turn": [6], "q": [7], "k": [8], "relative": [9], "att_turn": [10, 11],
                    "values": [12], "att_values": [13], "att_o": [14, 15]}]
        W_BUF = [0, 1, 2, 3, 0, 1, 0, 1]
        W_BEFORE = {4: 0, 5: 1, 6: 4, 7: 5}
        NW = 8

        def w_piece(i):
            if i < NW // 2:
                return A["L0_ffn_W1"].rearrange("(c p) e -> p c e", p=P)[:, 4 * i:4 * i + 4, :]
            return A["L0_ffn_W2"].rearrange("(c p) e -> p c e", p=P)[:, i - 4:i - 3, :]

        def before(k, u):
            return (k, 0) if u == 1 else (k - 1, 1)

        def after(k, u):
            return (k, 1) if u == 0 else (k + 1, 0)

        def turned(u, j):
            return bank[(u + j) % 2][:, 0:KC * P].bitcast(F16).rearrange("p (h c k) -> p h c k", h=2, c=KC)

        PV_AT = {j: (2, [j + 5]) for j in range(8)}
        PV_AT |= {9: (1, [0, 1]), 10: (1, [2]), 11: (1, [3]), 12: (1, [4])}

        def back(k, u, d):
            return (k, u) if d == 0 else back(*before(k, u), d - 1)

        def at_least(eng, semaphore, value):
            if not (isinstance(value, int) and value <= 0):
                eng.wait_ge(semaphore, value)

        def wait_alone(eng, semaphore, value):
            eng.wait_ge(s["ident_ready"], 1)
            eng.wait_ge(semaphore, value)

        out_rows = out.rearrange("b l d -> (b l) d")

        def rows(t):
            return slice(t * P, (t + 1) * P) if isinstance(t, int) else bass.ds(t * P, P)

        def tile(t):
            return x_sb[:, t, :] if isinstance(t, int) else x_sb[:, bass.ds(t, 1), :].squeeze(1)

        def run_dense(eng, step):
            step(0, True, False, False)
            step(1, True, True, False)
            step(2, True, True, True)
            with eng.Fori(3, NT - 1) as t:
                step(t, True, True, True)
            step(NT - 1, True, True, True)
            step(NT, False, True, True)
            step(NT + 1, False, False, True)

        block = ctx.enter_context(nc.Block())

        @block.sync
        def _(sp):
            sp.dma_start(wk[:, :, :], A["L0_xattn_Wk"].rearrange("(c p) e -> p c e", p=P)).then_inc(s["wk_loaded"], 16)
            sp.dma_start(wq[:, :, :], A["L0_xattn_Wq"].rearrange("(c p) e -> p c e", p=P)).then_inc(s["wq_loaded"], 16)
            for key, (r, n) in VEC.items():
                sp.dma_start(vec_rows[r:r + n, :], A["L0_" + key].rearrange("(c p) -> c p", p=P)).then_inc(s["vec_loaded"], 16)
            for t in range(NT):
                sp.dma_start(x_sb[:, t, :], A["x"].rearrange("b l d -> (b l) d")[t * P:(t + 1) * P, :]).then_inc(x_loaded[t // (NT // 2)], 16)

            def load_group(n, u, g):
                full = ctx_in[n, 0:FT * P, :] if isinstance(n, int) else ctx_in[bass.ds(n, 1), 0:FT * P, :].squeeze(0)
                full = full.rearrange("(p j) d -> p j d", j=FT)
                js = [j for j in GROUPS[g] if j < FT]
                sp.dma_start(raw[u][:, js[0]:js[-1] + 1, :], full[:, js[0]:js[-1] + 1, :]).then_inc(raw_loaded[u][g], 16)
                if g == NG - 1:
                    tail = ctx_in[n, FT * P:S, :] if isinstance(n, int) else ctx_in[bass.ds(n, 1), FT * P:S, :].squeeze(0)
                    sp.dma_start(raw[u][0:TAIL, FT, :], tail).then_inc(raw_loaded[u][g], 16)

            for g in range(NG):
                load_group(0, 0, g)
            sp.wait_ge(s["prep_ps"], 2 * KE + KD + 4)
            sp.dma_start(xwv, A["L0_xattn_Wv"].rearrange("(c p) e -> p c e", p=P)).then_inc(s["xvo_loaded"], 16)
            sp.dma_start(xwo, A["L0_xattn_Wo"].rearrange("(c p) e -> p c e", p=P)).then_inc(s["xvo_loaded"], 16)
            sp.wait_ge(s["xT_ready"], NT)
            for g in range(NG):
                load_group(1, 1, g)

            def load_a(n, u):
                sp.dma_start(acur[u][:, :, :], a_all[:, n, :, :] if isinstance(n, int) else
                             a_all[:, bass.ds(n, 1), :, :].squeeze(1)).then_inc(acur_loaded[u], 16)

            sp.wait_ge(s["a_part"], NAF)
            load_a(0, 0)
            load_a(1, 1)
            def load_next(k, u, between=None):
                for g in range(NG):
                    wait_alone(sp, s["lo_ready"], NJ * 2 * k + NJ * u + GROUPS[g][-1] + 1)
                    load_group(2 * k + 2 + u, u, g)
                    if between is not None:
                        between(g)
                wait_alone(sp, s["score_done"], NJ * 2 * k + NJ * (u + 1))
                load_a(2 * k + 2 + u, u)

            def load_for_sum(i):
                if i >= 4:
                    sp.wait_ge(s["wsum_done"], i - 3)
                src = w_piece(i)
                sp.dma_start(wsum_raw[:, i % 4, :].rearrange("p (c e) -> p c e", c=src.shape[1]), src).then_inc(wsum_loaded[i % 4], 16)

            load_next(0, 0)
            load_next(0, 1)
            sp.wait_ge(s["a_part"], 2 * NAF)
            sp.wait_ge(s["wo_ps"], XVO_ROW + 1)
            for i in range(4):
                load_for_sum(i)
            first_rel = MAXP - 1 - L
            for h in range(HC):
                sp.dma_start(rel_rows[:, h, :], A["L0_attn_rel_emb"][first_rel:first_rel + REL, :]).then_inc(s["rows_loaded"], 16)
            for dst, key in ((xbo, "xattn_bo"), (abo, "attn_bo"), (fb2, "ffn_b2")):
                sp.dma_start(dst, A["L0_" + key].partition_broadcast(P)).then_inc(s["rows_loaded"], 16)
            def more_for_sum(g):
                load_for_sum(4 + g)
                if g == NG - 1:
                    load_for_sum(NW - 1)

            load_next(1, 0, more_for_sum)
            load_next(1, 1)
            sp.wait_ge(s["wsum_done"], NW)
            for dst, key in ((awq, "attn_Wq"), (awk, "attn_Wk"), (awv, "attn_Wv"), (awo, "attn_Wo")):
                sp.dma_start(dst, A["L0_" + key].rearrange("(c p) e -> p c e", p=P)).then_inc(s["dense_loaded"], 16)
            with sp.Fori(2, B // 2 - 1) as k:
                load_next(k, 0)
                load_next(k, 1)

            sp.wait_ge(s["c_ready"], B)

            def load_w(i):
                if i in W_BEFORE:
                    sp.wait_ge(s["ter_done"], W_BEFORE[i] + 1)
                src = w_piece(i)
                sp.dma_start(wraw[W_BUF[i]].rearrange("p (c e) -> p c e", c=src.shape[1]), src).then_inc(wraw_loaded[W_BUF[i]], 16)

            for i in range(4):
                load_w(i)
            sp.wait_ge(s["xb_ready"], 1)
            sp.dma_start(abv, A["L0_attn_bv"].partition_broadcast(P)).then_inc(s["abv_loaded"], 16)
            for i in range(4, 6):
                load_w(i)

            def skew_store(t):
                at_least(sp, s["radd_done"], t)
                sp.wait_ge(s["g_taken"], KD * (t + 1))
                sp.dma_start(skew, gs.rearrange("p h r -> p (h r)")).then_inc(s["g_stored"], 16)

            def skew_load(t):
                sp.wait_ge(s["g_stored"], 16 * (t + 1))
                for v in range(2):
                    src = bass.AP(tensor=skew.tensor, offset=v * L * H * REL + L - 1, ap=[[H * REL - 1, L], [REL, H], [1, L]])
                    sp.dma_start(rsk[v * L:(v + 1) * L, :, :], src).then_inc(s["r_loaded"], 16)

            def store(t):
                wait_alone(sp, s["out_ready"], t + 1)
                sp.dma_start(out_rows[rows(t), :], ot).then_inc(s["stored"], 16)

            def dense(t, c1, c2, c3):
                if c1:
                    skew_store(t)
                    skew_load(t)
                if isinstance(t, int) and t == 0:
                    for i in range(6, NW):
                        load_w(i)
                if c3:
                    store(t - 2)
            run_dense(sp, dense)
            sp.wait_ge(s["stored"], 16 * NT)

        @block.gpsimd
        def _(pool):
            pool.memset(ones_f[:, :], 1.0).then_inc(s["consts_ready"], 1)
            pool.memset(minus_half[:, :], -0.5).then_inc(s["consts_ready"], 1)
            pool.wait_ge(s["consts_ready"], 2)
            pool.affine_select(out=ident_f[:, :], in_=ones_f[:, :], compare_op=ALU.is_equal, fill=0.0, base=0,
                               pattern=[[-1, P]], channel_multiplier=1).then_inc(s["ident_ready"], 1)
            pool.memset(sel_b[:, :], 0.0).then_inc(s["sel_ready"], 1)
            pool.wait_ge(s["sel_ready"], 1)
            for row in (0, 64, 96):
                pool.memset(sel_b[row:row + 1, :], 1.0).then_inc(s["sel_ready"], 1)
            pool.wait_ge(s["sel_ready"], 4)
            for i in range(4):
                sl = slice(NT // 2 * (i % 2), NT // 2 * (i % 2 + 1))
                pool.wait_ge(s["ln_var"], i + 1)
                pool.tensor_tensor(ln_r[:, sl], ln_ve[:, sl], minus_half[:, 0:NT // 2], ALU.pow).then_inc(s["ln_rstd"], 1)

            def rstd(k, u, g):
                n = 2 * k + u
                js = GROUPS[g]
                sl = slice(js[0], js[-1] + 1)
                pool.wait_ge(s["var_ready"], NG * n + g + 1)
                pool.tensor_tensor(rs[u][:, sl], ve[u][:, sl], minus_half[:, 0:len(js)], ALU.pow).then_inc(s["rstd_ready"], 1)
                pool.wait_ge(s["rstd_ready"], NG * n + g + 1)
                pool.tensor_tensor(nb[u][:, sl], nb[u][:, sl], rs[u][:, sl], ALU.mult).then_inc(s["nb_ready"], 1)

            def low_part(k, u, j):
                n = 2 * k + u
                m = P if j < FT else TAIL
                pool.wait_ge(s["hi_ready"], NJ * n + j + 1)
                pool.tensor_tensor(xl[u][0:m, j, :], raw[u][0:m, j, :], xh[u][0:m, j, :], ALU.subtract).then_inc(s["lo_ready"], 1)

            def p_low(k, u):
                n = 2 * k + u
                pool.wait_ge(s["ph_ready"], n + 1)
                pool.tensor_tensor(pl[u][:, :, :], pf[u][:, :, :], ph[u][:, :, :], ALU.subtract).then_inc(s["pl_ready"], 1)

            def step(k, u, first=False, last=False):
                for j in range(NJ):
                    low_part(k, u, j)
                    if j == 0:
                        rstd(k, u, 1)
                    if j == 4:
                        rstd(k, u, 2)
                    if j == 8 and not last:
                        rstd(*after(k, u), 0)
                    if j == 10 and not first:
                        p_low(*before(k, u))

            rstd(0, 0, 0)
            step(0, 0, first=True)
            step(0, 1)
            with pool.Fori(1, B // 2 - 1) as k:
                step(k, 0)
                step(k, 1)
            step(B // 2 - 1, 0)
            step(B // 2 - 1, 1, last=True)
            p_low(B // 2 - 1, 1)

            def pw(a, b, t, var, done):
                pool.wait_ge(s[var], t + 1)
                pool.tensor_tensor(sm(b), sm(a), minus_half[:, 0:1], ALU.pow).then_inc(s[done], 1)

            pool.wait_ge(s["c_ready"], B)
            pool.affine_select(out=anti_f[:, :], in_=ones_f[:, :], compare_op=ALU.is_equal, fill=0.0, base=-(P - 1),
                               pattern=[[1, P]], channel_multiplier=1).then_inc(s["rel_step"], 1)
            pool.wait_ge(s["rel_step"], 1)
            pool.wait_ge(s["rows_loaded"], 16 * (HC + 3))
            pool.tensor_tensor(xbo, xbo, xvo_bias, ALU.add).then_inc(s["xb_ready"], 1)
            pool.wait_ge(s["xb_ready"], 1)

            def with_bias(ts):
                for t in ts:
                    pool.tensor_tensor(x_sb[:, t, :], x_sb[:, t, :], xbo, ALU.add).then_inc(s["xb_ready"], 1)

            with_bias([0])
            pool.memset(kbd, 0.0).then_inc(s["zeros_done"], 1)
            pool.memset(vbd, 0.0).then_inc(s["zeros_done"], 1)

            def dense(t, c1, c2, c3):
                if c1:
                    pw(VE1, RS1, t, "va1", "rs1")
                if isinstance(t, int) and t == 0:
                    with_bias(range(1, NT))
                if c2:
                    pw(VE2, RS2, t - 1, "va2", "rs2")
                    pool.wait_ge(s["ao_taken"], t)
                    at_least(pool, s["out_ready"], t - 1)
                    pool.tensor_tensor(xb2, zc, fb2, ALU.add).then_inc(s["xb2_ready"], 1)
            run_dense(pool, dense)

        @block.scalar
        def _(act):
            act.wait_ge(s["ident_ready"], 1)
            act.copy(ident_h[:, :], ident_f[:, :]).then_inc(s["ident_ready"], 1)
            act.copy(ones_h[:, :], ones_f[:, :]).then_inc(s["ident_ready"], 1)
            act.wait_ge(s["vec_ready"], 2)
            for e in range(KE):
                act.wait_ge(s["prep_ps"], e + 1)
                act.copy(wkT[:, e, 0:DC], tb[e][:, 0:DC]).then_inc(s["prep_out"], 1)
            for e in range(KE):
                act.wait_ge(s["prep_ps"], KE + e + 1)
                act.copy(wqT[:, e, :], tb[e]).then_inc(s["prep_out"], 1)
            act.wait_ge(s["prep_ps"], 2 * KE + 2)
            for e in range(KE):
                act.activation(wkT[:, e, DC:DC + 1], u_ps[:, e:e + 1], ACT.Identity, bias=col("xattn_bk", e), scale=1.0).then_inc(s["prep_out"], 1)
            act.wait_ge(s["prep_ps"], 2 * KE + 2)
            for e in range(KE):
                act.activation(t_vec[:, e:e + 1], u_ps[:, KE + e:KE + e + 1], ACT.Identity, bias=col("xattn_bq", e), scale=1.0).then_inc(s["prep_out"], 1)
            for c in range(KD):
                act.wait_ge(s["prep_ps"], 2 * KE + 3 + c)
                act.activation(wqk[:, c, :], tb[c][:, 0:DC + 1], ACT.Identity, bias=0.0, scale=col("xattn_ln1_g", c)).then_inc(s["prep_out"], 1)
            act.wait_ge(s["prep_ps"], 2 * KE + KD + 4)
            act.copy(u_const[:, :], u_ps[:, 8:8 + KC]).then_inc(s["prep_out"], 1)
            act.copy(c_const[:, :], u_ps[:, 16:17]).then_inc(s["prep_out"], 1)

            def rows_out(h):
                for t in range(NT // 2 * h, NT // 2 * (h + 1)):
                    act.wait_ge(s["xT_ready"], t + 1)
                    act.copy(yT_all[:, :, t * P:(t + 1) * P], xb3[t % 3][:, :].rearrange("p (c r) -> p c r", c=KD)).then_inc(s["yT_out"], 1)

            def parts_out(h, part, cs=range(KC + 1)):
                HB = 512 // L
                for c in cs:
                    act.wait_ge(s["a_fp32"], NAF * h + (KC + 1) * part + c + 1)
                    if c < KC:
                        dst = a_all[:, h * HB:(h + 1) * HB, KC * part + c, :]
                        act.copy(dst, a_f[:, c, :].rearrange("p (b l) -> p b l", l=L)).then_inc(s["a_part"], 1)
                    else:
                        r = slice((0, 64, 96)[part], P)
                        act.copy(a_all[r, h * HB:(h + 1) * HB, NPART * KC, :],
                                 a_f[r, c, :].rearrange("p (b l) -> p b l", l=L)).then_inc(s["a_part"], 1)

            def xvo_out(i, src):
                act.wait_ge(s["wo_ps"], i + 1)
                if i == 0:
                    for e in range(KE):
                        act.activation(sv_vec[:, e:e + 1], src[:, e:e + 1], ACT.Identity, bias=col("xattn_bv", e), scale=1.0).then_inc(s["wo_out"], 1)
                elif i <= XVO_TURNED:
                    act.copy(wvT[:, i - 1, :], src[:, 0:DC]).then_inc(s["wo_out"], 1)
                elif i < XVO_ROW:
                    m = i - XVO_TURNED - 1
                    act.activation(xwvo[:, m, :], src[:, :], ACT.Identity, bias=0.0, scale=col("xattn_ln2_g", m)).then_inc(s["wo_out"], 1)
                else:
                    act.copy(xvo_bias, src[:, :]).then_inc(s["wo_out"], 1)

            rows_out(0)
            rows_out(1)
            parts_out(0, 0)
            xvo_out(0, u_ps)
            parts_out(0, 1)
            for i in range(1, 5):
                xvo_out(i, (u_ps, max_ps)[i % 2])
            parts_out(0, 2)

            def norm(k, u, j):
                n = 2 * k + u
                m = P if j < FT else TAIL
                act.wait_ge(s["nb_ready"], NG * n + GROUP_OF[j] + 1)
                act.activation(raw[u][0:m, j, :], raw[u][0:m, j, :], ACT.Identity, bias=nb[u][0:m, j:j + 1],
                               scale=rs[u][0:m, j:j + 1]).then_inc(s["xn_done"], 1)

            def high_part(k, u, j):
                n = 2 * k + u
                m = P if j < FT else TAIL
                act.wait_ge(s["xn_done"], NJ * n + j + 1)
                at_least(act, s["pv_done"], NJ * (n - 2) + j + 1 if not isinstance(n, int) or n >= 2 else 0)
                act.copy(xh[u][0:m, j, :], raw[u][0:m, j, :]).then_inc(s["hi_ready"], 1)

            def exps(k, u):
                n = 2 * k + u
                act.wait_ge(s["sub_done"], n + 1)
                act.activation(pf[u][:, :, :], pf[u][:, :, :], ACT.Exp, bias=0.0, scale=1.0).then_inc(s["exp_done"], 1)

            def p_high(k, u):
                n = 2 * k + u
                act.wait_ge(s["exp_done"], n + 1)
                act.copy(ph[u][:, :, :], pf[u][:, :, :]).then_inc(s["ph_ready"], 1)

            def magnitudes(i):
                act.wait_ge(wsum_loaded[i % 4], 16 * (i // 4 + 1))
                act.activation(wsum_raw[:, i % 4, :], wsum_raw[:, i % 4, :], ACT.Abs, bias=0.0, scale=1.0,
                               accum_out=sm(WSUM + i)).then_inc(s["wsum_done"], 1)

            def step(k, u, first=False, extra=None):
                for j in range(NJ):
                    norm(k, u, j)
                    if extra in (2, 3) and j in (3, 6, 9, 12):
                        magnitudes(NW // 2 * (extra - 2) + j // 3 - 1)
                    if extra == 0:
                        if j == 2:
                            xvo_out(5, max_ps)
                        if j in (7, 11):
                            xvo_out(*EXTRA[j - 3][1:3])
                    if extra == 1:
                        if j == 2:
                            xvo_out(*EXTRA[NJ - 1][1:3])
                        if j < NAF:
                            parts_out(1, j // (KC + 1), [j % (KC + 1)])
                    if j >= 1:
                        high_part(k, u, j - 1)
                    if j == 9 and not first:
                        exps(*before(k, u))
                    if j == 10 and not first:
                        p_high(*before(k, u))
                high_part(k, u, NJ - 1)

            step(0, 0, first=True, extra=0)
            step(0, 1, extra=1)
            step(1, 0, extra=2)
            step(1, 1, extra=3)
            with act.Fori(2, B // 2 - 1) as k:
                step(k, 0)
                step(k, 1)
            step(B // 2 - 1, 0)
            step(B // 2 - 1, 1)
            exps(B // 2 - 1, 1)
            p_high(B // 2 - 1, 1)

            def gelus(t, f4s):
                for f4 in f4s:
                    act.wait_ge(s["f_ps"], 4 * t + f4 + 1)
                    if f4 % 2 == 0:
                        at_least(act, s["gl_ready%d" % (f4 // 2)], t)
                    for f in range(4):
                        act.activation(gf[:, 4 * f4 + f, :], FBANK[f4][:, f * P:(f + 1) * P], ACT.Gelu, bias=col("ffn_b1", 4 * f4 + f),
                                       scale=1.0).then_inc(s["gelu_done"], 1)

            def row_exp(t):
                act.wait_ge(s["rowsub_done"], t + 1)
                act.activation(psb, ssb, ACT.Exp, bias=0.0, scale=1.0).then_inc(s["rowexp_done"], 1)

            def pt_out(t):
                for i in range(2):
                    act.wait_ge(s["pt_ps"], 2 * t + i + 1)
                    at_least(act, s["ctx_ps"], 2 * t)
                    act.copy(ptT[:, 4 * i:4 * i + 4, :].rearrange("p a b -> p (a b)"), gbank[i]).then_inc(s["pt_taken"], 1)

            def yT_out(t):
                act.wait_ge(s["yT_ps"], t + 1)
                at_least(act, s["v2_ps"], t)
                act.copy(yT.rearrange("p a b -> p (a b)"), ws[:, :]).then_inc(s["yT_taken"], 1)

            def q_out(t):
                act.wait_ge(s["q2_ps"], t + 1)
                for m in range(KD):
                    act.activation(q2T[:, m, :], wr[:, m * P:(m + 1) * P], ACT.Identity, bias=col("attn_bq", m), scale=1.0).then_inc(s["q2_taken"], 1)

            def k_out(t):
                if isinstance(t, int) and t == 0:
                    act.wait_ge(s["zeros_done"], 2)
                    act.wait_ge(s["small_done"], 1)
                act.wait_ge(s["k2_ps"], t + 1)
                for m in range(KD):
                    for h in range(HC):
                        act.activation(kbd[h * DH:(h + 1) * DH, m, :, h, :],
                                       ww[h * DH:(h + 1) * DH, m * P:(m + 1) * P].rearrange("p (b j) -> p b j", b=2), ACT.Identity,
                                       bias=ksc[h * DH:(h + 1) * DH, m:m + 1], scale=DH ** -0.5).then_inc(s["k2_taken"], 1)

            def g_out(t, cs):
                for c in cs:
                    act.wait_ge(s["g_ps"], KD * t + c + 1)
                    if c == cs[0]:
                        at_least(act, s["g_stored"], 16 * t)
                    act.copy(gs[:, HC * c:HC * (c + 1), :].rearrange("p a b -> p (a b)"), gbank[c % 2]).then_inc(s["g_taken"], 1)

            def z_out(t):
                act.wait_ge(s["zT_ps"], t + 1)
                at_least(act, s["f_ps"], 4 * t)
                act.copy(zh.rearrange("p a b -> p (a b)"), ww[:, :]).then_inc(s["zh_taken"], 1)

            def turned_out(t, place):
                if not isinstance(t, int) or t > 1:
                    return
                for g in TURN_AT[t].get(place, []):
                    act.wait_ge(s["turned_w_ps"], g + 1)
                    i, half = g // 2, g % 2
                    src = u_ps[:, :].bitcast(F16)
                    if i < NW // 2:
                        act.copy(w1T[:, 2 * half:2 * half + 2, 4 * i * P:4 * (i + 1) * P], src.rearrange("p (o f) -> p o f", o=2)).then_inc(s["turned_w"], 1)
                    else:
                        act.copy(w2T[:, 8 * half:8 * half + 8, (i - 4) * P:(i - 3) * P], src.rearrange("p (f o) -> p f o", f=8)).then_inc(s["turned_w"], 1)

            def dense(t, c1, c2, c3):
                turned_out(t, "scores")
                turned_out(t, "xattn_o")
                if c3:
                    z_out(t - 2)
                    gelus(t - 2, range(3))
                if c1:
                    yT_out(t)
                turned_out(t, "y_turn")
                if c3:
                    gelus(t - 2, [3])
                if c2:
                    row_exp(t - 1)
                if c1:
                    q_out(t)
                    turned_out(t, "q")
                    k_out(t)
                    turned_out(t, "k")
                    g_out(t, range(KD))
                turned_out(t, "relative")
                if c2:
                    pt_out(t - 1)
                for place in ("att_turn", "values", "att_values", "att_o"):
                    turned_out(t, place)
            run_dense(act, dense)

        @block.tensor
        def _(pe):
            pe.wait_ge(s["ident_ready"], 3)
            pe.wait_ge(s["vec_loaded"], 16 * len(VEC))
            pe.transpose(max_ps[:, 0:NVEC], vec_rows[:, :], ident_f[0:NVEC, 0:NVEC]).then_inc(s["vec_T"], 1)
            pe.wait_ge(s["wk_loaded"], 16)
            for e in range(KE):
                for c in range(KC):
                    ins = pe.transpose(tb[e][:, c * P:(c + 1) * P], wk[:, c, e * P:(e + 1) * P], ident_f[:, :])
                ins.then_inc(s["prep_ps"], 1)
            pe.wait_ge(s["wq_loaded"], 16)
            for e in range(KE):
                pe.wait_ge(s["prep_out"], e + 1)
                for c in range(KD):
                    ins = pe.transpose(tb[e][:, c * P:(c + 1) * P], wq[:, c, e * P:(e + 1) * P], ident_f[:, :])
                ins.then_inc(s["prep_ps"], 1)
            pe.wait_ge(s["vec_ready"], 2)
            for n, (w, vec_key, kk) in enumerate(((wk, "xattn_ln2_b", KC), (wq, "xattn_ln1_b", KD))):
                for e in range(KE):
                    for c in range(kk):
                        ins = pe.matmul(u_ps[:, KE * n + e:KE * n + e + 1], w[:, c, e * P:(e + 1) * P], col(vec_key, c),
                                        start=(c == 0), stop=(c == kk - 1))
                ins.then_inc(s["prep_ps"], 1)
            pe.wait_ge(s["prep_out"], OUT_S)
            for c in range(KD):
                for e in range(KE):
                    ins = pe.matmul(tb[c][:, 0:DC + 1], wqT[:, e, c * P:(c + 1) * P], wkT[:, e, :], start=(e == 0), stop=(e == KE - 1))
                ins.then_inc(s["prep_ps"], 1)
            pe.wait_ge(s["prep_out"], OUT_T)
            for m in range(KC):
                for e in range(KE):
                    ins = pe.matmul(u_ps[:, 8 + m:9 + m], wkT[:, e, m * P:(m + 1) * P], t_vec[:, e:e + 1], start=(e == 0), stop=(e == KE - 1))
            ins.then_inc(s["prep_ps"], 1)
            for e in range(KE):
                ins = pe.matmul(u_ps[:, 16:17], t_vec[:, e:e + 1].to_broadcast([P, P]), wkT[:, e, DC:DC + 1], start=(e == 0), stop=(e == KE - 1))
            ins.then_inc(s["prep_ps"], 1)

            def turn_rows(h):
                for t in range(NT // 2 * h, NT // 2 * (h + 1)):
                    pe.wait_ge(s["ln_done"], NT + t + 1)
                    at_least(pe, s["yT_out"], t - 2)
                    for c in range(KD):
                        ins = pe.transpose(xb3[t % 3][:, c * P:(c + 1) * P], y[:, t, c * P:(c + 1) * P], ident_f[:, :])
                    ins.then_inc(s["xT_ready"], 1)

            def fold(h, m, dst):
                if m == 0:
                    pe.wait_ge(s["yT_out"], NT // 2 * (h + 1))
                    pe.wait_ge(s["prep_out"], OUT_C)
                for c in range(KD):
                    w = wqk[:, c, m * P:(m + 1) * P] if m < KC else wqk[:, c, DC:DC + 1].to_broadcast([P, P])
                    ins = pe.matmul(dst[:, :], w, yT_all[:, c, h * 512:(h + 1) * 512], start=(c == 0), stop=(c == KD - 1))
                ins.then_inc(s["uc_ready"], 1)

            def xvo(i, dst):
                if i == 0:
                    pe.wait_ge(s["xvo_loaded"], 32)
                    for e in range(KE):
                        for c in range(KC):
                            ins = pe.matmul(dst[:, e:e + 1], xwv[:, c, e * P:(e + 1) * P], col("xattn_ln2_b", c), start=(c == 0), stop=(c == KC - 1))
                elif i <= XVO_TURNED:
                    for c in range(KC):
                        ins = pe.transpose(dst[:, c * P:(c + 1) * P], xwv[:, c, (i - 1) * P:i * P], ident_f[:, :])
                elif i < XVO_ROW:
                    m = i - XVO_TURNED - 1
                    pe.wait_ge(s["wo_out"], WO_OUT + XVO_TURNED)
                    for e in range(KE):
                        ins = pe.matmul(dst[:, :], wvT[:, e, m * P:(m + 1) * P], xwo[:, e, :], start=(e == 0), stop=(e == KE - 1))
                else:
                    for e in range(KE):
                        ins = pe.matmul(dst[:, :], sv_vec[:, e:e + 1].to_broadcast([P, P]), xwo[:, e, :], start=(e == 0), stop=(e == KE - 1))
                ins.then_inc(s["wo_ps"], 1)

            def extra(j):
                kind, i, dst, (readers, count) = EXTRA[j]
                pe.wait_ge(s[readers], count)
                if kind == "fold":
                    fold(1, i, dst)
                else:
                    xvo(i, dst)

            turn_rows(0)
            for m in range(KC + 1):
                fold(0, m, tb[m])
            turn_rows(1)
            pe.wait_ge(s["yT_out"], NT)
            for i in range(XVO_EARLY):
                at_least(pe, s["wo_out"], WO_OUT + i - 2 if i >= 2 else 0)
                xvo(i, (u_ps, max_ps)[i % 2])

            def turn(k, u, j):
                n, m = 2 * k + u, P if j < FT else TAIL
                pe.wait_ge(s["lo_ready"], NJ * n + j + 1)
                at_least(pe, s["evac_done"], NJ * n + j - 1)
                tp = turned(u, j)
                for h, src in enumerate((xh, xl)):
                    for c in range(KC):
                        ins = pe.transpose(tp[:, h, c, 0:m], src[u][0:m, j, c * P:(c + 1) * P], ident_h[0:m, 0:m])
                ins.then_inc(s["tp_ready"], 1)

            def scores(k, u, j):
                n, m = 2 * k + u, P if j < FT else TAIL
                if j == 0:
                    if isinstance(n, int) and n == 0:
                        pe.wait_ge(s["sel_ready"], 4)
                        pe.wait_ge(s["a_fp32"], KC + 1)
                    if isinstance(n, int) and n == 1:
                        pe.wait_ge(s["a_fp32"], NAF + KC + 1)
                        pe.wait_ge(s["wo_out"], WO_OUT + XVO_ROW)
                    at_least(pe, s["sub_done"], n - 1)
                    pe.wait_ge(acur_loaded[u], 16 * (k + 1))
                if j % BANKT == 0:
                    w = min(BANKT, NJ - j)
                    o = scores_ps[u][:, j * L:(j + w) * L].rearrange("p (t q) -> p t q", t=w)
                    pe.matmul(o, sel_b[:, :], acur[u][:, NPART * KC, :].unsqueeze(1).to_broadcast([P, w, L]),
                              start=True, stop=False, skip_group_check=True)
                pe.wait_ge(s["evac_done"], NJ * n + j + 1)
                for c in range(KC):
                    for h, parts in ((0, range(3)), (1, range(2))):
                        for part in parts:
                            ins = pe.matmul(scores_ps[u][0:m, j * L:(j + 1) * L], xT[(u + j) % 2][:, h, c, 0:m],
                                            acur[u][:, KC * part + c, :], start=False, stop=(c == KC - 1 and h == 1 and part == 1),
                                            skip_group_check=True)
                ins.then_inc(s["score_done"], 1)

            def turn_max(k, u):
                pe.wait_ge(s["max_all"], 2 * k + u + 1)
                pe.transpose(max_ps[:, 0:P], mx[:, :], ident_f[:, :]).then_inc(s["maxT_ready"], 1)

            def spread_max(k, u):
                pe.wait_ge(s["maxq_ready"], 2 * k + u + 1)
                pe.matmul(max_ps[:, P:P + L], mq[:, 0:1].to_broadcast([L, P]), ident_f[0:L, 0:L], start=True,
                          stop=True).then_inc(s["maxbc_ready"], 1)

            def products(k, u, js):
                n = 2 * k + u
                if js[0] == 0:
                    pe.wait_ge(s["pl_ready"], n + 1)
                    at_least(pe, s["c_ready"], n)
                for j in js:
                    m = P if j < FT else TAIL
                    for c in range(KC):
                        for a, b in ((xh, ph), (xh, pl), (xl, ph)):
                            pe.matmul(u_ps[:, c * L:(c + 1) * L], a[u][0:m, j, c * P:(c + 1) * P], b[u][0:m, j, :],
                                      start=(j == 0 and c == 0 and a is xh and b is ph), stop=(j == NJ - 1 and a is xl),
                                      skip_group_check=True)
                    for b in (ph, pl):
                        ins = pe.matmul(u_ps[:, KC * L:(KC + 1) * L], ones_h[0:m, :], b[u][0:m, j, :], start=False,
                                        stop=(j == NJ - 1 and b is pl), skip_group_check=True)
                    ins.then_inc(s["pv_done"], 1)

            def step(k, u, done=2):
                for j in range(NJ):
                    turn(k, u, j)
                    if j >= 1:
                        scores(k, u, j - 1)
                    elif done:
                        scores(*before(k, u), NJ - 1)
                    if done:
                        if j == 1:
                            turn_max(*before(k, u))
                        if j == 2:
                            spread_max(*before(k, u))
                    if j in PV_AT and PV_AT[j][0] <= done:
                        products(*back(k, u, PV_AT[j][0]), PV_AT[j][1])
                    if not done and j in EXTRA:
                        extra(j)

            step(0, 0, done=0)
            step(0, 1, done=1)
            with pe.Fori(1, B // 2 - 1) as k:
                step(k, 0)
                step(k, 1)
            step(B // 2 - 1, 0)
            step(B // 2 - 1, 1)
            scores(B // 2 - 1, 1, NJ - 1)
            products(B // 2 - 1, 0, range(5, NJ))
            turn_max(B // 2 - 1, 1)
            spread_max(B // 2 - 1, 1)
            products(B // 2 - 1, 1, range(NJ))

            pe.wait_ge(s["c_ready"], B)
            pe.wait_ge(s["dense_loaded"], 16 * 4)

            def small_sums():
                pe.wait_ge(s["rel_step"], 1)
                pe.wait_ge(s["rows_loaded"], 16 * (HC + 3))
                pe.matmul(wr[:, 0:REL], rel_rows.rearrange("r h d -> r (h d)"), anti_f[:, :], start=True, stop=True).then_inc(s["rel_ps"], 1)
                pe.wait_ge(s["wsum_done"], NW)
                pe.matmul(ww[:, 0:NW], ones_f[:, :], sm(WSUM, NW), start=True, stop=True).then_inc(s["rel_ps"], 1)
                pe.wait_ge(s["ab_step"], 1)
                pe.transpose(gbank[0][0:1, 0:P], sm(BMAX), ident_f[:, :]).then_inc(s["rel_ps"], 1)
                pe.wait_ge(s["ab_step"], 2)
                pe.matmul(gbank[1][:, 0:2], ones_f[0:1, :], small[0:1, 44:46], start=True, stop=True).then_inc(s["rel_ps"], 1)

            def turn_w(t, place):
                if not isinstance(t, int) or t > 1:
                    return
                for g in TURN_AT[t].get(place, []):
                    i, half = g // 2, g % 2
                    pe.wait_ge(s["ter_done"], i + 1)
                    at_least(pe, s["turned_w"], g)
                    for b in range(8):
                        at = (b % 4) * D + (2 * half + b // 4) * P if i < NW // 2 else (8 * half + b) * P
                        ins = pe.transpose(u_ps[:, b * P // 2:(b + 1) * P // 2].bitcast(F16), wter[i % 3][:, at:at + P], ident_h[:, :])
                    ins.then_inc(s["turned_w_ps"], 1)

            def xattn_o(t):
                pe.wait_ge(s["c2_ready"], t + 1)
                at_least(pe, s["ao_taken"], t - 1)
                for c in range(KC):
                    ins = pe.matmul(ws[:, :], c2T[:, c, :], xwvo[:, c, :], start=(c == 0), stop=(c == KC - 1))
                ins.then_inc(s["o_ps"], 1)

            def att_scores(t):
                pe.wait_ge(s["k2_taken"], KD * HC * (t + 1))
                pe.wait_ge(s["q2_taken"], KD * (t + 1))
                at_least(pe, s["ctx_taken"], 4 * t)
                for c in range(KD):
                    for v in range(2):
                        ins = pe.matmul(scores_ps[0][v * L:(v + 1) * L, c * HC * L:(c + 1) * HC * L], q2T[:, c, v * L:(v + 1) * L],
                                        kbd[:, c, v, :, :].rearrange("p h j -> p (h j)"), start=True, stop=True)
                ins.then_inc(s["s_ps"], 1)

            def ffn_in(t, f4s):
                for f4 in f4s:
                    if f4 == 0:
                        pe.wait_ge(s["zT_taken"], t + 1)
                    if f4 >= 2:
                        pe.wait_ge(s["gelu_done"], KF * t + 4 * (f4 - 1))
                    for f in range(4):
                        for c in range(KD):
                            for z in (zh, zl):
                                ins = pe.matmul(FBANK[f4][:, f * P:(f + 1) * P], w1T[:, c, (4 * f4 + f) * P:(4 * f4 + f + 1) * P], z[:, c, :],
                                                start=(c == 0 and z is zh), stop=(c == KD - 1 and z is zl))
                    ins.then_inc(s["f_ps"], 1)

            def att_turn(t):
                pe.wait_ge(s["pn_done"], t + 1)
                for i in range(2):
                    for q in range(4):
                        hp = 4 * i + q
                        ins = pe.transpose(gbank[i][:, q * P:(q + 1) * P], psb[:, 2 * hp:2 * hp + 2, :].rearrange("p a b -> p (a b)"), ident_f[:, :])
                    ins.then_inc(s["pt_ps"], 1)

            def y_turn(t):
                pe.wait_ge(s["y_ready"], t + 1)
                for c in range(KD):
                    ins = pe.transpose(ws[:, c * P:(c + 1) * P], yn[:, c * P:(c + 1) * P], ident_f[:, :])
                ins.then_inc(s["yT_ps"], 1)

            def ffn_out(t, half):
                pe.wait_ge(s["gl_ready%d" % half], t + 1)
                if half == 0:
                    at_least(pe, s["out_ready"], t)
                for f in range(KF // 2 * half, KF // 2 * (half + 1)):
                    for g in (gh, gl):
                        ins = pe.matmul(u_ps[:, :], g[:, f, :], w2T[:, f, :], start=(f == 0 and g is gh), stop=(f == KF - 1 and g is gl))
                if half == 1:
                    ins.then_inc(s["out_ps"], 1)

            def att_values(t):
                pe.wait_ge(s["pt_taken"], 2 * (t + 1))
                pe.wait_ge(s["v2_taken"], 4 * (t + 1))
                for i in range(2):
                    for q in range(4):
                        hp = 4 * i + q
                        ins = pe.matmul(scores_ps[0][:, hp * P:(hp + 1) * P], vbd[:, hp, :, :, :].rearrange("p a b c -> p (a b c)"), ptT[:, hp, :],
                                        start=True, stop=True)
                    ins.then_inc(s["ctx_ps"], 1)

            def q_or_k(t, dst, w, done, c3):
                pe.wait_ge(s["yT_taken"], t + 1)
                if c3:
                    pe.wait_ge(s["gelu_done"], KF * (t - 2) + (12 if w is awq else 16))
                for m in range(KD):
                    for c in range(KD):
                        ins = pe.matmul(dst[:, m * P:(m + 1) * P], w[:, c, m * P:(m + 1) * P], yT[:, c, :], start=(c == 0), stop=(c == KD - 1))
                ins.then_inc(s[done], 1)

            def att_o(t):
                pe.wait_ge(s["ctx_taken"], 4 * (t + 1))
                for c in range(KD):
                    ins = pe.matmul(ws[:, :], ctxT[:, c, :], awo[:, c, :], start=(c == 0), stop=(c == KD - 1))
                ins.then_inc(s["ao_ps"], 1)

            def relative(t):
                pe.wait_ge(s["q2_taken"], KD * (t + 1))
                at_least(pe, s["pt_taken"], 2 * (t - 1))
                for c in range(KD):
                    if c >= 2:
                        pe.wait_ge(s["g_taken"], KD * t + c - 1)
                    pe.matmul(gbank[c % 2], q2T[:, c, :], relbd.rearrange("p h r -> p (h r)"), start=True, stop=True).then_inc(s["g_ps"], 1)

            def values(t):
                pe.wait_ge(s["q2_taken"], KD * (t + 1))
                for c in range(KD):
                    ins = pe.matmul(wr[:, :], yT[:, c, :], awv[:, c, :], start=(c == 0), stop=(c == KD - 1))
                ins.then_inc(s["v2_ps"], 1)

            def z_turn(t):
                pe.wait_ge(s["z_ready"], t + 1)
                for c in range(KD):
                    ins = pe.transpose(ww[:, c * P:(c + 1) * P], zn[:, c * P:(c + 1) * P], ident_f[:, :])
                ins.then_inc(s["zT_ps"], 1)

            def dense(t, c1, c2, c3):
                if c2:
                    att_scores(t - 1)
                turn_w(t, "scores")
                if c3:
                    z_turn(t - 2)
                if c1:
                    xattn_o(t)
                if isinstance(t, int) and t == 0:
                    small_sums()
                turn_w(t, "xattn_o")
                if c3:
                    if isinstance(t, int) and t == 2:
                        pe.wait_ge(s["turned_w"], 2 * NW)
                    ffn_in(t - 2, range(3))
                if c1:
                    pe.wait_ge(s["o_taken"], t + 1)
                    y_turn(t)
                turn_w(t, "y_turn")
                if c3:
                    ffn_in(t - 2, [3])
                if c1:
                    if isinstance(t, int) and t == 0:
                        pe.wait_ge(s["small_done"], 1)
                    at_least(pe, s["v2_taken"], 4 * t)
                    q_or_k(t, wr, awq, "q2_ps", c3)
                    turn_w(t, "q")
                    q_or_k(t, ww, awk, "k2_ps", c3)
                    turn_w(t, "k")
                if c3:
                    ffn_out(t - 2, 0)
                if c1 and not c3:
                    values(t)
                if c1:
                    relative(t)
                turn_w(t, "relative")
                if c2:
                    if c1:
                        pe.wait_ge(s["g_taken"], KD * (t + 1))
                    att_turn(t - 1)
                turn_w(t, "att_turn")
                if c1 and c3:
                    values(t)
                turn_w(t, "values")
                if c2:
                    att_values(t - 1)
                turn_w(t, "att_values")
                if c3:
                    ffn_out(t - 2, 1)
                if c2:
                    att_o(t - 1)
                turn_w(t, "att_o")
            run_dense(pe, dense)

        @block.vector
        def _(dve):
            def stats(k, u, j):
                m, g = P if j < FT else TAIL, GROUP_OF[j]
                if j == GROUPS[g][0]:
                    dve.wait_ge(raw_loaded[u][g], (32 if g == NG - 1 else 16) * (k + 1))
                dve.bn_stats(st[u][0:m, j, :], raw[u][0:m, j, :]).then_inc(s["bn_done"], 1)

            def gather(k, u, j):
                n, m = 2 * k + u, P if j < FT else TAIL
                if isinstance(n, int):
                    dve.wait_ge(s["bn_done"], NJ * n + j + 1)
                dve.bn_aggr(mv[u][0:m, j, :], st[u][0:m, j, :]).then_inc(s["aggr_done"], 1)
                if j == GROUPS[GROUP_OF[j]][-1]:
                    variances(k, u, GROUP_OF[j])

            def variances(k, u, g):
                n, js = 2 * k + u, GROUPS[g]
                sl = slice(js[0], js[-1] + 1)
                dve.wait_ge(s["aggr_done"], NJ * n + js[-1] + 1)
                dve.tensor_scalar(nb[u][:, sl], mv[u][:, sl, 0], -1.0, None, ALU.mult).then_inc(s["negmu_ready"], 1)
                dve.tensor_scalar(ve[u][:, sl], mv[u][:, sl, 1], EPS, None, ALU.add).then_inc(s["var_ready"], 1)

            def early_stats():
                dve.wait_ge(s["raw_tail_zero"], 3)
                for j in range(NJ - 1):
                    stats(0, 0, j)
                for j in range(NJ - 2):
                    gather(0, 0, j)

            dve.wait_ge(s["vec_T"], 1)
            dve.tensor_copy(vec[:, :], max_ps[:, 0:NVEC]).then_inc(s["vec_ready"], 1)
            dve.tensor_scalar(vec_s[:, :], max_ps[:, 0:NVEC], SCALE, None, ALU.mult).then_inc(s["vec_ready"], 1)
            dve.memset(mx[:, L:P], 0.0).then_inc(s["raw_tail_zero"], 1)
            for u in range(2):
                dve.memset(mv[u][:, :, :], 1.0).then_inc(s["raw_tail_zero"], 1)
            def row_stats(i, h):
                src = (x_sb, y)[i]
                half = range(NT // 2 * h, NT // 2 * (h + 1))
                for t in half:
                    if i == 0:
                        dve.wait_ge(x_loaded[h], 16 * (NT // 2))
                    else:
                        dve.wait_ge(s["ln_done"], t + 1)
                    dve.bn_stats(ln_st[:, t, :], src[:, t, :]).then_inc(s["ln_stat"], 1)
                for t in half:
                    dve.wait_ge(s["ln_stat"], NT * i + t + 1)
                    dve.bn_aggr(ln_mv[:, t, :], ln_st[:, t, :]).then_inc(s["ln_aggr"], 1)
                dve.wait_ge(s["ln_aggr"], NT * i + half[-1] + 1)
                dve.tensor_scalar(ln_ve[:, half[0]:half[-1] + 1], ln_mv[:, half[0]:half[-1] + 1, 1], EPS, None, ALU.add).then_inc(s["ln_var"], 1)

            def row_norm(i, h):
                src = (x_sb, y)[i]
                dve.wait_ge(s["ln_rstd"], 2 * i + h + 1)
                for t in range(NT // 2 * h, NT // 2 * (h + 1)):
                    dve.tensor_scalar(y[:, t, :], src[:, t, :], ln_mv[:, t, 0:1], ln_r[:, t:t + 1], ALU.subtract,
                                      ALU.mult).then_inc(s["ln_done"], 1)

            row_stats(0, 0)
            row_stats(0, 1)
            row_norm(0, 0)
            row_stats(1, 0)
            row_norm(0, 1)
            row_stats(1, 1)
            row_norm(1, 0)
            row_norm(1, 1)
            early_stats()

            def weights(h, c, src):
                dve.wait_ge(s["uc_ready"], (KC + 1) * h + c + 1)
                at_least(dve, s["a_part"], NAF * h)
                if c < KC:
                    ins = dve.tensor_scalar(a_f[:, c, :], src[:, :], u_const[:, c:c + 1], cols("xattn_ln2_g", c), ALU.add, ALU.mult)
                else:
                    ins = dve.tensor_scalar(a_f[:, c, :], src[:, :], c_const[:, :], SCALE, ALU.add, ALU.mult)
                ins.then_inc(s["a_fp32"], 1)

            def leave(h, part, cs=range(KC + 1)):
                HB = 512 // L
                for c in cs:
                    dve.wait_ge(s["a_part"], NAF * h + (KC + 1) * (part - 1) + c + 1)
                    r = slice(0, P) if c < KC else slice((0, 64, 96)[part], P)
                    f = a_f[r, c, :].rearrange("p (b l) -> p b l", l=L)
                    dve.tensor_tensor(f, f, a_all[r, h * HB:(h + 1) * HB, KC * (part - 1) + c if c < KC else NPART * KC, :],
                                      ALU.subtract).then_inc(s["a_fp32"], 1)

            for c in range(KC + 1):
                weights(0, c, tb[c])
            for part in range(1, NPART):
                leave(0, part)

            def evacuate(k, u, j, taken):
                n, m = 2 * k + u, P if j < FT else TAIL + 1
                if taken:
                    dve.wait_ge(s["bn_done"], NJ * (2 * taken[0] + taken[1]) + taken[2] + 1)
                dve.wait_ge(s["tp_ready"], NJ * n + j + 1)
                at_least(dve, s["score_done"], NJ * n + j - 1)
                dve.tensor_copy(xT[(u + j) % 2][:, :, :, 0:m], turned(u, j)[:, :, :, 0:m]).then_inc(s["evac_done"], 1)

            def tiles_of(u, lo, hi):
                return scores_ps[u][:, lo * L:hi * L].rearrange("p (t q) -> p q t", q=L)

            def max_first(k, u):
                n = 2 * k + u
                dve.wait_ge(s["score_done"], NJ * n + BANKT)
                dve.tensor_reduce(mxa[:, :], tiles_of(u, 0, BANKT), AX.X, ALU.max).then_inc(s["max_a"], 1)

            def max_rest(k, u):
                n = 2 * k + u
                dve.wait_ge(s["score_done"], NJ * (n + 1))
                dve.tensor_reduce(mxb[:, :], tiles_of(u, BANKT, FT), AX.X, ALU.max).then_inc(s["max_b"], 1)
                dve.wait_ge(s["max_b"], n + 1)
                dve.tensor_tensor(mxb[0:TAIL, :], mxb[0:TAIL, :], scores_ps[u][0:TAIL, FT * L:NJ * L], ALU.max).then_inc(s["max_tail"], 1)
                dve.wait_ge(s["max_tail"], n + 1)
                dve.wait_ge(s["max_a"], n + 1)
                dve.tensor_tensor(mx[:, 0:L], mxa[:, :], mxb[:, :], ALU.max).then_inc(s["max_all"], 1)

            def max_of_query(k, u):
                n = 2 * k + u
                dve.wait_ge(s["maxT_ready"], n + 1)
                dve.tensor_reduce(mq[:, :], max_ps[0:L, 0:P], AX.X, ALU.max).then_inc(s["maxq_ready"], 1)

            def copy_max(k, u):
                n = 2 * k + u
                dve.wait_ge(s["maxbc_ready"], n + 1)
                dve.tensor_copy(mbc[:, :], max_ps[:, P:P + L]).then_inc(s["maxbc_copied"], 1)

            def subtract_max(k, u):
                n = 2 * k + u
                dve.wait_ge(s["maxbc_copied"], n + 1)
                at_least(dve, s["pl_ready"], n - 1)
                dve.tensor_tensor(pf[u][:, :, :], scores_ps[u][:, 0:NJ * L].rearrange("p (t q) -> p t q", q=L),
                                  mbc[:, :].unsqueeze(1).to_broadcast([P, NJ, L]), ALU.subtract).then_inc(s["sub_done"], 1)

            def context(k, u):
                n = 2 * k + u
                dve.wait_ge(s["pv_done"], NJ * (n + 1))
                dve.reciprocal(rz[:, :], u_ps[:, KC * L:(KC + 1) * L]).then_inc(s["rz_ready"], 1)
                dve.wait_ge(s["rz_ready"], n + 1)
                dve.tensor_tensor(cT[:, :, bass.ds(n * L, L)], u_ps[:, 0:KC * L].rearrange("p (c q) -> p c q", q=L),
                                  rz[:, :].unsqueeze(1).to_broadcast([P, KC, L]), ALU.mult).then_inc(s["c_ready"], 1)

            def step(k, u, done=2, last=False):
                for j in range(NJ):
                    ahead = (k, u, NJ - 1) if j == 0 else None if last else (*after(k, u), j - 1)
                    taken = (k, u, NJ - 2 + j) if j < 2 else None if last else (*after(k, u), j - 2)
                    if ahead:
                        stats(*ahead)
                    if done and j == 1:
                        max_rest(*before(k, u))
                    evacuate(k, u, j, taken)
                    if taken:
                        gather(*taken)
                    if done:
                        if j == 1:
                            max_of_query(*before(k, u))
                        if j == 3:
                            copy_max(*before(k, u))
                            subtract_max(*before(k, u))
                    if j == 8 and done == 2:
                        context(*back(k, u, 2))
                    if j == 9:
                        max_first(k, u)
                    if done == 0 and j - 1 in EXTRA and EXTRA[j - 1][0] == "fold":
                        weights(1, *EXTRA[j - 1][1:3])
                    if done == 1 and 1 <= j <= (NPART - 1) * (KC + 1):
                        leave(1, (j - 1) // (KC + 1) + 1, [(j - 1) % (KC + 1)])

            step(0, 0, done=0)
            step(0, 1, done=1)
            with dve.Fori(1, B // 2 - 1) as k:
                step(k, 0)
                step(k, 1)
            step(B // 2 - 1, 0)
            step(B // 2 - 1, 1, last=True)
            K = B // 2 - 1
            max_rest(K, 1)
            max_of_query(K, 1)
            copy_max(K, 1)
            subtract_max(K, 1)
            context(K, 0)
            context(K, 1)

            chain = [0]

            def link2(ins):
                chain[0] += 1
                ins.then_inc(s["ab2_step"], 1)
                dve.wait_ge(s["ab2_step"], chain[0])

            def small_values():
                dve.wait_ge(s["rel_ps"], 3)
                dve.tensor_reduce(small[0:1, 44:45], gbank[0][0:1, 0:P], AX.X, ALU.max).then_inc(s["inv_step"], 1)
                dve.tensor_reduce(small[0:1, 45:46], gbank[0][0:1, 0:P], AX.X, ALU.max).then_inc(s["inv_step"], 1)
                dve.wait_ge(s["inv_step"], 2)
                dve.tensor_scalar(ksc[:, :], vec[:, VEC["attn_bk"][0]:VEC["attn_bk"][0] + KD], DH ** -0.5, None, ALU.mult).then_inc(s["ab_step"], 1)
                for w in range(2):
                    link2(dve.tensor_reduce(sm(WSCALE + w), ww[:, NW // 2 * w:NW // 2 * (w + 1)], AX.X, ALU.add))
                link2(dve.tensor_scalar(sm(WTHR, 2), sm(WSCALE, 2), 1.0 / (F * D), 1e-8, ALU.mult, ALU.max))
                dve.tensor_scalar(sm(WNTHR, 2), sm(WTHR, 2), -0.5, None, ALU.mult).then_inc(s["wthr_ready"], 1)
                dve.wait_ge(s["wthr_ready"], 1)
                dve.tensor_scalar(sm(WTHR, 2), sm(WTHR, 2), 0.5, None, ALU.mult).then_inc(s["wthr_ready"], 1)
                dve.wait_ge(s["rel_ps"], 4)
                INT = mybir.dt.int32
                link2(dve.tensor_scalar(sm(BEXP), gbank[1][:, 0:1], float(D), None, ALU.add))
                link2(dve.tensor_scalar(sm(BEXP).bitcast(INT), sm(BEXP).bitcast(INT), 0x7F800000, None, ALU.bitwise_and))
                link2(dve.tensor_scalar(sm(FS).bitcast(INT), sm(BEXP).bitcast(INT), -1.0, float((127 + 14 + 127) << 23), ALU.mult, ALU.add))
                link2(dve.tensor_scalar(sm(FINV).bitcast(INT), sm(BEXP).bitcast(INT), 1.0, float(-(14 << 23)), ALU.mult, ALU.add))
                link2(dve.memset(relbd, 0.0))
                for h in range(HC - 1):
                    link2(dve.tensor_copy(relbd[h * DH:(h + 1) * DH, h, :], wr[h * DH:(h + 1) * DH, 0:REL]))
                dve.tensor_copy(relbd[(HC - 1) * DH:, HC - 1, :], wr[(HC - 1) * DH:, 0:REL]).then_inc(s["small_done"], 1)

            def ternary(i):
                dve.wait_ge(s["wthr_ready"], 2)
                dve.wait_ge(wraw_loaded[W_BUF[i]], 16 * (W_BUF[:i + 1].count(W_BUF[i])))
                at_least(dve, s["ter_done"], i)
                dve.tensor_scalar(wneg, wraw[W_BUF[i]], sm(WNTHR + i // 4), None, ALU.is_lt).then_inc(s["neg_done"], 1)
                dve.wait_ge(s["neg_done"], i + 1)
                at_least(dve, s["turned_w_ps"], 2 * (i - 2))
                dve.scalar_tensor_tensor(out=wter[i % 3], in0=wraw[W_BUF[i]], scalar=sm(WTHR + i // 4), in1=wneg, op0=ALU.is_gt,
                                         op1=ALU.subtract).then_inc(s["ter_done"], 1)

            dve.wait_ge(s["c_ready"], B)
            dve.wait_ge(s["pl_ready"], B)
            dve.tensor_reduce(sm(BMAX), vec[:, VEC["ffn_b1"][0]:VEC["ffn_b1"][0] + KF], AX.X, ALU.max, apply_absolute_value=True).then_inc(s["ab_step"], 1)

            def c2(t):
                at_least(dve, s["o_ps"], t)
                src = cT[:, :, t * P:(t + 1) * P] if isinstance(t, int) else cT[:, :, bass.ds(t * P, P)]
                dve.tensor_copy(c2T, src).then_inc(s["c2_ready"], 1)

            def layer_norm(t, src, dst, stat, mvc, vec_, rsc, names):
                a, b, c_, d_, e_ = names
                dve.bn_stats(sm(stat, 6), src).then_inc(s[a], 1)
                wait_alone(dve, s[a], t + 1)
                dve.bn_aggr(sm(mvc, 2), sm(stat, 6)).then_inc(s[b], 1)
                dve.wait_ge(s[b], t + 1)
                dve.tensor_scalar(sm(vec_), sm(mvc + 1), EPS, None, ALU.add).then_inc(s[c_], 1)
                dve.wait_ge(s[d_], t + 1)
                dve.tensor_scalar(dst, src, sm(mvc), sm(rsc), ALU.subtract, ALU.mult).then_inc(s[e_], 1)

            def softmax_a(t):
                dve.wait_ge(s["s_ps"], t + 1)
                at_least(dve, s["rowexp_done"], t)
                dve.tensor_scalar(ssb.rearrange("p a b -> p (a b)"), scores_ps[0][:, :], 1e5, -1e5, ALU.min, ALU.max).then_inc(s["clip_done"], 1)
                dve.wait_ge(s["clip_done"], t + 1)
                dve.wait_ge(s["r_loaded"], 32 * (t + 1))
                dve.tensor_tensor(ssb, ssb, rsk, ALU.add).then_inc(s["radd_done"], 1)
                dve.wait_ge(s["radd_done"], t + 1)
                dve.tensor_reduce(rows16[:, 0, :], ssb, AX.X, ALU.max).then_inc(s["rowmax_done"], 1)
                dve.wait_ge(s["rowmax_done"], t + 1)
                dve.tensor_tensor(ssb, ssb, rows16[:, 0, :].unsqueeze(2).to_broadcast([P, H, L]), ALU.subtract).then_inc(s["rowsub_done"], 1)

            def softmax_b(t):
                dve.wait_ge(s["rowexp_done"], t + 1)
                dve.tensor_reduce(rows16[:, 1, :], psb, AX.X, ALU.add).then_inc(s["rowsum_done"], 1)
                dve.wait_ge(s["rowsum_done"], t + 1)
                def lk(ins, i):
                    ins.then_inc(s["s_step"], 1)
                    dve.wait_ge(s["s_step"], 5 * t + i)
                lk(dve.reciprocal(rows16[:, 2, :], rows16[:, 1, :]), 1)
                lk(dve.tensor_tensor(rows16[:, 3, :], rows16[:, 1, :], rows16[:, 2, :], ALU.mult), 2)
                lk(dve.tensor_scalar(rows16[:, 3, :], rows16[:, 3, :], 1e-8, None, ALU.add), 3)
                lk(dve.reciprocal(rows16[:, 4, :], rows16[:, 3, :]), 4)
                lk(dve.tensor_tensor(rows16[:, 4, :], rows16[:, 4, :], rows16[:, 2, :], ALU.mult), 5)
                dve.tensor_tensor(psb, psb, rows16[:, 4, :].unsqueeze(2).to_broadcast([P, H, L]), ALU.mult).then_inc(s["pn_done"], 1)

            def x1(t):
                dve.wait_ge(s["xb_ready"], t + 2)
                dve.wait_ge(s["o_ps"], t + 1)
                dve.tensor_tensor(xc, tile(t), ws[:, :], ALU.add).then_inc(s["o_taken"], 1)
                dve.wait_ge(s["o_taken"], t + 1)
                dve.tensor_tensor(tile(t), xc, abo, ALU.add).then_inc(s["x1_step"], 1)
                layer_norm(t, xc, yn, STAT1, MV1, VE1, RS1, ("st1", "ag1", "va1", "rs1", "y_ready"))

            def x2(t):
                dve.wait_ge(s["x1_step"], t + 1)
                dve.wait_ge(s["ao_ps"], t + 1)
                at_least(dve, s["xb2_ready"], t)
                dve.tensor_tensor(zc, tile(t), ws[:, :], ALU.add).then_inc(s["ao_taken"], 1)
                dve.wait_ge(s["ao_taken"], t + 1)
                layer_norm(t, zc, zn, STAT2, MV2, VE2, RS2, ("st2", "ag2", "va2", "rs2", "z_ready"))

            def gelu_parts(t, half):
                sl = slice(KF // 2 * half, KF // 2 * (half + 1))
                dve.wait_ge(s["gelu_done"], KF * t + KF // 2 * (half + 1))
                if half == 0:
                    at_least(dve, s["out_ps"], t)
                dve.tensor_scalar(gh[:, sl, :], gf[:, sl, :], sm(FS), None, ALU.mult).then_inc(s["gh_ready"], 1)
                dve.wait_ge(s["gh_ready"], 2 * t + half + 1)
                dve.scalar_tensor_tensor(out=gl[:, sl, :], in0=gf[:, sl, :], scalar=sm(FS), in1=gh[:, sl, :], op0=ALU.mult,
                                         op1=ALU.subtract).then_inc(s["gl_ready%d" % half], 1)

            def ctx_out(t):
                dve.wait_ge(s["ctx_ps"], 2 * (t + 1))
                pv = scores_ps[0][:, :].rearrange("p (hc two r) -> p two hc r", two=2, r=P)
                for v in range(2):
                    for b2 in range(2):
                        dve.tensor_copy(ctxT[v * L:(v + 1) * L, :, b2 * L:(b2 + 1) * L],
                                        pv[b2 * L:(b2 + 1) * L, v, :, b2 * L:(b2 + 1) * L]).then_inc(s["ctx_taken"], 1)

            def v_out(t):
                dve.wait_ge(s["v2_ps"], t + 1)
                src = wr[:, :].rearrange("p (hp v d) -> p hp v d", v=2, d=DH)
                bias = abv.rearrange("p (hp v d) -> p hp v d", v=2, d=DH)
                for v in range(2):
                    for b2 in range(2):
                        r = slice(b2 * L, (b2 + 1) * L)
                        dve.tensor_tensor(vbd[v * L:(v + 1) * L, :, b2, v, :], src[r, :, v, :], bias[r, :, v, :],
                                          ALU.add).then_inc(s["v2_taken"], 1)

            def z_low(t):
                dve.wait_ge(s["zh_taken"], t + 1)
                dve.tensor_tensor(zl.rearrange("p a b -> p (a b)"), ww[:, :], zh.rearrange("p a b -> p (a b)"), ALU.subtract).then_inc(s["zT_taken"], 1)

            def result(t):
                dve.wait_ge(s["out_ps"], t + 1)
                dve.wait_ge(s["xb2_ready"], t + 1)
                at_least(dve, s["stored"], 16 * t)
                dve.scalar_tensor_tensor(out=ot, in0=u_ps[:, :], scalar=sm(FINV), in1=xb2, op0=ALU.mult, op1=ALU.add).then_inc(s["out_ready"], 1)

            def dense(t, c1, c2_, c3):
                first = t if isinstance(t, int) and t < 2 else None
                if c3:
                    z_low(t - 2)
                if c1:
                    x1(t)
                if first == 0:
                    small_values()
                if c1 and not (isinstance(t, int) and t == NT - 1):
                    c2(t + 1)
                if c2_:
                    softmax_a(t - 1)
                if first is not None:
                    ternary(4 * first)
                if c3:
                    gelu_parts(t - 2, 0)
                    gelu_parts(t - 2, 1)
                if c2_:
                    softmax_b(t - 1)
                if first is not None:
                    ternary(4 * first + 1)
                if first == 1:
                    ternary(6)
                if c2_:
                    ctx_out(t - 1)
                if first == 0:
                    dve.wait_ge(s["zeros_done"], 2)
                    dve.wait_ge(s["abv_loaded"], 16)
                if c1:
                    v_out(t)
                if first == 0:
                    ternary(2)
                    ternary(3)
                if c3:
                    result(t - 2)
                if first == 1:
                    ternary(7)
                if c2_:
                    x2(t - 1)
            c2(0)
            run_dense(dve, dense)


def kernel(**inputs):
    import numpy as _np
    import concourse.bacc as _bacc
    from concourse import mybir as _mybir
    from concourse.bass_utils import run_bass_kernel_spmd as _run

    nc = _bacc.Bacc("TRN2", target_bir_lowering=False, num_devices=1)
    arrays, args = {}, {}
    for name, a in inputs.items():
        a = _np.ascontiguousarray(a)
        arrays[f"in_{name}_dram"] = a
        args[name] = nc.dram_tensor(f"in_{name}_dram", a.shape, _mybir.dt.from_np(a.dtype), kind="ExternalInput").ap()
    out = nc.dram_tensor("out_dram", inputs["x"].shape, _mybir.dt.float32, kind="ExternalOutput").ap()
    build_program(nc, args, out)
    return _run(nc, [arrays], core_ids=[0]).results[0]["out_dram"]
```

```python
from contextlib import ExitStack

import concourse.bass as bass
from concourse import mybir

F32 = mybir.dt.float32
F16 = mybir.dt.float16
BF16 = mybir.dt.bfloat16
ALU = mybir.AluOpType
ACT = mybir.ActivationFunctionType
AX = mybir.AxisListType

P = 128


def build_program(nc, A, out):
    B, L, D = A["x"].shape
    _, S, DC = A["ctx_768"].shape
    E = A["L0_xattn_Wq"].shape[1]
    ROWS = B * L
    NT = ROWS // P
    KD, KC, KE = D // P, DC // P, E // P
    FT = S // P
    TAIL = S - FT * P
    NJ = FT + 1
    GROUPS = [range(0, 4), range(4, 9), range(9, NJ)]
    NG = len(GROUPS)
    GROUP_OF = {j: g for g, js in enumerate(GROUPS) for j in js}
    BANKT = 512 // L
    SCALE = float(E) ** -0.5
    EPS = 1e-5

    ctx = ExitStack()
    with ctx:
        def sb(name, shape, dt=F32):
            return ctx.enter_context(nc.sbuf_tensor(name, shape, dt))

        def sem(name):
            return ctx.enter_context(nc.semaphore(name))

        bank = [ctx.enter_context(nc.psum_tensor(f"bank{i}", [P, 512], F32)) for i in range(2)]
        scores_ps = [ctx.enter_context(nc.psum_tensor(f"scores_ps{i}", [P, 1024], F32)) for i in range(2)]
        u_ps = ctx.enter_context(nc.psum_tensor("u_ps", [P, 512], F32))
        max_ps = ctx.enter_context(nc.psum_tensor("max_ps", [P, 512], F32))

        ones_f = sb("ones_f", [P, P])
        ident_f = sb("ident_f", [P, P])
        ident_h = sb("ident_h", [P, P], F16)
        ones_h = sb("ones_h", [P, P], F16)
        minus_half = sb("minus_half", [P, 16])
        x_sb = sb("x_sb", [P, NT, D])
        VEC = {}
        rows = 0
        for key, n in (("xattn_ln1_g", KD), ("xattn_ln1_b", KD), ("xattn_bq", KE), ("xattn_bk", KE),
                       ("xattn_ln2_g", KC), ("xattn_ln2_b", KC), ("xattn_bv", KE), ("attn_bq", KD),
                       ("attn_bk", KD), ("ffn_b1", A["L0_ffn_b1"].shape[0] // P)):
            VEC[key] = (rows, n)
            rows += n
        NVEC = rows
        vec = sb("vec", [P, NVEC])
        vec_s = sb("vec_s", [P, NVEC])

        def cols(key, c):
            return vec_s[:, VEC[key][0] + c:VEC[key][0] + c + 1]

        def col(key, c):
            return vec[:, VEC[key][0] + c:VEC[key][0] + c + 1]

        yT_all = sb("yT_all", [P, KD, ROWS])
        cT = yT_all[:, 0:KC, :]
        sel_b = sb("sel_b", [P, P], BF16)
        t_vec = sb("t_vec", [P, KE])
        u_const = sb("u_const", [P, KC])
        c_const = sb("c_const", [P, 1])
        sv_vec = sb("sv_vec", [P, KE])
        AREA = 173 * 1024 + 288
        area = sb("area", [P, AREA // 4])

        def carve(at, shape, dt=F32):
            size = 1
            for n in shape[1:]:
                size *= n
            size *= mybir.dt.size(dt)
            assert at % 4 == 0 and at + size <= AREA, (at, size)
            v = area[0:shape[0], at // 4:(at + size + 3) // 4]
            v = v if dt == F32 else v.bitcast(dt)
            if len(shape) > 2:
                letters = "abcde"[:len(shape) - 1]
                v = v.rearrange(f"p ({' '.join(letters)}) -> p {' '.join(letters)}", **{l: n for l, n in zip(letters[1:], shape[2:])})
            return v, at + (size + 3) // 4 * 4

        at = 0
        wq, at = carve(at, [P, KD, E])
        wk, at = carve(at, [P, KC, E])
        wqT, at = carve(at, [P, KE, D])
        wkT, at = carve(at, [P, KE, DC + 1])
        wqk, at = carve(at, [P, KD, DC + 1])
        xwo, _ = carve(0, [P, KE, D])
        xwv, _ = carve(KD * E * 4, [P, KC, E])
        wvT, _ = carve((KD + KC) * E * 4, [P, KE, DC])
        DENSE_KEPT = at
        vec_rows, _ = carve(at, [NVEC, P])
        xwvo, at = carve(at, [P, KC, D])
        ln_st, ln_at = carve(at, [P, NT, 6])
        ln_mv, ln_at = carve(ln_at, [P, NT, 2])
        ln_ve, ln_at = carve(ln_at, [P, NT])
        ln_r, ln_at = carve(ln_at, [P, NT])
        abv, _ = carve(at, [P, D])
        xvo_bias, at = carve(at, [P, D])
        a_f, _ = carve(at, [P, KC + 1, 512])
        F = A["L0_ffn_b1"].shape[0]
        KF = F // P
        H = D // A["L0_attn_rel_emb"].shape[1]
        DH = D // H
        HC = P // DH
        HP = H // 2
        REL = 2 * L
        MAXP = (A["L0_attn_rel_emb"].shape[0] + 1) // 2
        rows16, _ = carve(at, [P, 5, H])
        rel_rows, at = carve(at, [REL, HC, DH])
        relbd, at = carve(at, [P, HC, REL])
        xbo, at = carve(at, [P, D])
        abo, at = carve(at, [P, D])
        fb2, at = carve(at, [P, D])
        small, at = carve(at, [P, 64])
        DENSE_BIG = at
        WPIECE = 4 * F // 4
        wsum_raw, _ = carve(0, [P, 4, WPIECE])

        def pair(shape, dt=F32):
            nonlocal at
            v0, at = carve(at, shape, dt)
            v1, at = carve(at, shape, dt)
            return [v0, v1]

        NPART = 3
        a_all, at = carve(at, [P, B, NPART * KC + 1, L], BF16)
        raw = pair([P, NJ, DC])
        y, _ = carve(at - NJ * DC * 4, [P, NT, D])
        xh, xl = [None, None], [None, None]
        for i in range(2):
            xh[i], at = carve(at, [P, NJ, DC], F16)
            xl[i], at = carve(at, [P, NJ, DC], F16)
        xT = pair([P, 2, KC, P], F16)
        st = pair([P, NJ, 6])
        mv = pair([P, NJ, 2])
        ve = pair([P, NJ])
        rs = pair([P, NJ])
        nb = pair([P, NJ])
        acur = pair([P, NPART * KC + 1, L], BF16)
        pf = pair([P, NJ, L])
        ph = pair([P, NJ, L], F16)
        pl = pair([P, NJ, L], F16)
        mxa, at = carve(at, [P, L])
        mxb, at = carve(at, [P, L])
        mx, at = carve(at, [P, P])
        mq, at = carve(at, [L, 1])
        mbc, at = carve(at, [P, L])
        rz, at = carve(at, [P, L])

        at = 0
        awq, at = carve(at, [P, KD, D])
        awk, at = carve(at, [P, KD, D])
        awv, at = carve(at, [P, KD, D])
        awo, at = carve(at, [P, KD, D])
        assert at <= DENSE_KEPT
        at = DENSE_BIG
        w1T, at = carve(at, [P, KD, F], F16)
        w2T, at = carve(at, [P, KF, D], F16)
        c2T, at = carve(at, [P, KC, P])
        yn, at = carve(at, [P, D])
        yT, at = carve(at, [P, KD, P])
        q2T, at = carve(at, [P, KD, P])
        kbd, at = carve(at, [P, KD, 2, HC, L])
        vbd, at = carve(at, [P, HP, 2, 2, DH])
        anti_f, _ = carve(at, [P, P])
        gs, at = carve(at, [P, H, REL])
        rsk, at = carve(at, [P, H, L])
        early_wraw = [carve(at + i * WPIECE * 4, [P, WPIECE])[0] for i in range(2)]
        ssb, at = carve(at, [P, H, L])
        psb, at = carve(at, [P, H, L])
        ptT, at = carve(at, [P, HP, P])
        ctxT, at = carve(at, [P, KD, P])
        zn, at = carve(at, [P, D])
        zh, at = carve(at, [P, KD, P], F16)
        zl, at = carve(at, [P, KD, P], F16)
        wneg, _ = carve(at, [P, WPIECE], F16)
        wter = [carve(at + (i + 1) * WPIECE * 2, [P, WPIECE], F16)[0] for i in range(3)]
        gf, at = carve(at, [P, KF, P])
        gh, at = carve(at, [P, KF, P], F16)
        gl, at = carve(at, [P, KF, P], F16)
        xb2, at = carve(at, [P, D])
        ot, at = carve(at, [P, D])
        xc, at = carve(at, [P, D])
        zc, at = carve(at, [P, D])
        wraw = [None, None]
        for i in range(2):
            wraw[i], at = carve(at, [P, WPIECE])
        wraw += early_wraw
        def sm(a, n=1):
            return small[:, a:a + n]
        STAT1, MV1, VE1, RS1, STAT2, MV2, VE2, RS2 = 0, 6, 8, 9, 10, 16, 18, 19
        WSUM, WSCALE, WTHR, WNTHR, BMAX, FS, FINV, BEXP = 20, 28, 30, 32, 39, 40, 41, 42
        ksc = sm(48, KD)
        skew = nc.dram_tensor("skew", (P, H * REL), F32, kind="Internal").ap()
        ws, wr, ww = bank[0], bank[1], max_ps
        gbank = [scores_ps[1][:, 0:512], scores_ps[1][:, 512:1024]]

        names = []
        names += ("consts_ready ident_ready sel_ready padding_set vec_loaded vec_turned vec_ready wq_loaded "
                    "wk_loaded xvo_loaded").split()
        names += ("ln_stat ln_aggr ln_var ln_rstd ln_done xT_ready yT_out").split()
        names += ("query_weights_ps query_weights_out folded_ps folded_f32 folded_part xvo_ps xvo_taken").split()
        names += ("key_stats_done key_moments_done var_ready negmu_ready rstd_ready shift_ready key_normed hi_ready "
                    "lo_ready key_turned turned_copied").split()
        names += ("score_done max_a max_b max_tail max_all maxT_ready maxq_ready maxbc_ready maxbc_copied sub_done "
                    "exp_done ph_ready pl_ready products_done reciprocal_ready context_ready").split()
        names += ("dense_loaded rows_loaded abv_loaded zeros_done anti_ready small_ps b1_step b1_max_step "
                    "small_step small_done wsum_done wthr_ready neg_done ternary_done turned_w_ps turned_w_taken "
                    "x_biased").split()
        names += ("context_tile_ready xattn_ps xattn_taken residual_ready ln1_stats ln1_moments ln1_var ln1_rstd "
                    "y_ready y_turned yT_taken").split()
        names += ("q_ps q_taken k_ps k_taken v_ps v_taken relative_ps relative_taken skew_stored skew_loaded").split()
        names += ("att_scores_ps clip_done radd_done rowmax_done rowsub_done rowexp_done rowsum_done row_scale_step "
                    "probs_ready probs_turned probs_taken values_ps values_taken att_out_ps att_out_taken ln2_stats "
                    "ln2_moments ln2_var ln2_rstd z_ready residual2_ready").split()
        names += ("z_turned z_high_ready z_low_ready hidden_ps gelu_done gelu_high_ready gelu_low_ready0 "
                    "gelu_low_ready1 ffn_out_ps out_ready stored").split()
        s = {n: sem(n) for n in names}
        raw_loaded = [[sem(f"raw_loaded{u}{g}") for g in range(NG)] for u in range(2)]
        x_loaded = [sem(f"x_loaded{h}") for h in range(2)]
        wsum_loaded = [sem(f"wsum_loaded{i}") for i in range(4)]
        wraw_loaded = [sem(f"wraw_loaded{i}") for i in range(4)]
        acur_loaded = [sem(f"acur_loaded{u}") for u in range(2)]

        ctx_in = A["ctx_768"]
        NAF = NPART * (KC + 1)
        tb = [scores_ps[0][:, 0:512], scores_ps[0][:, 512:1024], scores_ps[1][:, 0:512], scores_ps[1][:, 512:1024]]
        xb3 = [bank[0], bank[1], max_ps]
        OUT_S = 3 * KE
        OUT_T = OUT_S + KE
        OUT_C = OUT_T + KD + 2
        XVO_TURNED, XVO_ROW = KE, KE + KC + 1
        WO_OUT = KE
        XVO_EARLY = KE + 2
        EXTRA = {0: ("fold", 0, tb[2], ("folded_f32", KC + 1)),
                 2: ("fold", 1, tb[3], ("folded_f32", KC + 1)),
                 4: ("xvo", XVO_EARLY, u_ps, ("xvo_taken", WO_OUT + XVO_EARLY - 2)),
                 6: ("fold", 2, tb[2], ("folded_f32", NAF + 1)),
                 8: ("xvo", XVO_EARLY + 1, tb[3], ("folded_f32", NAF + 2)),
                 10: ("fold", 3, u_ps, ("xvo_taken", WO_OUT + XVO_EARLY)),
                 12: ("xvo", XVO_EARLY + 2, tb[2], ("folded_f32", NAF + 3))}
        FBANK = [wr, ww, wr, ww]
        TURN_AT = [{"k": [0], "relative": [1, 2], "values": [3]},
                   {"scores": [4], "xattn_o": [5], "y_turn": [6], "q": [7], "k": [8], "relative": [9], "att_turn": [10, 11],
                    "values": [12], "att_values": [13], "att_o": [14, 15]}]
        W_BUF = [0, 1, 2, 3, 0, 1, 0, 1]
        W_BEFORE = {4: 0, 5: 1, 6: 4, 7: 5}
        NW = 8

        def w_piece(i):
            if i < NW // 2:
                return A["L0_ffn_W1"].rearrange("(c p) e -> p c e", p=P)[:, 4 * i:4 * i + 4, :]
            return A["L0_ffn_W2"].rearrange("(c p) e -> p c e", p=P)[:, i - 4:i - 3, :]

        def before(k, u):
            return (k, 0) if u == 1 else (k - 1, 1)

        def after(k, u):
            return (k, 1) if u == 0 else (k + 1, 0)

        def turned(u, j):
            return bank[(u + j) % 2][:, 0:KC * P].bitcast(F16).rearrange("p (h c k) -> p h c k", h=2, c=KC)

        PV_AT = {j: (2, [j + 5]) for j in range(8)}
        PV_AT |= {9: (1, [0, 1]), 10: (1, [2]), 11: (1, [3]), 12: (1, [4])}

        def back(k, u, d):
            return (k, u) if d == 0 else back(*before(k, u), d - 1)

        def at_least(eng, semaphore, value):
            if not (isinstance(value, int) and value <= 0):
                eng.wait_ge(semaphore, value)

        def wait_alone(eng, semaphore, value):
            eng.wait_ge(s["ident_ready"], 1)
            eng.wait_ge(semaphore, value)

        out_rows = out.rearrange("b l d -> (b l) d")

        def rows(t):
            return slice(t * P, (t + 1) * P) if isinstance(t, int) else bass.ds(t * P, P)

        def tile(t):
            return x_sb[:, t, :] if isinstance(t, int) else x_sb[:, bass.ds(t, 1), :].squeeze(1)

        def run_dense(eng, step):
            step(0, True, False, False)
            step(1, True, True, False)
            step(2, True, True, True)
            with eng.Fori(3, NT - 1) as t:
                step(t, True, True, True)
            step(NT - 1, True, True, True)
            step(NT, False, True, True)
            step(NT + 1, False, False, True)

        block = ctx.enter_context(nc.Block())

        @block.sync
        def _(sp):
            sp.dma_start(wk[:, :, :], A["L0_xattn_Wk"].rearrange("(c p) e -> p c e", p=P)).then_inc(s["wk_loaded"], 16)
            sp.dma_start(wq[:, :, :], A["L0_xattn_Wq"].rearrange("(c p) e -> p c e", p=P)).then_inc(s["wq_loaded"], 16)
            for key, (r, n) in VEC.items():
                sp.dma_start(vec_rows[r:r + n, :], A["L0_" + key].rearrange("(c p) -> c p", p=P)).then_inc(s["vec_loaded"], 16)
            for t in range(NT):
                sp.dma_start(x_sb[:, t, :], A["x"].rearrange("b l d -> (b l) d")[t * P:(t + 1) * P, :]).then_inc(x_loaded[t // (NT // 2)], 16)

            def load_group(n, u, g):
                full = ctx_in[n, 0:FT * P, :] if isinstance(n, int) else ctx_in[bass.ds(n, 1), 0:FT * P, :].squeeze(0)
                full = full.rearrange("(p j) d -> p j d", j=FT)
                js = [j for j in GROUPS[g] if j < FT]
                sp.dma_start(raw[u][:, js[0]:js[-1] + 1, :], full[:, js[0]:js[-1] + 1, :]).then_inc(raw_loaded[u][g], 16)
                if g == NG - 1:
                    tail = ctx_in[n, FT * P:S, :] if isinstance(n, int) else ctx_in[bass.ds(n, 1), FT * P:S, :].squeeze(0)
                    sp.dma_start(raw[u][0:TAIL, FT, :], tail).then_inc(raw_loaded[u][g], 16)

            for g in range(NG):
                load_group(0, 0, g)
            sp.wait_ge(s["query_weights_ps"], 2 * KE + KD + 4)
            sp.dma_start(xwv, A["L0_xattn_Wv"].rearrange("(c p) e -> p c e", p=P)).then_inc(s["xvo_loaded"], 16)
            sp.dma_start(xwo, A["L0_xattn_Wo"].rearrange("(c p) e -> p c e", p=P)).then_inc(s["xvo_loaded"], 16)
            sp.wait_ge(s["xT_ready"], NT)
            for g in range(NG):
                load_group(1, 1, g)

            def load_a(n, u):
                sp.dma_start(acur[u][:, :, :], a_all[:, n, :, :] if isinstance(n, int) else
                             a_all[:, bass.ds(n, 1), :, :].squeeze(1)).then_inc(acur_loaded[u], 16)

            sp.wait_ge(s["folded_part"], NAF)
            load_a(0, 0)
            load_a(1, 1)

            def load_next(k, u, between=None):
                for g in range(NG):
                    wait_alone(sp, s["lo_ready"], NJ * 2 * k + NJ * u + GROUPS[g][-1] + 1)
                    load_group(2 * k + 2 + u, u, g)
                    if between is not None:
                        between(g)
                wait_alone(sp, s["score_done"], NJ * 2 * k + NJ * (u + 1))
                load_a(2 * k + 2 + u, u)

            def load_for_sum(i):
                if i >= 4:
                    sp.wait_ge(s["wsum_done"], i - 3)
                src = w_piece(i)
                sp.dma_start(wsum_raw[:, i % 4, :].rearrange("p (c e) -> p c e", c=src.shape[1]), src).then_inc(wsum_loaded[i % 4], 16)

            load_next(0, 0)
            load_next(0, 1)
            sp.wait_ge(s["folded_part"], 2 * NAF)
            sp.wait_ge(s["xvo_ps"], XVO_ROW + 1)
            for i in range(4):
                load_for_sum(i)
            first_rel = MAXP - 1 - L
            for h in range(HC):
                sp.dma_start(rel_rows[:, h, :], A["L0_attn_rel_emb"][first_rel:first_rel + REL, :]).then_inc(s["rows_loaded"], 16)
            for dst, key in ((xbo, "xattn_bo"), (abo, "attn_bo"), (fb2, "ffn_b2")):
                sp.dma_start(dst, A["L0_" + key].partition_broadcast(P)).then_inc(s["rows_loaded"], 16)

            def more_for_sum(g):
                load_for_sum(4 + g)
                if g == NG - 1:
                    load_for_sum(NW - 1)

            load_next(1, 0, more_for_sum)
            load_next(1, 1)
            sp.wait_ge(s["wsum_done"], NW)
            for dst, key in ((awq, "attn_Wq"), (awk, "attn_Wk"), (awv, "attn_Wv"), (awo, "attn_Wo")):
                sp.dma_start(dst, A["L0_" + key].rearrange("(c p) e -> p c e", p=P)).then_inc(s["dense_loaded"], 16)
            with sp.Fori(2, B // 2 - 1) as k:
                load_next(k, 0)
                load_next(k, 1)

            sp.wait_ge(s["context_ready"], B)

            def load_w(i):
                if i in W_BEFORE:
                    sp.wait_ge(s["ternary_done"], W_BEFORE[i] + 1)
                src = w_piece(i)
                sp.dma_start(wraw[W_BUF[i]].rearrange("p (c e) -> p c e", c=src.shape[1]), src).then_inc(wraw_loaded[W_BUF[i]], 16)

            for i in range(4):
                load_w(i)
            sp.wait_ge(s["x_biased"], 1)
            sp.dma_start(abv, A["L0_attn_bv"].partition_broadcast(P)).then_inc(s["abv_loaded"], 16)
            for i in range(4, 6):
                load_w(i)

            def skew_store(t):
                at_least(sp, s["radd_done"], t)
                sp.wait_ge(s["relative_taken"], KD * (t + 1))
                sp.dma_start(skew, gs.rearrange("p h r -> p (h r)")).then_inc(s["skew_stored"], 16)

            def skew_load(t):
                sp.wait_ge(s["skew_stored"], 16 * (t + 1))
                for v in range(2):
                    src = bass.AP(tensor=skew.tensor, offset=v * L * H * REL + L - 1, ap=[[H * REL - 1, L], [REL, H], [1, L]])
                    sp.dma_start(rsk[v * L:(v + 1) * L, :, :], src).then_inc(s["skew_loaded"], 16)

            def store(t):
                wait_alone(sp, s["out_ready"], t + 1)
                sp.dma_start(out_rows[rows(t), :], ot).then_inc(s["stored"], 16)

            def dense(t, proj, att, ffn):
                if proj:
                    skew_store(t)
                    skew_load(t)
                if isinstance(t, int) and t == 0:
                    for i in range(6, NW):
                        load_w(i)
                if ffn:
                    store(t - 2)
            run_dense(sp, dense)
            sp.wait_ge(s["stored"], 16 * NT)

        @block.gpsimd
        def _(pool):
            pool.memset(ones_f[:, :], 1.0).then_inc(s["consts_ready"], 1)
            pool.memset(minus_half[:, :], -0.5).then_inc(s["consts_ready"], 1)
            pool.wait_ge(s["consts_ready"], 2)
            pool.affine_select(out=ident_f[:, :], in_=ones_f[:, :], compare_op=ALU.is_equal, fill=0.0, base=0,
                               pattern=[[-1, P]], channel_multiplier=1).then_inc(s["ident_ready"], 1)
            pool.memset(sel_b[:, :], 0.0).then_inc(s["sel_ready"], 1)
            pool.wait_ge(s["sel_ready"], 1)
            for row in (0, 64, 96):
                pool.memset(sel_b[row:row + 1, :], 1.0).then_inc(s["sel_ready"], 1)
            pool.wait_ge(s["sel_ready"], 4)
            for i in range(4):
                sl = slice(NT // 2 * (i % 2), NT // 2 * (i % 2 + 1))
                pool.wait_ge(s["ln_var"], i + 1)
                pool.tensor_tensor(ln_r[:, sl], ln_ve[:, sl], minus_half[:, 0:NT // 2], ALU.pow).then_inc(s["ln_rstd"], 1)

            def rstd(k, u, g):
                n = 2 * k + u
                js = GROUPS[g]
                sl = slice(js[0], js[-1] + 1)
                pool.wait_ge(s["var_ready"], NG * n + g + 1)
                pool.tensor_tensor(rs[u][:, sl], ve[u][:, sl], minus_half[:, 0:len(js)], ALU.pow).then_inc(s["rstd_ready"], 1)
                pool.wait_ge(s["rstd_ready"], NG * n + g + 1)
                pool.tensor_tensor(nb[u][:, sl], nb[u][:, sl], rs[u][:, sl], ALU.mult).then_inc(s["shift_ready"], 1)

            def low_part(k, u, j):
                n = 2 * k + u
                m = P if j < FT else TAIL
                pool.wait_ge(s["hi_ready"], NJ * n + j + 1)
                pool.tensor_tensor(xl[u][0:m, j, :], raw[u][0:m, j, :], xh[u][0:m, j, :], ALU.subtract).then_inc(s["lo_ready"], 1)

            def p_low(k, u):
                n = 2 * k + u
                pool.wait_ge(s["ph_ready"], n + 1)
                pool.tensor_tensor(pl[u][:, :, :], pf[u][:, :, :], ph[u][:, :, :], ALU.subtract).then_inc(s["pl_ready"], 1)

            def step(k, u, first=False, last=False):
                for j in range(NJ):
                    low_part(k, u, j)
                    if j == 0:
                        rstd(k, u, 1)
                    if j == 4:
                        rstd(k, u, 2)
                    if j == 8 and not last:
                        rstd(*after(k, u), 0)
                    if j == 10 and not first:
                        p_low(*before(k, u))

            rstd(0, 0, 0)
            step(0, 0, first=True)
            step(0, 1)
            with pool.Fori(1, B // 2 - 1) as k:
                step(k, 0)
                step(k, 1)
            step(B // 2 - 1, 0)
            step(B // 2 - 1, 1, last=True)
            p_low(B // 2 - 1, 1)

            def pw(a, b, t, var, done):
                pool.wait_ge(s[var], t + 1)
                pool.tensor_tensor(sm(b), sm(a), minus_half[:, 0:1], ALU.pow).then_inc(s[done], 1)

            pool.wait_ge(s["context_ready"], B)
            pool.affine_select(out=anti_f[:, :], in_=ones_f[:, :], compare_op=ALU.is_equal, fill=0.0, base=-(P - 1),
                               pattern=[[1, P]], channel_multiplier=1).then_inc(s["anti_ready"], 1)
            pool.wait_ge(s["anti_ready"], 1)
            pool.wait_ge(s["rows_loaded"], 16 * (HC + 3))
            pool.tensor_tensor(xbo, xbo, xvo_bias, ALU.add).then_inc(s["x_biased"], 1)
            pool.wait_ge(s["x_biased"], 1)

            def with_bias(ts):
                for t in ts:
                    pool.tensor_tensor(x_sb[:, t, :], x_sb[:, t, :], xbo, ALU.add).then_inc(s["x_biased"], 1)

            with_bias([0])
            pool.memset(kbd, 0.0).then_inc(s["zeros_done"], 1)
            pool.memset(vbd, 0.0).then_inc(s["zeros_done"], 1)

            def dense(t, proj, att, ffn):
                if proj:
                    pw(VE1, RS1, t, "ln1_var", "ln1_rstd")
                if isinstance(t, int) and t == 0:
                    with_bias(range(1, NT))
                if att:
                    pw(VE2, RS2, t - 1, "ln2_var", "ln2_rstd")
                    pool.wait_ge(s["att_out_taken"], t)
                    at_least(pool, s["out_ready"], t - 1)
                    pool.tensor_tensor(xb2, zc, fb2, ALU.add).then_inc(s["residual2_ready"], 1)
            run_dense(pool, dense)

        @block.scalar
        def _(act):
            act.wait_ge(s["ident_ready"], 1)
            act.copy(ident_h[:, :], ident_f[:, :]).then_inc(s["ident_ready"], 1)
            act.copy(ones_h[:, :], ones_f[:, :]).then_inc(s["ident_ready"], 1)
            act.wait_ge(s["vec_ready"], 2)
            for e in range(KE):
                act.wait_ge(s["query_weights_ps"], e + 1)
                act.copy(wkT[:, e, 0:DC], tb[e][:, 0:DC]).then_inc(s["query_weights_out"], 1)
            for e in range(KE):
                act.wait_ge(s["query_weights_ps"], KE + e + 1)
                act.copy(wqT[:, e, :], tb[e]).then_inc(s["query_weights_out"], 1)
            act.wait_ge(s["query_weights_ps"], 2 * KE + 2)
            for e in range(KE):
                act.activation(wkT[:, e, DC:DC + 1], u_ps[:, e:e + 1], ACT.Identity, bias=col("xattn_bk", e), scale=1.0).then_inc(s["query_weights_out"], 1)
            act.wait_ge(s["query_weights_ps"], 2 * KE + 2)
            for e in range(KE):
                act.activation(t_vec[:, e:e + 1], u_ps[:, KE + e:KE + e + 1], ACT.Identity, bias=col("xattn_bq", e), scale=1.0).then_inc(s["query_weights_out"], 1)
            for c in range(KD):
                act.wait_ge(s["query_weights_ps"], 2 * KE + 3 + c)
                act.activation(wqk[:, c, :], tb[c][:, 0:DC + 1], ACT.Identity, bias=0.0, scale=col("xattn_ln1_g", c)).then_inc(s["query_weights_out"], 1)
            act.wait_ge(s["query_weights_ps"], 2 * KE + KD + 4)
            act.copy(u_const[:, :], u_ps[:, 8:8 + KC]).then_inc(s["query_weights_out"], 1)
            act.copy(c_const[:, :], u_ps[:, 16:17]).then_inc(s["query_weights_out"], 1)

            def rows_out(h):
                for t in range(NT // 2 * h, NT // 2 * (h + 1)):
                    act.wait_ge(s["xT_ready"], t + 1)
                    act.copy(yT_all[:, :, t * P:(t + 1) * P], xb3[t % 3][:, :].rearrange("p (c r) -> p c r", c=KD)).then_inc(s["yT_out"], 1)

            def parts_out(h, part, cs=range(KC + 1)):
                HB = 512 // L
                for c in cs:
                    act.wait_ge(s["folded_f32"], NAF * h + (KC + 1) * part + c + 1)
                    if c < KC:
                        dst = a_all[:, h * HB:(h + 1) * HB, KC * part + c, :]
                        act.copy(dst, a_f[:, c, :].rearrange("p (b l) -> p b l", l=L)).then_inc(s["folded_part"], 1)
                    else:
                        r = slice((0, 64, 96)[part], P)
                        act.copy(a_all[r, h * HB:(h + 1) * HB, NPART * KC, :],
                                 a_f[r, c, :].rearrange("p (b l) -> p b l", l=L)).then_inc(s["folded_part"], 1)

            def xvo_out(i, src):
                act.wait_ge(s["xvo_ps"], i + 1)
                if i == 0:
                    for e in range(KE):
                        act.activation(sv_vec[:, e:e + 1], src[:, e:e + 1], ACT.Identity, bias=col("xattn_bv", e), scale=1.0).then_inc(s["xvo_taken"], 1)
                elif i <= XVO_TURNED:
                    act.copy(wvT[:, i - 1, :], src[:, 0:DC]).then_inc(s["xvo_taken"], 1)
                elif i < XVO_ROW:
                    m = i - XVO_TURNED - 1
                    act.activation(xwvo[:, m, :], src[:, :], ACT.Identity, bias=0.0, scale=col("xattn_ln2_g", m)).then_inc(s["xvo_taken"], 1)
                else:
                    act.copy(xvo_bias, src[:, :]).then_inc(s["xvo_taken"], 1)

            rows_out(0)
            rows_out(1)
            parts_out(0, 0)
            xvo_out(0, u_ps)
            parts_out(0, 1)
            for i in range(1, 5):
                xvo_out(i, (u_ps, max_ps)[i % 2])
            parts_out(0, 2)

            def norm(k, u, j):
                n = 2 * k + u
                m = P if j < FT else TAIL
                act.wait_ge(s["shift_ready"], NG * n + GROUP_OF[j] + 1)
                act.activation(raw[u][0:m, j, :], raw[u][0:m, j, :], ACT.Identity, bias=nb[u][0:m, j:j + 1],
                               scale=rs[u][0:m, j:j + 1]).then_inc(s["key_normed"], 1)

            def high_part(k, u, j):
                n = 2 * k + u
                m = P if j < FT else TAIL
                act.wait_ge(s["key_normed"], NJ * n + j + 1)
                at_least(act, s["products_done"], NJ * (n - 2) + j + 1 if not isinstance(n, int) or n >= 2 else 0)
                act.copy(xh[u][0:m, j, :], raw[u][0:m, j, :]).then_inc(s["hi_ready"], 1)

            def exps(k, u):
                n = 2 * k + u
                act.wait_ge(s["sub_done"], n + 1)
                act.activation(pf[u][:, :, :], pf[u][:, :, :], ACT.Exp, bias=0.0, scale=1.0).then_inc(s["exp_done"], 1)

            def p_high(k, u):
                n = 2 * k + u
                act.wait_ge(s["exp_done"], n + 1)
                act.copy(ph[u][:, :, :], pf[u][:, :, :]).then_inc(s["ph_ready"], 1)

            def magnitudes(i):
                act.wait_ge(wsum_loaded[i % 4], 16 * (i // 4 + 1))
                act.activation(wsum_raw[:, i % 4, :], wsum_raw[:, i % 4, :], ACT.Abs, bias=0.0, scale=1.0,
                               accum_out=sm(WSUM + i)).then_inc(s["wsum_done"], 1)

            def step(k, u, first=False, extra=None):
                for j in range(NJ):
                    norm(k, u, j)
                    if extra in (2, 3) and j in (3, 6, 9, 12):
                        magnitudes(NW // 2 * (extra - 2) + j // 3 - 1)
                    if extra == 0:
                        if j == 2:
                            xvo_out(5, max_ps)
                        if j in (7, 11):
                            xvo_out(*EXTRA[j - 3][1:3])
                    if extra == 1:
                        if j == 2:
                            xvo_out(*EXTRA[NJ - 1][1:3])
                        if j < NAF:
                            parts_out(1, j // (KC + 1), [j % (KC + 1)])
                    if j >= 1:
                        high_part(k, u, j - 1)
                    if j == 9 and not first:
                        exps(*before(k, u))
                    if j == 10 and not first:
                        p_high(*before(k, u))
                high_part(k, u, NJ - 1)

            step(0, 0, first=True, extra=0)
            step(0, 1, extra=1)
            step(1, 0, extra=2)
            step(1, 1, extra=3)
            with act.Fori(2, B // 2 - 1) as k:
                step(k, 0)
                step(k, 1)
            step(B // 2 - 1, 0)
            step(B // 2 - 1, 1)
            exps(B // 2 - 1, 1)
            p_high(B // 2 - 1, 1)

            def gelus(t, f4s):
                for f4 in f4s:
                    act.wait_ge(s["hidden_ps"], 4 * t + f4 + 1)
                    if f4 % 2 == 0:
                        at_least(act, s["gelu_low_ready%d" % (f4 // 2)], t)
                    for f in range(4):
                        act.activation(gf[:, 4 * f4 + f, :], FBANK[f4][:, f * P:(f + 1) * P], ACT.Gelu, bias=col("ffn_b1", 4 * f4 + f),
                                       scale=1.0).then_inc(s["gelu_done"], 1)

            def row_exp(t):
                act.wait_ge(s["rowsub_done"], t + 1)
                act.activation(psb, ssb, ACT.Exp, bias=0.0, scale=1.0).then_inc(s["rowexp_done"], 1)

            def pt_out(t):
                for i in range(2):
                    act.wait_ge(s["probs_turned"], 2 * t + i + 1)
                    at_least(act, s["values_ps"], 2 * t)
                    act.copy(ptT[:, 4 * i:4 * i + 4, :].rearrange("p a b -> p (a b)"), gbank[i]).then_inc(s["probs_taken"], 1)

            def yT_out(t):
                act.wait_ge(s["y_turned"], t + 1)
                at_least(act, s["v_ps"], t)
                act.copy(yT.rearrange("p a b -> p (a b)"), ws[:, :]).then_inc(s["yT_taken"], 1)

            def q_out(t):
                act.wait_ge(s["q_ps"], t + 1)
                for m in range(KD):
                    act.activation(q2T[:, m, :], wr[:, m * P:(m + 1) * P], ACT.Identity, bias=col("attn_bq", m), scale=1.0).then_inc(s["q_taken"], 1)

            def k_out(t):
                if isinstance(t, int) and t == 0:
                    act.wait_ge(s["zeros_done"], 2)
                    act.wait_ge(s["small_done"], 1)
                act.wait_ge(s["k_ps"], t + 1)
                for m in range(KD):
                    for h in range(HC):
                        act.activation(kbd[h * DH:(h + 1) * DH, m, :, h, :],
                                       ww[h * DH:(h + 1) * DH, m * P:(m + 1) * P].rearrange("p (b j) -> p b j", b=2), ACT.Identity,
                                       bias=ksc[h * DH:(h + 1) * DH, m:m + 1], scale=DH ** -0.5).then_inc(s["k_taken"], 1)

            def g_out(t, cs):
                for c in cs:
                    act.wait_ge(s["relative_ps"], KD * t + c + 1)
                    if c == cs[0]:
                        at_least(act, s["skew_stored"], 16 * t)
                    act.copy(gs[:, HC * c:HC * (c + 1), :].rearrange("p a b -> p (a b)"), gbank[c % 2]).then_inc(s["relative_taken"], 1)

            def z_out(t):
                act.wait_ge(s["z_turned"], t + 1)
                at_least(act, s["hidden_ps"], 4 * t)
                act.copy(zh.rearrange("p a b -> p (a b)"), ww[:, :]).then_inc(s["z_high_ready"], 1)

            def turned_out(t, place):
                if not isinstance(t, int) or t > 1:
                    return
                for g in TURN_AT[t].get(place, []):
                    act.wait_ge(s["turned_w_ps"], g + 1)
                    i, half = g // 2, g % 2
                    src = u_ps[:, :].bitcast(F16)
                    if i < NW // 2:
                        act.copy(w1T[:, 2 * half:2 * half + 2, 4 * i * P:4 * (i + 1) * P], src.rearrange("p (o f) -> p o f", o=2)).then_inc(s["turned_w_taken"], 1)
                    else:
                        act.copy(w2T[:, 8 * half:8 * half + 8, (i - 4) * P:(i - 3) * P], src.rearrange("p (f o) -> p f o", f=8)).then_inc(s["turned_w_taken"], 1)

            def dense(t, proj, att, ffn):
                turned_out(t, "scores")
                turned_out(t, "xattn_o")
                if ffn:
                    z_out(t - 2)
                    gelus(t - 2, range(3))
                if proj:
                    yT_out(t)
                turned_out(t, "y_turn")
                if ffn:
                    gelus(t - 2, [3])
                if att:
                    row_exp(t - 1)
                if proj:
                    q_out(t)
                    turned_out(t, "q")
                    k_out(t)
                    turned_out(t, "k")
                    g_out(t, range(KD))
                turned_out(t, "relative")
                if att:
                    pt_out(t - 1)
                for place in ("att_turn", "values", "att_values", "att_o"):
                    turned_out(t, place)
            run_dense(act, dense)

        @block.tensor
        def _(pe):
            pe.wait_ge(s["ident_ready"], 3)
            pe.wait_ge(s["vec_loaded"], 16 * len(VEC))
            pe.transpose(max_ps[:, 0:NVEC], vec_rows[:, :], ident_f[0:NVEC, 0:NVEC]).then_inc(s["vec_turned"], 1)
            pe.wait_ge(s["wk_loaded"], 16)
            for e in range(KE):
                for c in range(KC):
                    ins = pe.transpose(tb[e][:, c * P:(c + 1) * P], wk[:, c, e * P:(e + 1) * P], ident_f[:, :])
                ins.then_inc(s["query_weights_ps"], 1)
            pe.wait_ge(s["wq_loaded"], 16)
            for e in range(KE):
                pe.wait_ge(s["query_weights_out"], e + 1)
                for c in range(KD):
                    ins = pe.transpose(tb[e][:, c * P:(c + 1) * P], wq[:, c, e * P:(e + 1) * P], ident_f[:, :])
                ins.then_inc(s["query_weights_ps"], 1)
            pe.wait_ge(s["vec_ready"], 2)
            for n, (w, vec_key, kk) in enumerate(((wk, "xattn_ln2_b", KC), (wq, "xattn_ln1_b", KD))):
                for e in range(KE):
                    for c in range(kk):
                        ins = pe.matmul(u_ps[:, KE * n + e:KE * n + e + 1], w[:, c, e * P:(e + 1) * P], col(vec_key, c),
                                        start=(c == 0), stop=(c == kk - 1))
                ins.then_inc(s["query_weights_ps"], 1)
            pe.wait_ge(s["query_weights_out"], OUT_S)
            for c in range(KD):
                for e in range(KE):
                    ins = pe.matmul(tb[c][:, 0:DC + 1], wqT[:, e, c * P:(c + 1) * P], wkT[:, e, :], start=(e == 0), stop=(e == KE - 1))
                ins.then_inc(s["query_weights_ps"], 1)
            pe.wait_ge(s["query_weights_out"], OUT_T)
            for m in range(KC):
                for e in range(KE):
                    ins = pe.matmul(u_ps[:, 8 + m:9 + m], wkT[:, e, m * P:(m + 1) * P], t_vec[:, e:e + 1], start=(e == 0), stop=(e == KE - 1))
            ins.then_inc(s["query_weights_ps"], 1)
            for e in range(KE):
                ins = pe.matmul(u_ps[:, 16:17], t_vec[:, e:e + 1].to_broadcast([P, P]), wkT[:, e, DC:DC + 1], start=(e == 0), stop=(e == KE - 1))
            ins.then_inc(s["query_weights_ps"], 1)

            def turn_rows(h):
                for t in range(NT // 2 * h, NT // 2 * (h + 1)):
                    pe.wait_ge(s["ln_done"], NT + t + 1)
                    at_least(pe, s["yT_out"], t - 2)
                    for c in range(KD):
                        ins = pe.transpose(xb3[t % 3][:, c * P:(c + 1) * P], y[:, t, c * P:(c + 1) * P], ident_f[:, :])
                    ins.then_inc(s["xT_ready"], 1)

            def fold(h, m, dst):
                if m == 0:
                    pe.wait_ge(s["yT_out"], NT // 2 * (h + 1))
                    pe.wait_ge(s["query_weights_out"], OUT_C)
                for c in range(KD):
                    w = wqk[:, c, m * P:(m + 1) * P] if m < KC else wqk[:, c, DC:DC + 1].to_broadcast([P, P])
                    ins = pe.matmul(dst[:, :], w, yT_all[:, c, h * 512:(h + 1) * 512], start=(c == 0), stop=(c == KD - 1))
                ins.then_inc(s["folded_ps"], 1)

            def xvo(i, dst):
                if i == 0:
                    pe.wait_ge(s["xvo_loaded"], 32)
                    for e in range(KE):
                        for c in range(KC):
                            ins = pe.matmul(dst[:, e:e + 1], xwv[:, c, e * P:(e + 1) * P], col("xattn_ln2_b", c), start=(c == 0), stop=(c == KC - 1))
                elif i <= XVO_TURNED:
                    for c in range(KC):
                        ins = pe.transpose(dst[:, c * P:(c + 1) * P], xwv[:, c, (i - 1) * P:i * P], ident_f[:, :])
                elif i < XVO_ROW:
                    m = i - XVO_TURNED - 1
                    pe.wait_ge(s["xvo_taken"], WO_OUT + XVO_TURNED)
                    for e in range(KE):
                        ins = pe.matmul(dst[:, :], wvT[:, e, m * P:(m + 1) * P], xwo[:, e, :], start=(e == 0), stop=(e == KE - 1))
                else:
                    for e in range(KE):
                        ins = pe.matmul(dst[:, :], sv_vec[:, e:e + 1].to_broadcast([P, P]), xwo[:, e, :], start=(e == 0), stop=(e == KE - 1))
                ins.then_inc(s["xvo_ps"], 1)

            def extra(j):
                kind, i, dst, (readers, count) = EXTRA[j]
                pe.wait_ge(s[readers], count)
                if kind == "fold":
                    fold(1, i, dst)
                else:
                    xvo(i, dst)

            turn_rows(0)
            for m in range(KC + 1):
                fold(0, m, tb[m])
            turn_rows(1)
            pe.wait_ge(s["yT_out"], NT)
            for i in range(XVO_EARLY):
                at_least(pe, s["xvo_taken"], WO_OUT + i - 2 if i >= 2 else 0)
                xvo(i, (u_ps, max_ps)[i % 2])

            def turn(k, u, j):
                n, m = 2 * k + u, P if j < FT else TAIL
                pe.wait_ge(s["lo_ready"], NJ * n + j + 1)
                at_least(pe, s["turned_copied"], NJ * n + j - 1)
                tp = turned(u, j)
                for h, src in enumerate((xh, xl)):
                    for c in range(KC):
                        ins = pe.transpose(tp[:, h, c, 0:m], src[u][0:m, j, c * P:(c + 1) * P], ident_h[0:m, 0:m])
                ins.then_inc(s["key_turned"], 1)

            def scores(k, u, j):
                n, m = 2 * k + u, P if j < FT else TAIL
                if j == 0:
                    if isinstance(n, int) and n == 0:
                        pe.wait_ge(s["sel_ready"], 4)
                        pe.wait_ge(s["folded_f32"], KC + 1)
                    if isinstance(n, int) and n == 1:
                        pe.wait_ge(s["folded_f32"], NAF + KC + 1)
                        pe.wait_ge(s["xvo_taken"], WO_OUT + XVO_ROW)
                    at_least(pe, s["sub_done"], n - 1)
                    pe.wait_ge(acur_loaded[u], 16 * (k + 1))
                if j % BANKT == 0:
                    w = min(BANKT, NJ - j)
                    o = scores_ps[u][:, j * L:(j + w) * L].rearrange("p (t q) -> p t q", t=w)
                    pe.matmul(o, sel_b[:, :], acur[u][:, NPART * KC, :].unsqueeze(1).to_broadcast([P, w, L]),
                              start=True, stop=False, skip_group_check=True)
                pe.wait_ge(s["turned_copied"], NJ * n + j + 1)
                for c in range(KC):
                    for h, parts in ((0, range(3)), (1, range(2))):
                        for part in parts:
                            ins = pe.matmul(scores_ps[u][0:m, j * L:(j + 1) * L], xT[(u + j) % 2][:, h, c, 0:m],
                                            acur[u][:, KC * part + c, :], start=False, stop=(c == KC - 1 and h == 1 and part == 1),
                                            skip_group_check=True)
                ins.then_inc(s["score_done"], 1)

            def turn_max(k, u):
                pe.wait_ge(s["max_all"], 2 * k + u + 1)
                pe.transpose(max_ps[:, 0:P], mx[:, :], ident_f[:, :]).then_inc(s["maxT_ready"], 1)

            def spread_max(k, u):
                pe.wait_ge(s["maxq_ready"], 2 * k + u + 1)
                pe.matmul(max_ps[:, P:P + L], mq[:, 0:1].to_broadcast([L, P]), ident_f[0:L, 0:L], start=True,
                          stop=True).then_inc(s["maxbc_ready"], 1)

            def products(k, u, js):
                n = 2 * k + u
                if js[0] == 0:
                    pe.wait_ge(s["pl_ready"], n + 1)
                    at_least(pe, s["context_ready"], n)
                for j in js:
                    m = P if j < FT else TAIL
                    for c in range(KC):
                        for a, b in ((xh, ph), (xh, pl), (xl, ph)):
                            pe.matmul(u_ps[:, c * L:(c + 1) * L], a[u][0:m, j, c * P:(c + 1) * P], b[u][0:m, j, :],
                                      start=(j == 0 and c == 0 and a is xh and b is ph), stop=(j == NJ - 1 and a is xl),
                                      skip_group_check=True)
                    for b in (ph, pl):
                        ins = pe.matmul(u_ps[:, KC * L:(KC + 1) * L], ones_h[0:m, :], b[u][0:m, j, :], start=False,
                                        stop=(j == NJ - 1 and b is pl), skip_group_check=True)
                    ins.then_inc(s["products_done"], 1)

            def step(k, u, done=2):
                for j in range(NJ):
                    turn(k, u, j)
                    if j >= 1:
                        scores(k, u, j - 1)
                    elif done:
                        scores(*before(k, u), NJ - 1)
                    if done:
                        if j == 1:
                            turn_max(*before(k, u))
                        if j == 2:
                            spread_max(*before(k, u))
                    if j in PV_AT and PV_AT[j][0] <= done:
                        products(*back(k, u, PV_AT[j][0]), PV_AT[j][1])
                    if not done and j in EXTRA:
                        extra(j)

            step(0, 0, done=0)
            step(0, 1, done=1)
            with pe.Fori(1, B // 2 - 1) as k:
                step(k, 0)
                step(k, 1)
            step(B // 2 - 1, 0)
            step(B // 2 - 1, 1)
            scores(B // 2 - 1, 1, NJ - 1)
            products(B // 2 - 1, 0, range(5, NJ))
            turn_max(B // 2 - 1, 1)
            spread_max(B // 2 - 1, 1)
            products(B // 2 - 1, 1, range(NJ))

            pe.wait_ge(s["context_ready"], B)
            pe.wait_ge(s["dense_loaded"], 16 * 4)

            def small_sums():
                pe.wait_ge(s["anti_ready"], 1)
                pe.wait_ge(s["rows_loaded"], 16 * (HC + 3))
                pe.matmul(wr[:, 0:REL], rel_rows.rearrange("r h d -> r (h d)"), anti_f[:, :], start=True, stop=True).then_inc(s["small_ps"], 1)
                pe.wait_ge(s["wsum_done"], NW)
                pe.matmul(ww[:, 0:NW], ones_f[:, :], sm(WSUM, NW), start=True, stop=True).then_inc(s["small_ps"], 1)
                pe.wait_ge(s["b1_step"], 1)
                pe.transpose(gbank[0][0:1, 0:P], sm(BMAX), ident_f[:, :]).then_inc(s["small_ps"], 1)
                pe.wait_ge(s["b1_step"], 2)
                pe.matmul(gbank[1][:, 0:2], ones_f[0:1, :], small[0:1, 44:46], start=True, stop=True).then_inc(s["small_ps"], 1)

            def turn_w(t, place):
                if not isinstance(t, int) or t > 1:
                    return
                for g in TURN_AT[t].get(place, []):
                    i, half = g // 2, g % 2
                    pe.wait_ge(s["ternary_done"], i + 1)
                    at_least(pe, s["turned_w_taken"], g)
                    for b in range(8):
                        at = (b % 4) * D + (2 * half + b // 4) * P if i < NW // 2 else (8 * half + b) * P
                        ins = pe.transpose(u_ps[:, b * P // 2:(b + 1) * P // 2].bitcast(F16), wter[i % 3][:, at:at + P], ident_h[:, :])
                    ins.then_inc(s["turned_w_ps"], 1)

            def xattn_o(t):
                pe.wait_ge(s["context_tile_ready"], t + 1)
                at_least(pe, s["att_out_taken"], t - 1)
                for c in range(KC):
                    ins = pe.matmul(ws[:, :], c2T[:, c, :], xwvo[:, c, :], start=(c == 0), stop=(c == KC - 1))
                ins.then_inc(s["xattn_ps"], 1)

            def att_scores(t):
                pe.wait_ge(s["k_taken"], KD * HC * (t + 1))
                pe.wait_ge(s["q_taken"], KD * (t + 1))
                at_least(pe, s["values_taken"], 4 * t)
                for c in range(KD):
                    for v in range(2):
                        ins = pe.matmul(scores_ps[0][v * L:(v + 1) * L, c * HC * L:(c + 1) * HC * L], q2T[:, c, v * L:(v + 1) * L],
                                        kbd[:, c, v, :, :].rearrange("p h j -> p (h j)"), start=True, stop=True)
                ins.then_inc(s["att_scores_ps"], 1)

            def ffn_in(t, f4s):
                for f4 in f4s:
                    if f4 == 0:
                        pe.wait_ge(s["z_low_ready"], t + 1)
                    if f4 >= 2:
                        pe.wait_ge(s["gelu_done"], KF * t + 4 * (f4 - 1))
                    for f in range(4):
                        for c in range(KD):
                            for z in (zh, zl):
                                ins = pe.matmul(FBANK[f4][:, f * P:(f + 1) * P], w1T[:, c, (4 * f4 + f) * P:(4 * f4 + f + 1) * P], z[:, c, :],
                                                start=(c == 0 and z is zh), stop=(c == KD - 1 and z is zl))
                    ins.then_inc(s["hidden_ps"], 1)

            def att_turn(t):
                pe.wait_ge(s["probs_ready"], t + 1)
                for i in range(2):
                    for q in range(4):
                        hp = 4 * i + q
                        ins = pe.transpose(gbank[i][:, q * P:(q + 1) * P], psb[:, 2 * hp:2 * hp + 2, :].rearrange("p a b -> p (a b)"), ident_f[:, :])
                    ins.then_inc(s["probs_turned"], 1)

            def y_turn(t):
                pe.wait_ge(s["y_ready"], t + 1)
                for c in range(KD):
                    ins = pe.transpose(ws[:, c * P:(c + 1) * P], yn[:, c * P:(c + 1) * P], ident_f[:, :])
                ins.then_inc(s["y_turned"], 1)

            def ffn_out(t, quarters):
                half = quarters[0] // 2
                pe.wait_ge(s["gelu_low_ready%d" % half], t + 1)
                if quarters[0] == 0:
                    at_least(pe, s["out_ready"], t)
                for f in range(KF // 4 * quarters[0], KF // 4 * (quarters[-1] + 1)):
                    for g in (gh, gl):
                        ins = pe.matmul(u_ps[:, :], g[:, f, :], w2T[:, f, :], start=(f == 0 and g is gh), stop=(f == KF - 1 and g is gl))
                if quarters[-1] == 3:
                    ins.then_inc(s["ffn_out_ps"], 1)

            def att_values(t):
                pe.wait_ge(s["probs_taken"], 2 * (t + 1))
                pe.wait_ge(s["v_taken"], 4 * (t + 1))
                for i in range(2):
                    for q in range(4):
                        hp = 4 * i + q
                        ins = pe.matmul(scores_ps[0][:, hp * P:(hp + 1) * P], vbd[:, hp, :, :, :].rearrange("p a b c -> p (a b c)"), ptT[:, hp, :],
                                        start=True, stop=True)
                    ins.then_inc(s["values_ps"], 1)

            def q_or_k(t, dst, w, done, ffn):
                pe.wait_ge(s["yT_taken"], t + 1)
                if ffn:
                    pe.wait_ge(s["gelu_done"], KF * (t - 2) + (12 if w is awq else 16))
                for m in range(KD):
                    for c in range(KD):
                        ins = pe.matmul(dst[:, m * P:(m + 1) * P], w[:, c, m * P:(m + 1) * P], yT[:, c, :], start=(c == 0), stop=(c == KD - 1))
                ins.then_inc(s[done], 1)

            def att_o(t):
                pe.wait_ge(s["values_taken"], 4 * (t + 1))
                for c in range(KD):
                    ins = pe.matmul(ws[:, :], ctxT[:, c, :], awo[:, c, :], start=(c == 0), stop=(c == KD - 1))
                ins.then_inc(s["att_out_ps"], 1)

            def relative(t):
                pe.wait_ge(s["q_taken"], KD * (t + 1))
                at_least(pe, s["probs_taken"], 2 * (t - 1))
                for c in range(KD):
                    if c >= 2:
                        pe.wait_ge(s["relative_taken"], KD * t + c - 1)
                    pe.matmul(gbank[c % 2], q2T[:, c, :], relbd.rearrange("p h r -> p (h r)"), start=True, stop=True).then_inc(s["relative_ps"], 1)

            def values(t):
                pe.wait_ge(s["q_taken"], KD * (t + 1))
                for c in range(KD):
                    ins = pe.matmul(wr[:, :], yT[:, c, :], awv[:, c, :], start=(c == 0), stop=(c == KD - 1))
                ins.then_inc(s["v_ps"], 1)

            def z_turn(t):
                pe.wait_ge(s["z_ready"], t + 1)
                for c in range(KD):
                    ins = pe.transpose(ww[:, c * P:(c + 1) * P], zn[:, c * P:(c + 1) * P], ident_f[:, :])
                ins.then_inc(s["z_turned"], 1)

            def dense(t, proj, att, ffn):
                if att:
                    att_scores(t - 1)
                turn_w(t, "scores")
                if ffn:
                    z_turn(t - 2)
                if proj:
                    xattn_o(t)
                if isinstance(t, int) and t == 0:
                    small_sums()
                turn_w(t, "xattn_o")
                if ffn:
                    if isinstance(t, int) and t == 2:
                        pe.wait_ge(s["turned_w_taken"], 2 * NW)
                    ffn_in(t - 2, range(3))
                if proj:
                    pe.wait_ge(s["xattn_taken"], t + 1)
                    y_turn(t)
                turn_w(t, "y_turn")
                if ffn:
                    ffn_in(t - 2, [3])
                if proj:
                    if isinstance(t, int) and t == 0:
                        pe.wait_ge(s["small_done"], 1)
                    at_least(pe, s["v_taken"], 4 * t)
                    q_or_k(t, wr, awq, "q_ps", ffn)
                    turn_w(t, "q")
                    q_or_k(t, ww, awk, "k_ps", ffn)
                    turn_w(t, "k")
                if ffn:
                    ffn_out(t - 2, [0, 1])
                if proj and not ffn:
                    values(t)
                if proj:
                    relative(t)
                turn_w(t, "relative")
                if att:
                    if proj:
                        pe.wait_ge(s["relative_taken"], KD * (t + 1))
                    att_turn(t - 1)
                turn_w(t, "att_turn")
                if proj and ffn:
                    values(t)
                turn_w(t, "values")
                if att:
                    att_values(t - 1)
                turn_w(t, "att_values")
                if ffn:
                    ffn_out(t - 2, [2])
                if att:
                    att_o(t - 1)
                if ffn:
                    ffn_out(t - 2, [3])
                turn_w(t, "att_o")
            run_dense(pe, dense)

        @block.vector
        def _(dve):
            def stats(k, u, j):
                m, g = P if j < FT else TAIL, GROUP_OF[j]
                if j == GROUPS[g][0]:
                    dve.wait_ge(raw_loaded[u][g], (32 if g == NG - 1 else 16) * (k + 1))
                dve.bn_stats(st[u][0:m, j, :], raw[u][0:m, j, :]).then_inc(s["key_stats_done"], 1)

            def gather(k, u, j):
                n, m = 2 * k + u, P if j < FT else TAIL
                if isinstance(n, int):
                    dve.wait_ge(s["key_stats_done"], NJ * n + j + 1)
                dve.bn_aggr(mv[u][0:m, j, :], st[u][0:m, j, :]).then_inc(s["key_moments_done"], 1)
                if j == GROUPS[GROUP_OF[j]][-1]:
                    variances(k, u, GROUP_OF[j])

            def variances(k, u, g):
                n, js = 2 * k + u, GROUPS[g]
                sl = slice(js[0], js[-1] + 1)
                dve.wait_ge(s["key_moments_done"], NJ * n + js[-1] + 1)
                dve.tensor_scalar(nb[u][:, sl], mv[u][:, sl, 0], -1.0, None, ALU.mult).then_inc(s["negmu_ready"], 1)
                dve.tensor_scalar(ve[u][:, sl], mv[u][:, sl, 1], EPS, None, ALU.add).then_inc(s["var_ready"], 1)

            def early_stats():
                dve.wait_ge(s["padding_set"], 3)
                for j in range(NJ - 1):
                    stats(0, 0, j)
                for j in range(NJ - 2):
                    gather(0, 0, j)

            dve.wait_ge(s["vec_turned"], 1)
            dve.tensor_copy(vec[:, :], max_ps[:, 0:NVEC]).then_inc(s["vec_ready"], 1)
            dve.tensor_scalar(vec_s[:, :], max_ps[:, 0:NVEC], SCALE, None, ALU.mult).then_inc(s["vec_ready"], 1)
            dve.memset(mx[:, L:P], 0.0).then_inc(s["padding_set"], 1)
            for u in range(2):
                dve.memset(mv[u][:, :, :], 1.0).then_inc(s["padding_set"], 1)
            def row_stats(i, h):
                src = (x_sb, y)[i]
                half = range(NT // 2 * h, NT // 2 * (h + 1))
                for t in half:
                    if i == 0:
                        dve.wait_ge(x_loaded[h], 16 * (NT // 2))
                    else:
                        dve.wait_ge(s["ln_done"], t + 1)
                    dve.bn_stats(ln_st[:, t, :], src[:, t, :]).then_inc(s["ln_stat"], 1)
                for t in half:
                    dve.wait_ge(s["ln_stat"], NT * i + t + 1)
                    dve.bn_aggr(ln_mv[:, t, :], ln_st[:, t, :]).then_inc(s["ln_aggr"], 1)
                dve.wait_ge(s["ln_aggr"], NT * i + half[-1] + 1)
                dve.tensor_scalar(ln_ve[:, half[0]:half[-1] + 1], ln_mv[:, half[0]:half[-1] + 1, 1], EPS, None, ALU.add).then_inc(s["ln_var"], 1)

            def row_norm(i, h):
                src = (x_sb, y)[i]
                dve.wait_ge(s["ln_rstd"], 2 * i + h + 1)
                for t in range(NT // 2 * h, NT // 2 * (h + 1)):
                    dve.tensor_scalar(y[:, t, :], src[:, t, :], ln_mv[:, t, 0:1], ln_r[:, t:t + 1], ALU.subtract,
                                      ALU.mult).then_inc(s["ln_done"], 1)

            row_stats(0, 0)
            row_stats(0, 1)
            row_norm(0, 0)
            row_stats(1, 0)
            row_norm(0, 1)
            row_stats(1, 1)
            row_norm(1, 0)
            row_norm(1, 1)
            early_stats()

            def weights(h, c, src):
                dve.wait_ge(s["folded_ps"], (KC + 1) * h + c + 1)
                at_least(dve, s["folded_part"], NAF * h)
                if c < KC:
                    ins = dve.tensor_scalar(a_f[:, c, :], src[:, :], u_const[:, c:c + 1], cols("xattn_ln2_g", c), ALU.add, ALU.mult)
                else:
                    ins = dve.tensor_scalar(a_f[:, c, :], src[:, :], c_const[:, :], SCALE, ALU.add, ALU.mult)
                ins.then_inc(s["folded_f32"], 1)

            def leave(h, part, cs=range(KC + 1)):
                HB = 512 // L
                for c in cs:
                    dve.wait_ge(s["folded_part"], NAF * h + (KC + 1) * (part - 1) + c + 1)
                    r = slice(0, P) if c < KC else slice((0, 64, 96)[part], P)
                    f = a_f[r, c, :].rearrange("p (b l) -> p b l", l=L)
                    dve.tensor_tensor(f, f, a_all[r, h * HB:(h + 1) * HB, KC * (part - 1) + c if c < KC else NPART * KC, :],
                                      ALU.subtract).then_inc(s["folded_f32"], 1)

            for c in range(KC + 1):
                weights(0, c, tb[c])
            for part in range(1, NPART):
                leave(0, part)

            def evacuate(k, u, j, taken):
                n, m = 2 * k + u, P if j < FT else TAIL + 1
                if taken:
                    dve.wait_ge(s["key_stats_done"], NJ * (2 * taken[0] + taken[1]) + taken[2] + 1)
                dve.wait_ge(s["key_turned"], NJ * n + j + 1)
                at_least(dve, s["score_done"], NJ * n + j - 1)
                dve.tensor_copy(xT[(u + j) % 2][:, :, :, 0:m], turned(u, j)[:, :, :, 0:m]).then_inc(s["turned_copied"], 1)

            def tiles_of(u, lo, hi):
                return scores_ps[u][:, lo * L:hi * L].rearrange("p (t q) -> p q t", q=L)

            def max_first(k, u):
                n = 2 * k + u
                dve.wait_ge(s["score_done"], NJ * n + BANKT)
                dve.tensor_reduce(mxa[:, :], tiles_of(u, 0, BANKT), AX.X, ALU.max).then_inc(s["max_a"], 1)

            def max_rest(k, u):
                n = 2 * k + u
                dve.wait_ge(s["score_done"], NJ * (n + 1))
                dve.tensor_reduce(mxb[:, :], tiles_of(u, BANKT, FT), AX.X, ALU.max).then_inc(s["max_b"], 1)
                dve.wait_ge(s["max_b"], n + 1)
                dve.tensor_tensor(mxb[0:TAIL, :], mxb[0:TAIL, :], scores_ps[u][0:TAIL, FT * L:NJ * L], ALU.max).then_inc(s["max_tail"], 1)
                dve.wait_ge(s["max_tail"], n + 1)
                dve.wait_ge(s["max_a"], n + 1)
                dve.tensor_tensor(mx[:, 0:L], mxa[:, :], mxb[:, :], ALU.max).then_inc(s["max_all"], 1)

            def max_of_query(k, u):
                n = 2 * k + u
                dve.wait_ge(s["maxT_ready"], n + 1)
                dve.tensor_reduce(mq[:, :], max_ps[0:L, 0:P], AX.X, ALU.max).then_inc(s["maxq_ready"], 1)

            def copy_max(k, u):
                n = 2 * k + u
                dve.wait_ge(s["maxbc_ready"], n + 1)
                dve.tensor_copy(mbc[:, :], max_ps[:, P:P + L]).then_inc(s["maxbc_copied"], 1)

            def subtract_max(k, u):
                n = 2 * k + u
                dve.wait_ge(s["maxbc_copied"], n + 1)
                at_least(dve, s["pl_ready"], n - 1)
                dve.tensor_tensor(pf[u][:, :, :], scores_ps[u][:, 0:NJ * L].rearrange("p (t q) -> p t q", q=L),
                                  mbc[:, :].unsqueeze(1).to_broadcast([P, NJ, L]), ALU.subtract).then_inc(s["sub_done"], 1)

            def context(k, u):
                n = 2 * k + u
                dve.wait_ge(s["products_done"], NJ * (n + 1))
                dve.reciprocal(rz[:, :], u_ps[:, KC * L:(KC + 1) * L]).then_inc(s["reciprocal_ready"], 1)
                dve.wait_ge(s["reciprocal_ready"], n + 1)
                dve.tensor_tensor(cT[:, :, bass.ds(n * L, L)], u_ps[:, 0:KC * L].rearrange("p (c q) -> p c q", q=L),
                                  rz[:, :].unsqueeze(1).to_broadcast([P, KC, L]), ALU.mult).then_inc(s["context_ready"], 1)

            def step(k, u, done=2, last=False):
                for j in range(NJ):
                    ahead = (k, u, NJ - 1) if j == 0 else None if last else (*after(k, u), j - 1)
                    taken = (k, u, NJ - 2 + j) if j < 2 else None if last else (*after(k, u), j - 2)
                    if ahead:
                        stats(*ahead)
                    if done and j == 1:
                        max_rest(*before(k, u))
                    evacuate(k, u, j, taken)
                    if taken:
                        gather(*taken)
                    if done:
                        if j == 1:
                            max_of_query(*before(k, u))
                        if j == 3:
                            copy_max(*before(k, u))
                            subtract_max(*before(k, u))
                    if j == 8 and done == 2:
                        context(*back(k, u, 2))
                    if j == 9:
                        max_first(k, u)
                    if done == 0 and j - 1 in EXTRA and EXTRA[j - 1][0] == "fold":
                        weights(1, *EXTRA[j - 1][1:3])
                    if done == 1 and 1 <= j <= (NPART - 1) * (KC + 1):
                        leave(1, (j - 1) // (KC + 1) + 1, [(j - 1) % (KC + 1)])

            step(0, 0, done=0)
            step(0, 1, done=1)
            with dve.Fori(1, B // 2 - 1) as k:
                step(k, 0)
                step(k, 1)
            step(B // 2 - 1, 0)
            step(B // 2 - 1, 1, last=True)
            K = B // 2 - 1
            max_rest(K, 1)
            max_of_query(K, 1)
            copy_max(K, 1)
            subtract_max(K, 1)
            context(K, 0)
            context(K, 1)

            chain = [0]

            def link(ins):
                chain[0] += 1
                ins.then_inc(s["small_step"], 1)
                dve.wait_ge(s["small_step"], chain[0])

            def small_values():
                dve.wait_ge(s["small_ps"], 3)
                dve.tensor_reduce(small[0:1, 44:45], gbank[0][0:1, 0:P], AX.X, ALU.max).then_inc(s["b1_max_step"], 1)
                dve.tensor_reduce(small[0:1, 45:46], gbank[0][0:1, 0:P], AX.X, ALU.max).then_inc(s["b1_max_step"], 1)
                dve.wait_ge(s["b1_max_step"], 2)
                dve.tensor_scalar(ksc[:, :], vec[:, VEC["attn_bk"][0]:VEC["attn_bk"][0] + KD], DH ** -0.5, None, ALU.mult).then_inc(s["b1_step"], 1)
                for w in range(2):
                    link(dve.tensor_reduce(sm(WSCALE + w), ww[:, NW // 2 * w:NW // 2 * (w + 1)], AX.X, ALU.add))
                link(dve.tensor_scalar(sm(WTHR, 2), sm(WSCALE, 2), 1.0 / (F * D), 1e-8, ALU.mult, ALU.max))
                dve.tensor_scalar(sm(WNTHR, 2), sm(WTHR, 2), -0.5, None, ALU.mult).then_inc(s["wthr_ready"], 1)
                dve.wait_ge(s["wthr_ready"], 1)
                dve.tensor_scalar(sm(WTHR, 2), sm(WTHR, 2), 0.5, None, ALU.mult).then_inc(s["wthr_ready"], 1)
                dve.wait_ge(s["small_ps"], 4)
                INT = mybir.dt.int32
                link(dve.tensor_scalar(sm(BEXP), gbank[1][:, 0:1], float(D), None, ALU.add))
                link(dve.tensor_scalar(sm(BEXP).bitcast(INT), sm(BEXP).bitcast(INT), 0x7F800000, None, ALU.bitwise_and))
                link(dve.tensor_scalar(sm(FS).bitcast(INT), sm(BEXP).bitcast(INT), -1.0, float((127 + 14 + 127) << 23), ALU.mult, ALU.add))
                link(dve.tensor_scalar(sm(FINV).bitcast(INT), sm(BEXP).bitcast(INT), 1.0, float(-(14 << 23)), ALU.mult, ALU.add))
                link(dve.memset(relbd, 0.0))
                for h in range(HC - 1):
                    link(dve.tensor_copy(relbd[h * DH:(h + 1) * DH, h, :], wr[h * DH:(h + 1) * DH, 0:REL]))
                dve.tensor_copy(relbd[(HC - 1) * DH:, HC - 1, :], wr[(HC - 1) * DH:, 0:REL]).then_inc(s["small_done"], 1)

            def ternary(i):
                dve.wait_ge(s["wthr_ready"], 2)
                dve.wait_ge(wraw_loaded[W_BUF[i]], 16 * (W_BUF[:i + 1].count(W_BUF[i])))
                at_least(dve, s["ternary_done"], i)
                dve.tensor_scalar(wneg, wraw[W_BUF[i]], sm(WNTHR + i // 4), None, ALU.is_lt).then_inc(s["neg_done"], 1)
                dve.wait_ge(s["neg_done"], i + 1)
                at_least(dve, s["turned_w_ps"], 2 * (i - 2))
                dve.scalar_tensor_tensor(out=wter[i % 3], in0=wraw[W_BUF[i]], scalar=sm(WTHR + i // 4), in1=wneg, op0=ALU.is_gt,
                                         op1=ALU.subtract).then_inc(s["ternary_done"], 1)

            dve.wait_ge(s["context_ready"], B)
            dve.wait_ge(s["pl_ready"], B)
            dve.tensor_reduce(sm(BMAX), vec[:, VEC["ffn_b1"][0]:VEC["ffn_b1"][0] + KF], AX.X, ALU.max, apply_absolute_value=True).then_inc(s["b1_step"], 1)

            def context_tile(t):
                at_least(dve, s["xattn_ps"], t)
                src = cT[:, :, t * P:(t + 1) * P] if isinstance(t, int) else cT[:, :, bass.ds(t * P, P)]
                dve.tensor_copy(c2T, src).then_inc(s["context_tile_ready"], 1)

            def layer_norm(t, src, dst, stat, mvc, vec_, rsc, names):
                a, b, c_, d_, e_ = names
                dve.bn_stats(sm(stat, 6), src).then_inc(s[a], 1)
                wait_alone(dve, s[a], t + 1)
                dve.bn_aggr(sm(mvc, 2), sm(stat, 6)).then_inc(s[b], 1)
                dve.wait_ge(s[b], t + 1)
                dve.tensor_scalar(sm(vec_), sm(mvc + 1), EPS, None, ALU.add).then_inc(s[c_], 1)
                dve.wait_ge(s[d_], t + 1)
                dve.tensor_scalar(dst, src, sm(mvc), sm(rsc), ALU.subtract, ALU.mult).then_inc(s[e_], 1)

            def softmax_a(t):
                dve.wait_ge(s["att_scores_ps"], t + 1)
                at_least(dve, s["rowexp_done"], t)
                dve.tensor_scalar(ssb.rearrange("p a b -> p (a b)"), scores_ps[0][:, :], 1e5, -1e5, ALU.min, ALU.max).then_inc(s["clip_done"], 1)
                dve.wait_ge(s["clip_done"], t + 1)
                dve.wait_ge(s["skew_loaded"], 32 * (t + 1))
                dve.tensor_tensor(ssb, ssb, rsk, ALU.add).then_inc(s["radd_done"], 1)
                dve.wait_ge(s["radd_done"], t + 1)
                dve.tensor_reduce(rows16[:, 0, :], ssb, AX.X, ALU.max).then_inc(s["rowmax_done"], 1)
                dve.wait_ge(s["rowmax_done"], t + 1)
                dve.tensor_tensor(ssb, ssb, rows16[:, 0, :].unsqueeze(2).to_broadcast([P, H, L]), ALU.subtract).then_inc(s["rowsub_done"], 1)

            def softmax_b(t):
                dve.wait_ge(s["rowexp_done"], t + 1)
                dve.tensor_reduce(rows16[:, 1, :], psb, AX.X, ALU.add).then_inc(s["rowsum_done"], 1)
                dve.wait_ge(s["rowsum_done"], t + 1)
                def lk(ins, i):
                    ins.then_inc(s["row_scale_step"], 1)
                    dve.wait_ge(s["row_scale_step"], 5 * t + i)
                lk(dve.reciprocal(rows16[:, 2, :], rows16[:, 1, :]), 1)
                lk(dve.tensor_tensor(rows16[:, 3, :], rows16[:, 1, :], rows16[:, 2, :], ALU.mult), 2)
                lk(dve.tensor_scalar(rows16[:, 3, :], rows16[:, 3, :], 1e-8, None, ALU.add), 3)
                lk(dve.reciprocal(rows16[:, 4, :], rows16[:, 3, :]), 4)
                lk(dve.tensor_tensor(rows16[:, 4, :], rows16[:, 4, :], rows16[:, 2, :], ALU.mult), 5)
                dve.tensor_tensor(psb, psb, rows16[:, 4, :].unsqueeze(2).to_broadcast([P, H, L]), ALU.mult).then_inc(s["probs_ready"], 1)

            def x1(t):
                dve.wait_ge(s["x_biased"], t + 2)
                dve.wait_ge(s["xattn_ps"], t + 1)
                dve.tensor_tensor(xc, tile(t), ws[:, :], ALU.add).then_inc(s["xattn_taken"], 1)
                dve.wait_ge(s["xattn_taken"], t + 1)
                dve.tensor_tensor(tile(t), xc, abo, ALU.add).then_inc(s["residual_ready"], 1)
                layer_norm(t, xc, yn, STAT1, MV1, VE1, RS1, ("ln1_stats", "ln1_moments", "ln1_var", "ln1_rstd", "y_ready"))

            def x2(t):
                dve.wait_ge(s["residual_ready"], t + 1)
                dve.wait_ge(s["att_out_ps"], t + 1)
                at_least(dve, s["residual2_ready"], t)
                dve.tensor_tensor(zc, tile(t), ws[:, :], ALU.add).then_inc(s["att_out_taken"], 1)
                dve.wait_ge(s["att_out_taken"], t + 1)
                layer_norm(t, zc, zn, STAT2, MV2, VE2, RS2, ("ln2_stats", "ln2_moments", "ln2_var", "ln2_rstd", "z_ready"))

            def gelu_parts(t, half):
                sl = slice(KF // 2 * half, KF // 2 * (half + 1))
                dve.wait_ge(s["gelu_done"], KF * t + KF // 2 * (half + 1))
                if half == 0:
                    at_least(dve, s["ffn_out_ps"], t)
                dve.tensor_scalar(gh[:, sl, :], gf[:, sl, :], sm(FS), None, ALU.mult).then_inc(s["gelu_high_ready"], 1)
                dve.wait_ge(s["gelu_high_ready"], 2 * t + half + 1)
                dve.scalar_tensor_tensor(out=gl[:, sl, :], in0=gf[:, sl, :], scalar=sm(FS), in1=gh[:, sl, :], op0=ALU.mult,
                                         op1=ALU.subtract).then_inc(s["gelu_low_ready%d" % half], 1)

            def ctx_out(t):
                dve.wait_ge(s["values_ps"], 2 * (t + 1))
                pv = scores_ps[0][:, :].rearrange("p (hc two r) -> p two hc r", two=2, r=P)
                for v in range(2):
                    for b2 in range(2):
                        dve.tensor_copy(ctxT[v * L:(v + 1) * L, :, b2 * L:(b2 + 1) * L],
                                        pv[b2 * L:(b2 + 1) * L, v, :, b2 * L:(b2 + 1) * L]).then_inc(s["values_taken"], 1)

            def v_out(t):
                dve.wait_ge(s["v_ps"], t + 1)
                src = wr[:, :].rearrange("p (hp v d) -> p hp v d", v=2, d=DH)
                bias = abv.rearrange("p (hp v d) -> p hp v d", v=2, d=DH)
                for v in range(2):
                    for b2 in range(2):
                        r = slice(b2 * L, (b2 + 1) * L)
                        dve.tensor_tensor(vbd[v * L:(v + 1) * L, :, b2, v, :], src[r, :, v, :], bias[r, :, v, :],
                                          ALU.add).then_inc(s["v_taken"], 1)

            def z_low(t):
                dve.wait_ge(s["z_high_ready"], t + 1)
                dve.tensor_tensor(zl.rearrange("p a b -> p (a b)"), ww[:, :], zh.rearrange("p a b -> p (a b)"), ALU.subtract).then_inc(s["z_low_ready"], 1)

            def result(t):
                dve.wait_ge(s["ffn_out_ps"], t + 1)
                dve.wait_ge(s["residual2_ready"], t + 1)
                at_least(dve, s["stored"], 16 * t)
                dve.scalar_tensor_tensor(out=ot, in0=u_ps[:, :], scalar=sm(FINV), in1=xb2, op0=ALU.mult, op1=ALU.add).then_inc(s["out_ready"], 1)

            def dense(t, proj, att, ffn):
                first = t if isinstance(t, int) and t < 2 else None
                if ffn:
                    z_low(t - 2)
                if proj:
                    x1(t)
                if first == 0:
                    small_values()
                if proj and not (isinstance(t, int) and t == NT - 1):
                    context_tile(t + 1)
                if att:
                    softmax_a(t - 1)
                if first is not None:
                    ternary(4 * first)
                if ffn:
                    gelu_parts(t - 2, 0)
                    gelu_parts(t - 2, 1)
                if att:
                    softmax_b(t - 1)
                if first is not None:
                    ternary(4 * first + 1)
                if first == 1:
                    ternary(6)
                if att:
                    ctx_out(t - 1)
                if first == 0:
                    dve.wait_ge(s["zeros_done"], 2)
                    dve.wait_ge(s["abv_loaded"], 16)
                if proj:
                    v_out(t)
                if first == 0:
                    ternary(2)
                    ternary(3)
                if first == 1:
                    ternary(7)
                if att:
                    x2(t - 1)
                if ffn:
                    result(t - 2)
            context_tile(0)
            run_dense(dve, dense)


def kernel(**inputs):
    import numpy as _np
    import concourse.bacc as _bacc
    from concourse import mybir as _mybir
    from concourse.bass_utils import run_bass_kernel_spmd as _run

    nc = _bacc.Bacc("TRN2", target_bir_lowering=False, num_devices=1)
    arrays, args = {}, {}
    for name, a in inputs.items():
        a = _np.ascontiguousarray(a)
        arrays[f"in_{name}_dram"] = a
        args[name] = nc.dram_tensor(f"in_{name}_dram", a.shape, _mybir.dt.from_np(a.dtype), kind="ExternalInput").ap()
    out = nc.dram_tensor("out_dram", inputs["x"].shape, _mybir.dt.float32, kind="ExternalOutput").ap()
    build_program(nc, args, out)
    return _run(nc, [arrays], core_ids=[0]).results[0]["out_dram"]
```
